# Optimizing a Trainium2 kernel written in Bass

```python
import numpy as np
import jax
import jax.numpy as jnp

def _softmax(x, axis=-1):
    return jax.nn.softmax(x, axis=axis)

def _gelu(x):
    return jax.nn.gelu(x, approximate=True)

def _silu(x):
    return jax.nn.silu(x)

def _sigmoid(x):
    return jax.nn.sigmoid(x)

def _layernorm(x, axis=-1, eps=1e-05):
    m = jnp.mean(x, axis=axis, keepdims=True)
    v = jnp.var(x, axis=axis, keepdims=True)
    return (x - m) / jnp.sqrt(v + eps)

def _scatter_add(tgt, idx, src, axis=0):
    return tgt.at[idx].add(src)

def _segment_sum(src, seg, n):
    return jax.ops.segment_sum(src, seg, n)
kernel_name = 'mk_xattn_ffn_d2_seqx_r2_1b20c8'

def setup_inputs(seed: int=0):
    np.random.seed(seed)
    _w = jnp.asarray

    def _rec_inputs():
        import jax
        import jax.numpy as jnp
        _rk = jax.random.key(seed)
        x = -0.0003929 + 0.9999 * jax.random.normal(jax.random.fold_in(_rk, 1), (8, 512, 512), jnp.float32)
        _lenS = 512 - jax.random.randint(jax.random.fold_in(_rk, 7), (8,), 0, max(1, 512 // 4) + 1, jnp.int32)
        _lenS2 = 120 - jax.random.randint(jax.random.fold_in(_rk, 8), (8,), 0, max(1, 120 // 4) + 1, jnp.int32)
        _ctx_1024P = jax.random.normal(jax.random.fold_in(_rk, 11), (8, 16, 512), jnp.float32)
        _ctx_1024c = jax.random.dirichlet(jax.random.fold_in(_rk, 511), 0.3 * jnp.ones((16,), jnp.float32), (8, 120))
        _ctx_1024t = jnp.einsum('bsk,bkd->bsd', _ctx_1024c, _ctx_1024P)
        _ctx_1024t = _ctx_1024t * jax.lax.rsqrt(jnp.mean(jnp.square(_ctx_1024t)) + 1e-12) * 0.953939
        ctx_1024 = 2.81802e-05 + 1.00001 * (_ctx_1024t + 0.3 * jax.random.normal(jax.random.fold_in(_rk, 611), (8, 120, 512), jnp.float32))
        return (x, ctx_1024)
    x, ctx_1024 = _rec_inputs()

    def _L0_xattn_setup():
        import jax, jax.numpy as jnp
        import numpy as np
        EMBED = 512
        B, I, J = (8, 1024, 1024)
        SCALE = EMBED ** (-0.5)
        key = jax.random.key(seed)
        ks = jax.random.split(key, 5)
        s = EMBED ** (-0.5)
        return {'q_in': jax.random.normal(ks[0], (B, I, EMBED), dtype=jnp.float32), 'k_v': jax.random.normal(ks[1], (B, J, EMBED), dtype=jnp.float32), 'Wq': jax.random.normal(ks[2], (EMBED, EMBED), dtype=jnp.float32) * s, 'bq': jnp.zeros((EMBED,), dtype=jnp.float32), 'Wk': jax.random.normal(ks[3], (EMBED, EMBED), dtype=jnp.float32) * s, 'bk': jnp.zeros((EMBED,), dtype=jnp.float32), 'Wv': jax.random.normal(ks[4], (EMBED, EMBED), dtype=jnp.float32) * s, 'bv': jnp.zeros((EMBED,), dtype=jnp.float32)}
    _L0_xattn_all = _L0_xattn_setup()
    _L0_xattn_in = {k: v for k, v in _L0_xattn_all.items() if k in ('Wq', 'bq', 'Wk', 'bk', 'Wv', 'bv')}
    del _L0_xattn_all

    def _L0_ffn_setup():
        import jax, jax.numpy as jnp
        import numpy as np
        INT8_MAX = 127.0

        def _absmax_scale(x, axes):
            amax = jnp.max(jnp.abs(x), axis=axes, keepdims=True)
            return jnp.maximum(amax, 1e-12) / INT8_MAX
        key = jax.random.key(seed)
        k1, k2 = jax.random.split(key)
        lhs = jax.random.normal(k1, (4, 4096, 512), dtype=jnp.float32)
        rhs = jax.random.normal(k2, (512, 512), dtype=jnp.float32)
        return {'lhs': lhs, 'rhs': rhs}
    _L0_ffn_all = _L0_ffn_setup()
    _L0_ffn_in = {k: v for k, v in _L0_ffn_all.items() if k in ('rhs',)}
    del _L0_ffn_all

    def _L1_xattn_setup():
        import jax, jax.numpy as jnp
        import numpy as np
        D_MODEL = 512
        N_HEADS = 16
        HEAD_DIM = D_MODEL // N_HEADS
        key = jax.random.key(seed)
        k1, k2, k3, k4, k5, k6 = jax.random.split(key, 6)
        B, T_q, T_kv = (4, 512, 2048)
        s = 1.0 / np.sqrt(D_MODEL)
        return {'query': jax.random.normal(k1, (B, T_q, D_MODEL), dtype=jnp.float32), 'kv_source': jax.random.normal(k2, (B, T_kv, D_MODEL), dtype=jnp.float32), 'w_q': jax.random.normal(k3, (D_MODEL, D_MODEL), dtype=jnp.float32) * s, 'w_k': jax.random.normal(k4, (D_MODEL, D_MODEL), dtype=jnp.float32) * s, 'w_v': jax.random.normal(k5, (D_MODEL, D_MODEL), dtype=jnp.float32) * s, 'w_o': jax.random.normal(k6, (D_MODEL, D_MODEL), dtype=jnp.float32) * s}
    _L1_xattn_all = _L1_xattn_setup()
    _L1_xattn_in = {k: v for k, v in _L1_xattn_all.items() if k in ('w_q', 'w_k', 'w_v', 'w_o')}
    del _L1_xattn_all

    def _L1_ffn_setup():
        import jax, jax.numpy as jnp
        import numpy as np
        B, S, H = (2, 1024, 512)
        E_DYN, E_FIX = (8, 1)
        I_DYN, I_FIX = (256, 1024)
        TOP_K = 4
        TOP_P = 0.75
        JITTER_EPS = 0.1
        CAPACITY_FACTOR = 1.25
        MIN_CAPACITY = 4

        def _sparse_mixer(scores):
            T = scores.shape[0]
            rows = jnp.arange(T)
            masked_scores = scores
            mults, sels = ([], [])
            for _ in range(TOP_K):
                thr = jnp.max(masked_scores, axis=-1, keepdims=True)
                sel = jnp.argmax(masked_scores, axis=-1)
                factor = jnp.maximum(jnp.abs(scores), jnp.abs(thr))
                jmask = (thr - scores) / factor > 2.0 * JITTER_EPS
                gates = jax.nn.softmax(jnp.where(jmask, -jnp.inf, masked_scores), axis=-1)
                mult = jnp.take_along_axis(gates, sel[:, None], axis=-1)[:, 0]
                masked_scores = masked_scores.at[rows, sel].set(-jnp.inf)
                mults.append(mult)
                sels.append(sel)
            return (jnp.stack(mults, axis=-1), jnp.stack(sels, axis=-1))
        key = jax.random.key(seed)
        k = jax.random.split(key, 8)
        sc = 0.02
        return {'hidden_states': jax.random.normal(k[0], (B, S, H), jnp.float32), 'gate_w': jax.random.normal(k[1], (E_DYN + E_FIX, H), jnp.float32) * sc, 'dyn_gate_w': jax.random.normal(k[2], (E_DYN, I_DYN, H), jnp.float32) * sc, 'dyn_up_w': jax.random.normal(k[3], (E_DYN, I_DYN, H), jnp.float32) * sc, 'dyn_down_w': jax.random.normal(k[4], (E_DYN, H, I_DYN), jnp.float32) * sc, 'sh_gate_w': jax.random.normal(k[5], (E_FIX, I_FIX, H), jnp.float32) * sc, 'sh_up_w': jax.random.normal(k[6], (E_FIX, I_FIX, H), jnp.float32) * sc, 'sh_down_w': jax.random.normal(k[7], (E_FIX, H, I_FIX), jnp.float32) * sc}
    _L1_ffn_all = _L1_ffn_setup()
    _L1_ffn_in = {k: v for k, v in _L1_ffn_all.items() if k in ('gate_w', 'dyn_gate_w', 'dyn_up_w', 'dyn_down_w', 'sh_gate_w', 'sh_up_w', 'sh_down_w')}
    del _L1_ffn_all
    return {'x': x, 'ctx_1024': ctx_1024, 'L0_xattn_Wq': _L0_xattn_in['Wq'], 'L0_xattn_bq': _L0_xattn_in['bq'], 'L0_xattn_Wk': _L0_xattn_in['Wk'], 'L0_xattn_bk': _L0_xattn_in['bk'], 'L0_xattn_Wv': _L0_xattn_in['Wv'], 'L0_xattn_bv': _L0_xattn_in['bv'], 'L0_ffn_rhs': _L0_ffn_in['rhs'], 'L1_xattn_w_q': _L1_xattn_in['w_q'], 'L1_xattn_w_k': _L1_xattn_in['w_k'], 'L1_xattn_w_v': _L1_xattn_in['w_v'], 'L1_xattn_w_o': _L1_xattn_in['w_o'], 'L1_ffn_gate_w': _L1_ffn_in['gate_w'], 'L1_ffn_dyn_gate_w': _L1_ffn_in['dyn_gate_w'], 'L1_ffn_dyn_up_w': _L1_ffn_in['dyn_up_w'], 'L1_ffn_dyn_down_w': _L1_ffn_in['dyn_down_w'], 'L1_ffn_sh_gate_w': _L1_ffn_in['sh_gate_w'], 'L1_ffn_sh_up_w': _L1_ffn_in['sh_up_w'], 'L1_ffn_sh_down_w': _L1_ffn_in['sh_down_w']}

def reference(x, ctx_1024, L0_xattn_Wq, L0_xattn_bq, L0_xattn_Wk, L0_xattn_bk, L0_xattn_Wv, L0_xattn_bv, L0_ffn_rhs, L1_xattn_w_q, L1_xattn_w_k, L1_xattn_w_v, L1_xattn_w_o, L1_ffn_gate_w, L1_ffn_dyn_gate_w, L1_ffn_dyn_up_w, L1_ffn_dyn_down_w, L1_ffn_sh_gate_w, L1_ffn_sh_up_w, L1_ffn_sh_down_w):
    import jax
    import jax.numpy as jnp

    def _L0_xattn_ref(q_in, k_v, Wq, bq, Wk, bk, Wv, bv):
        import jax, jax.numpy as jnp
        import numpy as np
        EMBED = 512
        B, I, J = (8, 1024, 1024)
        SCALE = EMBED ** (-0.5)
        q = q_in @ Wq + bq
        k = k_v @ Wk + bk
        v = k_v @ Wv + bv
        sim = jnp.einsum('bid,bjd->bij', q, k) * SCALE
        attn = jax.nn.softmax(sim, axis=-1)
        out = jnp.einsum('bij,bjd->bid', attn, v)
        return out

    def _L0_ffn_ref(lhs, rhs):
        import jax, jax.numpy as jnp
        import numpy as np
        INT8_MAX = 127.0

        def _absmax_scale(x, axes):
            amax = jnp.max(jnp.abs(x), axis=axes, keepdims=True)
            return jnp.maximum(amax, 1e-12) / INT8_MAX
        lhs_scale = _absmax_scale(lhs, (2,))
        rhs_scale = _absmax_scale(rhs, (0,))
        q_lhs = jnp.clip(jnp.round(lhs / lhs_scale), -INT8_MAX, INT8_MAX).astype(jnp.int8)
        q_rhs = jnp.clip(jnp.round(rhs / rhs_scale), -INT8_MAX, INT8_MAX).astype(jnp.int8)
        acc = jax.lax.dot_general(q_lhs, q_rhs, (((2,), (0,)), ((), ())), preferred_element_type=jnp.int32)
        return acc.astype(jnp.float32) * lhs_scale * rhs_scale

    def _L1_xattn_ref(query, kv_source, w_q, w_k, w_v, w_o):
        import jax, jax.numpy as jnp
        import numpy as np
        D_MODEL = 512
        N_HEADS = 16
        HEAD_DIM = D_MODEL // N_HEADS
        B, T_q, _ = query.shape
        T_kv = kv_source.shape[1]
        q = (query @ w_q.T).reshape(B, T_q, N_HEADS, HEAD_DIM)
        k = (kv_source @ w_k.T).reshape(B, T_kv, N_HEADS, HEAD_DIM)
        v = (kv_source @ w_v.T).reshape(B, T_kv, N_HEADS, HEAD_DIM)
        scale = HEAD_DIM ** (-0.5)
        attn = jax.nn.softmax(jnp.einsum('bqhd,bkhd->bhqk', q, k) * scale, axis=-1)
        out = jnp.einsum('bhqk,bkhd->bqhd', attn, v).reshape(B, T_q, D_MODEL)
        return out @ w_o.T

    def _L1_ffn_ref(hidden_states, gate_w, dyn_gate_w, dyn_up_w, dyn_down_w, sh_gate_w, sh_up_w, sh_down_w):
        import jax, jax.numpy as jnp
        import numpy as np
        B, S, H = (2, 1024, 512)
        E_DYN, E_FIX = (8, 1)
        I_DYN, I_FIX = (256, 1024)
        TOP_K = 4
        TOP_P = 0.75
        JITTER_EPS = 0.1
        CAPACITY_FACTOR = 1.25
        MIN_CAPACITY = 4

        def _sparse_mixer(scores):
            T = scores.shape[0]
            rows = jnp.arange(T)
            masked_scores = scores
            mults, sels = ([], [])
            for _ in range(TOP_K):
                thr = jnp.max(masked_scores, axis=-1, keepdims=True)
                sel = jnp.argmax(masked_scores, axis=-1)
                factor = jnp.maximum(jnp.abs(scores), jnp.abs(thr))
                jmask = (thr - scores) / factor > 2.0 * JITTER_EPS
                gates = jax.nn.softmax(jnp.where(jmask, -jnp.inf, masked_scores), axis=-1)
                mult = jnp.take_along_axis(gates, sel[:, None], axis=-1)[:, 0]
                masked_scores = masked_scores.at[rows, sel].set(-jnp.inf)
                mults.append(mult)
                sels.append(sel)
            return (jnp.stack(mults, axis=-1), jnp.stack(sels, axis=-1))
        Bv, Sv, Hv = hidden_states.shape
        T = Bv * Sv
        x = hidden_states.reshape(T, Hv)
        full_logits = x @ gate_w.T
        dyn_logits = full_logits[:, :E_DYN]
        probs = jax.nn.softmax(dyn_logits, axis=-1)
        sorted_p = jnp.sort(probs, axis=-1)[:, ::-1]
        csum = jnp.cumsum(sorted_p, axis=-1)
        dyn_k = jnp.minimum(jnp.sum(csum < TOP_P, axis=-1) + 1, TOP_K)
        mult, sel = _sparse_mixer(dyn_logits)
        slot_valid = jnp.arange(TOP_K)[None, :] < dyn_k[:, None]
        mult = jnp.where(slot_valid, mult, 0.0)
        rows = jnp.arange(T)
        rw = jnp.zeros((T, E_DYN), x.dtype).at[rows[:, None], sel].add(mult)
        rw = rw / jnp.sum(rw, axis=-1, keepdims=True)
        mask_dyn = (rw > 0).astype(jnp.int32)
        cap = max(int(np.ceil(T / E_DYN * CAPACITY_FACTOR)), MIN_CAPACITY)
        mask_dyn = mask_dyn * (jnp.cumsum(mask_dyn, axis=0) <= cap)
        expert_mask = jnp.concatenate([mask_dyn, jnp.ones((T, E_FIX), jnp.int32)], axis=-1)
        maskf = expert_mask.astype(x.dtype)
        gw = jax.nn.softmax(jnp.where(expert_mask == 0, -jnp.inf, full_logits), axis=-1)
        gd = rw * jnp.sum(gw[:, :E_DYN], axis=-1, keepdims=True)
        global_w = jnp.concatenate([gd, gw[:, E_DYN:]], axis=-1) * maskf
        g = jnp.einsum('th,eih->tei', x, dyn_gate_w)
        u = jnp.einsum('th,eih->tei', x, dyn_up_w)
        y_dyn = jnp.einsum('tei,ehi->teh', jax.nn.silu(g) * u, dyn_down_w)
        out = jnp.einsum('te,teh->th', global_w[:, :E_DYN], y_dyn)
        gs = jnp.einsum('th,fih->tfi', x, sh_gate_w)
        us = jnp.einsum('th,fih->tfi', x, sh_up_w)
        y_sh = jnp.einsum('tfi,fhi->tfh', jax.nn.silu(gs) * us, sh_down_w)
        out = out + jnp.einsum('tf,tfh->th', global_w[:, E_DYN:], y_sh)
        return out.reshape(Bv, Sv, Hv)
    x = x + _L0_xattn_ref(_layernorm(x, axis=-1), ctx_1024, L0_xattn_Wq, L0_xattn_bq, L0_xattn_Wk, L0_xattn_bk, L0_xattn_Wv, L0_xattn_bv)
    x = x + _L0_ffn_ref(_layernorm(x, axis=-1), L0_ffn_rhs)
    x = x + _L1_xattn_ref(_layernorm(x, axis=-1), ctx_1024, L1_xattn_w_q, L1_xattn_w_k, L1_xattn_w_v, L1_xattn_w_o)
    x = x + _L1_ffn_ref(_layernorm(x, axis=-1), L1_ffn_gate_w, L1_ffn_dyn_gate_w, L1_ffn_dyn_up_w, L1_ffn_dyn_down_w, L1_ffn_sh_gate_w, L1_ffn_sh_up_w, L1_ffn_sh_down_w)
    return x

_drawn_inputs = setup_inputs


def setup_inputs(seed=0):
    import zlib

    import numpy as np

    out = dict(_drawn_inputs(seed))
    spreads = {'L0_xattn_bq': (0.0, 0.336), 'L0_xattn_bk': (0.0, 0.8), 'L0_xattn_bv': (0.0, 0.1)}
    factors = {'L1_xattn_w_q': 6.261,
     'L1_xattn_w_k': 6.255,
     'L1_ffn_gate_w': 8.0,
     'L1_ffn_dyn_gate_w': 8.0,
     'L1_ffn_dyn_up_w': 8.0,
     'L1_ffn_dyn_down_w': 8.0,
     'L1_ffn_sh_gate_w': 8.0,
     'L1_ffn_sh_up_w': 8.0,
     'L1_ffn_sh_down_w': 8.0}
    for name, (base, spread) in spreads.items():
        noise = np.random.default_rng([zlib.crc32(name.encode()), seed]).standard_normal(out[name].shape)
        drawn = base * np.exp(spread * noise) if base else spread * noise
        out[name] = jnp.asarray(drawn.astype(out[name].dtype))
    for name, factor in factors.items():
        out[name] = (out[name] * factor).astype(out[name].dtype)
    return out
```

```python
import concourse.bass as bass
from concourse import mybir
from contextlib import ExitStack

f32 = mybir.dt.float32
f16 = mybir.dt.float16
bf16 = mybir.dt.bfloat16
u32 = mybir.dt.uint32
ALU = mybir.AluOpType
ACT = mybir.ActivationFunctionType
AX = mybir.AxisListType

P = 128
B, S, D = 8, 512, 512
J = 120
T = B * S
NT = T // P
TB = S // P
KC = D // P
JB = B * J
HEADS, DH = 16, 32
HC = P // DH
E = 8
IE, IS = 256, 1024
CAP = 640
EPS = 1e-5
WS = 64.0
HS = 1.0 / 16
SC0 = float(D) ** -0.5
SC1 = float(DH) ** -0.5
PASSES = ((0, 0), (1, 0), (0, 1))
ROUND = 1.5 * 2.0 ** 23


def need(eng, sem, n):
    if isinstance(n, int) and n <= 0:
        return
    eng.wait_ge(sem, n)


def live(t):
    return not isinstance(t, int) or 0 <= t < NT


def pipeline(eng, step, lead, lag, n=NT, by=TB):
    rounds = (n - by - lead) // by
    for s in range(-lead, by):
        step(s, s % by)
    with eng.Fori(1, rounds + 1) as i:
        for d in range(by):
            step(i * by + d, d)
    for s in range((rounds + 1) * by, n + lag):
        step(s, s % by)


class Scope:

    semaphores: list = []

    def __init__(self, nc, ctx, stage):
        self.nc, self.ctx, self.stage = nc, ctx, stage + "_"

    def sb(self, name, shape, dt=f32):
        return self.ctx.enter_context(self.nc.sbuf_tensor(self.stage + name, shape, dt))

    def ps(self, name, shape, dt=f32):
        return self.ctx.enter_context(self.nc.psum_tensor(self.stage + name, shape, dt))

    def sem(self, name):
        handle = self.nc.alloc_semaphore(self.stage + name)
        Scope.semaphores.append(handle)
        return handle

    @classmethod
    def clear_semaphores(cls, nc):
        nc.clear_and_free_semaphores(cls.semaphores)
        nc.all_engine_barrier()
        cls.semaphores = []


def matmuls(pe, out, lhs, rhs, ks=range(KC)):
    terms = [(k, a, b) for k in ks for a, b in PASSES]
    for n, (k, a, b) in enumerate(terms):
        last = pe.matmul(out, lhs(a, k), rhs(b, k), start=n == 0, stop=n == len(terms) - 1)
    return last


def setup(nc, g, io):
    with ExitStack() as ctx:
        m = Scope(nc, ctx, "setup")
        W = ["L0_Wk", "L0_Wv", "L0_WqT", "L1_wkT", "L1_wvT", "L1_wqT", "L1_woT", "L0_rhs"]
        NW = len(W)
        raw = g.x[:, NT - 12:NT, :].rearrange("p (w k) n -> p w k n", w=3)
        ctx_s = m.sb("ctx_s", [P, 2, KC, JB], f16)
        wk = g.x[:, NT - 24:NT - 12, :].rearrange("p (w q k) n -> p w q (k n)", w=3, q=2) \
            .bitcast(f16).rearrange("p w q (k n) -> p w q k n", k=KC)
        k0f = m.sb("k0f", [P, KC, JB])
        ctxf = k0f
        k0 = m.sb("k0", [P, 2, KC, JB], f16)
        fstage = m.sb("fstage", [P, 2, D])
        bvb = m.sb("bvb", [P, D])
        bqk = m.sb("bqk", [P, 2, KC])
        bqb = m.sb("bqb", [P, KC, P])
        ones = m.sb("ones", [P, P])
        qabs = m.sb("qabs", [P, KC])
        qinv = m.sb("qinv", [P, KC])
        rT = k0[:, :, :, :].rearrange("p q k n -> p (q k n)")[:, 0:2 * KC * D].bitcast(f32) \
            .rearrange("p (k n) -> p k n", k=KC)
        dg = bqb
        ring = [m.ps(f"ring{i}", [P, D]) for i in range(4)]
        bps = [m.ps(f"bps{i}", [P, D]) for i in range(2)]
        xp = [m.ps(f"xp{i}", [P, KC, P]) for i in range(2)]

        loaded = [m.sem(f"loaded{n}") for n in range(NW)]
        x_in, ctx_in, bias_in = g.x_in, m.sem("ctx_in"), m.sem("bias_in")
        hi_done, lo_done = m.sem("hi_done"), m.sem("lo_done")
        ctx_hi, ctx_lo = m.sem("ctx_hi"), m.sem("ctx_lo")
        bq_done, ones_done = m.sem("bq_done"), m.sem("ones_done")
        job_mm, job_f, job_hi, job_lo = (m.sem(n) for n in ("job_mm", "job_f", "job_hi", "job_lo"))
        bias_mm, bias_out = m.sem("bias_mm"), m.sem("bias_out")
        id0, id1 = m.sem("id0"), m.sem("id1")
        r_mm, r_abs, r_s1, r_s2, r_q, r_b, r_out, r_dg, r_bc = (
            m.sem(n) for n in ("r_mm", "r_abs", "r_s1", "r_s2", "r_q", "r_b", "r_out", "r_dg", "r_bc"))

        jobs = [("k0", (mm, h)) for mm in range(KC) for h in range(2)]
        jobs += [("v0", b) for b in range(B)]
        jobs += [("m0", (mm, h)) for mm in range(KC) for h in range(2)]
        jobs += [("k1", (mm, h)) for mm in range(KC) for h in range(2)]
        jobs += [("v1", b) for b in range(B)]
        last_job = [8, 16, 24, 32, 40]
        weight_of = {"k0": 0, "v0": 1, "m0": 2, "k1": 3, "v1": 4}
        NH = JB // 2

        def shape(kind):
            return (slice(0, J), slice(0, D)) if kind[0] == "v" else (slice(0, P), slice(0, NH))

        def parts(kind, ix):
            if kind == "v0":
                return g.v0[0:J, 0, ix, :], g.v0[0:J, 1, ix, :]
            if kind == "v1":
                return g.v1[0:J, 0, ix, :], g.v1[0:J, 1, ix, :]
            to = {"k0": k0, "m0": g.m0, "k1": g.k1}[kind]
            mm, h = ix
            return tuple(to[:, q, mm, h * NH:(h + 1) * NH] for q in range(2))

        def f_of(n):
            kind, ix = jobs[n]
            if kind == "k0":
                return k0f[:, ix[0], ix[1] * NH:(ix[1] + 1) * NH]
            rows, cols = shape(kind)
            return fstage[rows, n % 2, cols]

        def w_part(n, q):
            if n < 5:
                return wk[:, n % 3, q]
            return {5: g.wq1, 6: g.wo1}[n][:, q]

        with nc.Block() as block:

            @block.sync
            def _(sp):
                sp.dma_start(ctxf[:, :, :], io["ctxT"].rearrange("(k p) n -> p k n", p=P)).then_inc(ctx_in, 16)
                sp.dma_start(bvb[:, :], io["L0_bv"].partition_broadcast(P)).then_inc(bias_in, 16)
                sp.dma_start(bqk[:, 0, :], io["L0_bq"]).then_inc(bias_in, 16)
                sp.dma_start(bqk[:, 1, :], io["L0_bk"]).then_inc(bias_in, 16)
                for n in range(NW - 1):
                    if n >= 3:
                        sp.wait_ge(hi_done, n - 2)
                        sp.wait_ge(lo_done, n - 2)
                    sp.dma_start(raw[:, n % 3], io[W[n]].rearrange("(k p) n -> p k n", p=P)).then_inc(loaded[n], 16)
                sp.wait_ge(job_mm, 24)
                sp.dma_start(rT[:, :, :], io["L0_rhsT"].rearrange("(k p) n -> p k n", p=P)).then_inc(loaded[NW - 1], 16)
                xs = io["x"].rearrange("(t p) d -> p t d", p=P)
                for t0, t1 in ((0, 8),):
                    sp.dma_start(g.x[:, t0:t1, :], xs[:, t0:t1, :]).then_inc(x_in, 16)
                sp.wait_ge(hi_done, NW - 1)
                sp.wait_ge(lo_done, NW - 1)
                for t0, t1 in ((NT - 12, NT),):
                    sp.dma_start(g.x[:, t0:t1, :], xs[:, t0:t1, :]).then_inc(x_in, 16)
                sp.wait_ge(job_mm, len(jobs))
                for t0, t1 in ((8, NT - 12),):
                    sp.dma_start(g.x[:, t0:t1, :], xs[:, t0:t1, :]).then_inc(x_in, 16)

            @block.gpsimd
            def _(pool):
                pool.memset(g.ident[:, :], 0.0).then_inc(id0, 1)
                pool.memset(ones[:, :], 1.0).then_inc(ones_done, 1)
                pool.memset(g.half[:, :], -0.5).then_inc(id1, 1)
                pool.memset(g.eps[:, :], EPS).then_inc(id1, 1)
                pool.memset(g.one[:, :], 1.0).then_inc(id1, 1)
                pool.wait_ge(id0, 1)
                pool.affine_select(out=g.ident[:, :], in_=g.ident[:, :], compare_op=ALU.not_equal, fill=1.0,
                                   base=0, pattern=[[-1, P]], channel_multiplier=1).then_inc(id0, 1)

            @block.scalar
            def _(act):
                act.wait_ge(ctx_in, 16)
                act.activation(ctx_s[:, 0], ctxf[:, :, :], ACT.Copy).then_inc(ctx_hi, 1)

                def split(n):
                    act.wait_ge(loaded[n], 16)
                    if 3 <= n < 5:
                        act.wait_ge(job_mm, last_job[n - 3])
                    act.activation(w_part(n, 0), raw[:, n % 3], ACT.Copy, scale=WS).then_inc(hi_done, 1)

                split(0)
                split(1)
                for n, (kind, ix) in enumerate(jobs):
                    act.wait_ge(job_f, n + 1)
                    act.activation(parts(kind, ix)[0], f_of(n), ACT.Copy).then_inc(job_hi, 1)
                    if n % 4 == 3 and n // 4 + 2 < NW - 1:
                        split(n // 4 + 2)
                act.wait_ge(r_s2, 1)
                act.wait_ge(r_abs, 2)
                for k in range(KC):
                    act.activation(rT[:, k, :], rT[:, k, :], ACT.Identity, scale=qinv[:, k:k + 1],
                                   bias=g.round_c[:, 0:1]).then_inc(r_q, 1)

            @block.vector
            def _(dve):
                dve.memset(g.round_c[:, 0:1], ROUND).then_inc(r_abs, 1)
                dve.memset(g.round_c[:, 1:2], -ROUND).then_inc(r_abs, 1)
                dve.wait_ge(ctx_hi, 1)
                dve.tensor_tensor(ctx_s[:, 1], ctxf[:, :, :], ctx_s[:, 0], ALU.subtract).then_inc(ctx_lo, 1)

                def split(n):
                    dve.wait_ge(hi_done, n + 1)
                    dve.scalar_tensor_tensor(w_part(n, 1), raw[:, n % 3], WS, w_part(n, 0), ALU.mult,
                                             ALU.subtract).then_inc(lo_done, 1)

                split(0)
                split(1)
                dve.wait_ge(bias_in, 48)
                dve.wait_ge(ones_done, 1)
                for k in range(KC):
                    dve.tensor_scalar(bqb[:, k, :], ones[:, :], bqk[:, 0, k:k + 1], None, ALU.mult).then_inc(bq_done, 1)
                for n, (kind, ix) in enumerate(jobs):
                    rows, cols = shape(kind)
                    out, bank = f_of(n), ring[n % 4][rows, cols]
                    dve.wait_ge(job_mm, n + 1)
                    need(dve, job_hi, n - 1)
                    need(dve, job_lo, n - 1)
                    if kind == "k0":
                        dve.tensor_scalar(out, bank, 1 / WS, bqk[:, 1, ix[0]:ix[0] + 1], ALU.mult, ALU.add).then_inc(job_f, 1)
                    elif kind == "v0":
                        dve.scalar_tensor_tensor(out, bank, 1 / WS, bvb[rows, :], ALU.mult, ALU.add).then_inc(job_f, 1)
                    else:
                        dve.tensor_scalar(out, bank, 1 / WS, None, ALU.mult).then_inc(job_f, 1)
                    dve.wait_ge(job_hi, n + 1)
                    dve.wait_ge(job_f, n + 1)
                    hi, lo = parts(kind, ix)
                    dve.tensor_tensor(lo, out, hi, ALU.subtract).then_inc(job_lo, 1)
                    if n % 4 == 3 and n // 4 + 2 < NW - 1:
                        split(n // 4 + 2)
                    if n == 15:
                        for h in range(2):
                            dve.wait_ge(bias_mm, h + 1)
                            dve.tensor_scalar(g.simb[:, h * NH:(h + 1) * NH], bps[h][:, 0:NH], SC0, None,
                                              ALU.mult).then_inc(bias_out, 1)
                dve.wait_ge(loaded[NW - 1], 16)
                dve.tensor_reduce(qabs[:, :], rT[:, :, :], AX.X, ALU.max, apply_absolute_value=True).then_inc(r_s1, 1)
                dve.wait_ge(r_s1, 1)
                dve.tensor_scalar(qabs[:, :], qabs[:, :], 1e-12, 1 / 127.0, ALU.max, ALU.mult).then_inc(r_s1, 1)
                dve.wait_ge(r_s1, 2)
                dve.reciprocal(qinv[:, :], qabs[:, :]).then_inc(r_s2, 1)
                dve.wait_ge(id0, 2)
                for k in range(KC):
                    dve.tensor_scalar(dg[:, k, :], g.ident[:, :], qabs[:, k:k + 1], None, ALU.mult).then_inc(r_dg, 1)
                for c in range(KC):
                    dve.wait_ge(r_mm, c + 1)
                    dve.tensor_scalar(g.qr[:, c, :].rearrange("p (k n) -> p k n", k=KC), xp[c % 2][:, :, :], ROUND,
                                      None, ALU.subtract).then_inc(r_out, 1)
                dve.wait_ge(r_bc, 1)
                dve.tensor_copy(g.rs[:, :], bps[0][:, :]).then_inc(r_b, 1)

            @block.tensor
            def _(pe):
                pe.wait_ge(ctx_lo, 1)
                seen = -1
                for n, (kind, ix) in enumerate(jobs):
                    rows, cols = shape(kind)
                    w = weight_of[kind]
                    if w > seen:
                        pe.wait_ge(lo_done, w + 1)
                        pe.wait_ge(hi_done, w + 1)
                        seen = w
                    if n >= 4:
                        pe.wait_ge(job_f, n - 3)
                    out = ring[n % 4][rows, cols]
                    if kind[0] == "v":
                        last = matmuls(pe, out, lambda q, k: ctx_s[:, q, k, ix * J:(ix + 1) * J],
                                       lambda q, k: wk[:, w % 3, q, k, :])
                    else:
                        mm, h = ix
                        if kind == "m0" and n == 16:
                            pe.wait_ge(job_lo, 8)
                        src = k0 if kind == "m0" else ctx_s
                        last = matmuls(pe, out, lambda q, k: wk[:, w % 3, q, k, mm * P:(mm + 1) * P],
                                       lambda q, k: src[:, q, k, h * NH:(h + 1) * NH])
                    last.then_inc(job_mm, 1)
                    if n == 15:
                        pe.wait_ge(bq_done, KC)
                        pe.wait_ge(job_f, 8)
                        for h in range(2):
                            for k in range(KC):
                                last = pe.matmul(bps[h][:, 0:NH], bqb[:, k, :], k0f[:, k, h * NH:(h + 1) * NH],
                                                 start=k == 0, stop=k == KC - 1)
                            last.then_inc(bias_mm, 1)
                pe.wait_ge(id0, 2)
                pe.wait_ge(r_q, KC)
                for c in range(KC):
                    if c >= 2:
                        pe.wait_ge(r_out, c - 1)
                    for k in range(KC):
                        last = pe.transpose(xp[c % 2][:, k, :], rT[:, k, c * P:(c + 1) * P], g.ident[:, :])
                    last.then_inc(r_mm, 1)
                pe.wait_ge(r_dg, KC)
                pe.wait_ge(bias_out, 2)
                for k in range(KC):
                    last = pe.matmul(bps[0][:, k * P:(k + 1) * P], ones[:, :], dg[:, k, :], start=True, stop=True)
                last.then_inc(r_bc, 1)


def attention0(nc, g):
    with ExitStack() as ctx:
        m = Scope(nc, ctx, "attention0")
        ln = Norm(m, "a")
        xn = ln.xn
        xT = m.sb("xT", [P, 2, 2, KC, P], f16)
        sim = m.sb("sim", [P, 2, J])
        nmax = m.sb("nmax", [P, 2, 1])
        prob = m.sb("prob", [P, 2, J])
        y = m.sb("y", [P, 2, D])
        rsum = m.sb("rsum", [P, 4, 1])
        rinv = m.sb("rinv", [P, 4, 1])
        pT = m.sb("pT", [P, 2, 2, P], f16)
        ps_x = [m.ps(f"ps_x{i}", [P, KC, P]) for i in range(2)]
        ps_s = [m.ps(f"ps_s{i}", [P, D]) for i in range(2)]
        ps_p = [m.ps(f"ps_p{i}", [P, D]) for i in range(2)]
        ps_y = [m.ps(f"ps_y{i}", [P, D]) for i in range(2)]
        names = ("xt_mm", "xt_hi", "xt_lo", "sim_mm", "sim_ok",
                 "max_ok", "exp_ok", "sum_ok", "p_mm", "p_hi", "p_lo", "y_mm", "y_ok", "x_new")
        s = {n: m.sem("a0_" + n) for n in names}

        with nc.Block() as block:

            @block.gpsimd
            def _(pool):
                def step(t, d):
                    if live(t + 3):
                        ln.inverse_root(pool, g, t + 3, (d + 3) % 4)
                    u = t - 3
                    if live(u):
                        pool.wait_ge(s["y_ok"], u + 1)
                        pool.tensor_tensor(g.x[:, u, :], g.x[:, u, :], y[:, (d + 1) % 2], ALU.add).then_inc(s["x_new"], 1)
                pipeline(pool, step, 3, 3)

            @block.vector
            def _(dve):
                def step(t, d):
                    if live(t + 5) or live(t + 4):
                        ln.statistics(dve, g, t + 5, (d + 1) % 4)
                    u = t
                    if live(u):
                        c = d % 2
                        dve.wait_ge(s["sim_mm"], u + 1)
                        need(dve, s["exp_ok"], u - 1)
                        dve.scalar_tensor_tensor(sim[:, c], ps_s[c][:, 0:J], SC0, g.simb[:, bass.ds((u // TB) * J, J)],
                                                 ALU.mult, ALU.add).then_inc(s["sim_ok"], 1)
                        dve.wait_ge(s["sim_ok"], u + 1)
                        dve.tensor_reduce(nmax[:, c], sim[:, c], AX.X, ALU.max, negate=True).then_inc(s["max_ok"], 1)
                    u = t + 1
                    if live(u):
                        c = (d + 1) % 2
                        dve.wait_ge(s["xt_hi"], u + 1)
                        dve.tensor_tensor(xT[:, c, 1], ps_x[c][:, :, :], xT[:, c, 0], ALU.subtract).then_inc(s["xt_lo"], 1)
                    u = t - 1
                    if live(u):
                        c = (d + 1) % 2
                        dve.wait_ge(s["p_hi"], u + 1)
                        dve.tensor_tensor(pT[0:J, c, 1], ps_p[c][0:J, 0:P], pT[0:J, c, 0], ALU.subtract).then_inc(s["p_lo"], 1)
                        q = (d + 3) % 4
                        dve.wait_ge(s["exp_ok"], u + 1)
                        dve.reciprocal(rinv[:, q], rsum[:, q]).then_inc(s["sum_ok"], 1)
                    if live(t + 2):
                        ln.apply(dve, g, t + 2, (d + 2) % 4, s["xt_mm"])
                dve.wait_ge(g.x_in, 48)
                pipeline(dve, step, 5, 1)

            @block.scalar
            def _(act):
                def step(t, d):
                    u = t + 1
                    if live(u):
                        c = (d + 1) % 2
                        act.wait_ge(s["xt_mm"], u + 1)
                        need(act, s["sim_mm"], u - 1)
                        act.activation(xT[:, c, 0], ps_x[c][:, :, :], ACT.Copy).then_inc(s["xt_hi"], 1)
                    u = t - 1
                    if live(u):
                        c = (d + 1) % 2
                        act.wait_ge(s["p_mm"], u + 1)
                        need(act, s["y_mm"], u - 1)
                        act.activation(pT[0:J, c, 0], ps_p[c][0:J, 0:P], ACT.Copy).then_inc(s["p_hi"], 1)
                    u = t - 2
                    if live(u):
                        c, q = d % 2, (d + 2) % 4
                        act.wait_ge(s["y_mm"], u + 1)
                        act.wait_ge(s["sum_ok"], u + 1)
                        need(act, s["x_new"], u - 1)
                        act.activation(y[:, c], ps_y[c][:, :], ACT.Copy, scale=rinv[:, q]).then_inc(s["y_ok"], 1)
                    u = t
                    if live(u):
                        c = d % 2
                        act.wait_ge(s["max_ok"], u + 1)
                        need(act, s["p_mm"], u - 1)
                        need(act, s["sum_ok"], u - 3)
                        act.activation(prob[:, c], sim[:, c], ACT.Exp, bias=nmax[:, c],
                                       accum_out=rsum[:, d]).then_inc(s["exp_ok"], 1)
                pipeline(act, step, 1, 2)

            @block.tensor
            def _(pe):
                def step(t, d):
                    u = t
                    if live(u):
                        c = d % 2
                        pe.wait_ge(s["xt_lo"], u + 1)
                        need(pe, s["sim_ok"], u - 1)
                        j0 = (u // TB) * J
                        matmuls(pe, ps_s[c][:, 0:J], lambda q, k: xT[:, c, q, k, :],
                                lambda q, k: g.m0[:, q, k, bass.ds(j0, J)]).then_inc(s["sim_mm"], 1)
                    u = t - 1
                    if live(u):
                        c = (d + 1) % 2
                        pe.wait_ge(s["exp_ok"], u + 1)
                        need(pe, s["p_lo"], u - 1)
                        pe.transpose(ps_p[c][0:J, 0:P], prob[:, c], g.ident[:, :]).then_inc(s["p_mm"], 1)
                    u = t - 2
                    if live(u):
                        c = d % 2
                        pe.wait_ge(s["p_lo"], u + 1)
                        need(pe, s["y_ok"], u - 1)
                        b = u // TB
                        matmuls(pe, ps_y[c][:, :], lambda q, k: pT[0:J, c, q, :],
                                lambda q, k: g.v0[0:J, q, b, :], ks=(0,)).then_inc(s["y_mm"], 1)
                    u = t + 2
                    if live(u):
                        c = d % 2
                        pe.wait_ge(ln.ok, u + 1)
                        need(pe, s["xt_lo"], u - 1)
                        for k in range(KC):
                            last = pe.transpose(ps_x[c][:, k, :], xn[:, c, k * P:(k + 1) * P], g.ident[:, :])
                        last.then_inc(s["xt_mm"], 1)
                pipeline(pe, step, 2, 2)


class Norm:

    def __init__(self, m, name):
        self.st = m.sb(name + "_st", [P, 4, 6])
        self.mv = m.sb(name + "_mv", [P, 4, 2])
        self.ve = m.sb(name + "_ve", [P, 4, 1])
        self.rstd = m.sb(name + "_rstd", [P, 4, 1])
        self.xn = m.sb(name + "_xn", [P, 2, D])
        self.stats, self.aggr, self.var, self.root, self.ok = (
            m.sem(f"{name}_{n}") for n in ("stats", "aggr", "var", "root", "ok"))

    def statistics(self, dve, g, u, d):
        need(dve, self.stats, u)
        need(dve, self.root, u - 4)
        if live(u):
            dve.bn_stats(self.st[:, d], g.x[:, u, :]).then_inc(self.stats, 1)
        if live(u - 1):
            dve.bn_aggr(self.mv[:, (d + 3) % 4], self.st[:, (d + 3) % 4]).then_inc(self.aggr, 1)

    def inverse_root(self, pool, g, u, d):
        pool.wait_ge(self.aggr, u + 1)
        need(pool, self.ok, u - 3)
        pool.tensor_tensor(self.ve[:, d], self.mv[:, d, 1:2], g.eps[:, :], ALU.add).then_inc(self.var, 1)
        pool.wait_ge(self.var, u + 1)
        pool.tensor_tensor(self.rstd[:, d], self.ve[:, d], g.half[:, :], ALU.pow).then_inc(self.root, 1)

    def apply(self, dve, g, u, d, read, behind=1):
        dve.wait_ge(self.root, u + 1)
        need(dve, read, u - behind)
        dve.tensor_scalar(self.xn[:, d % 2], g.x[:, u, :], self.mv[:, d, 0:1], self.rstd[:, d], ALU.subtract,
                          ALU.mult).then_inc(self.ok, 1)


def quantised(nc, g):
    with ExitStack() as ctx:
        m = Scope(nc, ctx, "quantised")
        ln = Norm(m, "q")
        amax = m.sb("amax", [P, 4, 1])
        scale = m.sb("scale", [P, 4, 1])
        inv = m.sb("inv", [P, 4, 1])
        xr = m.sb("xr", [P, 2, D])
        qT = m.sb("qT", [P, 2, KC, P], bf16)
        y = m.sb("y", [P, 2, D])
        ps_x = [m.ps(f"ps_x{i}", [P, KC, P]) for i in range(2)]
        ps_y = [m.ps(f"ps_y{i}", [P, D]) for i in range(2)]
        s = {n: m.sem("q_" + n) for n in ("amax", "scale", "inv", "xr", "xt_mm", "xt_ok", "y_mm", "y_ok", "x_new")}

        with nc.Block() as block:

            @block.gpsimd
            def _(pool):
                def step(t, d):
                    u = t + 3
                    if live(u):
                        ln.inverse_root(pool, g, u, (d + 3) % 4)
                    u = t - 1
                    if live(u):
                        pool.wait_ge(s["y_ok"], u + 1)
                        pool.tensor_tensor(g.x[:, u, :], g.x[:, u, :], y[:, (d + 1) % 2], ALU.add).then_inc(s["x_new"], 1)
                pipeline(pool, step, 3, 1)

            @block.vector
            def _(dve):
                def step(t, d):
                    u, c = t + 3, (d + 3) % 4
                    if live(u):
                        ln.apply(dve, g, u, c, s["xr"])
                    if live(t + 5) or live(t + 4):
                        ln.statistics(dve, g, t + 5, (d + 1) % 4)
                    if live(u):
                        dve.wait_ge(ln.ok, u + 1)
                        dve.tensor_reduce(amax[:, c], ln.xn[:, c % 2], AX.X, ALU.max,
                                          apply_absolute_value=True).then_inc(s["amax"], 1)
                    if live(t):
                        dve.wait_ge(s["y_mm"], t + 1)
                        need(dve, s["x_new"], t - 1)
                        dve.scalar_tensor_tensor(y[:, d % 2], ps_y[d % 2][:, :], scale[:, d],
                                                 g.rs[:, :], ALU.mult, ALU.mult).then_inc(s["y_ok"], 1)
                    if live(u):
                        dve.wait_ge(s["amax"], u + 1)
                        need(dve, s["y_ok"], u - 3)
                        dve.tensor_scalar(scale[:, c], amax[:, c], 1e-12, 1 / 127.0, ALU.max, ALU.mult).then_inc(s["scale"], 1)
                        dve.wait_ge(s["scale"], u + 1)
                        need(dve, s["xr"], u - 3)
                        dve.reciprocal(inv[:, c], scale[:, c]).then_inc(s["inv"], 1)
                pipeline(dve, step, 5, 0)

            @block.scalar
            def _(act):
                def step(t, d):
                    u = t + 2
                    if live(u):
                        c = (d + 2) % 4
                        act.wait_ge(s["inv"], u + 1)
                        need(act, s["xt_mm"], u - 1)
                        act.activation(xr[:, c % 2], ln.xn[:, c % 2], ACT.Identity, scale=inv[:, c],
                                       bias=g.round_c[:, 0:1]).then_inc(s["xr"], 1)
                    u = t + 1
                    if live(u):
                        c = (d + 1) % 4
                        act.wait_ge(s["xt_mm"], u + 1)
                        need(act, s["y_mm"], u - 1)
                        act.activation(qT[:, c % 2], ps_x[c % 2][:, :, :], ACT.Identity,
                                       bias=g.round_c[:, 1:2]).then_inc(s["xt_ok"], 1)
                pipeline(act, step, 2, 0)

            @block.tensor
            def _(pe):
                def step(t, d):
                    u = t
                    if live(u):
                        pe.wait_ge(s["xt_ok"], u + 1)
                        need(pe, s["y_ok"], u - 1)
                        for k in range(KC):
                            last = pe.matmul(ps_y[d % 2][:, :], qT[:, d % 2, k, :], g.qr[:, k, :], start=k == 0, stop=k == KC - 1)
                        last.then_inc(s["y_mm"], 1)
                    u = t + 2
                    if live(u):
                        c = (d + 2) % 4
                        pe.wait_ge(s["xr"], u + 1)
                        need(pe, s["xt_ok"], u - 1)
                        for k in range(KC):
                            last = pe.transpose(ps_x[c % 2][:, k, :], xr[:, c % 2, k * P:(k + 1) * P], g.ident[:, :])
                        last.then_inc(s["xt_mm"], 1)
                pipeline(pe, step, 2, 0)


def attention1(nc, g):
    with ExitStack() as ctx:
        m = Scope(nc, ctx, "attention1")
        ln = Norm(m, "b")
        xT = m.sb("xT", [P, 2, 2, KC, P], f16)
        qT = m.sb("qT", [P, 2, 2, KC, P], f16)
        kbd = m.sb("kbd", [P, 2, KC, HC, J], f16)
        vst = m.sb("vst", [P, 2, D], f16)
        nmax = m.sb("nmax", [P, 2, KC, HC])
        prob = m.sb("prob", [P, 4, HC, J])
        pT = m.sb("pT", [P, 4, 2, HC, P], f16)
        rsum = m.sb("rsum", [P, 2, HEADS])
        rinv = m.sb("rinv", [P, 2, HEADS])
        wide = m.sb("wide", [P, D])
        rcp = m.sb("rcp", [P, KC, P])
        of = m.sb("of", [P, KC, P])
        oT = m.sb("oT", [P, 2, 2, KC, P], f16)
        ps_s = [m.ps(f"ps_s{i}", [P, D])[:, 0:HC * J].rearrange("p (h j) -> p h j", h=HC) for i in range(2)]
        ps_p = [m.ps(f"ps_p{i}", [P, HC, P]) for i in range(2)]
        ps_x = m.ps("ps_x", [P, KC, P])
        ps_q = m.ps("ps_q", [P, KC, P])
        ps_o = m.ps("ps_o", [P, KC, P])
        ps_r = m.ps("ps_r", [P, KC, P])
        ps_y = ps_r[:, :, :].rearrange("p k n -> p (k n)")
        s = {n: m.sem("b_" + n) for n in ("xt_mm", "xt_hi", "xt_lo", "q_mm", "q_hi", "q_lo", "inv", "wide", "r_mm", "rcp", "of", "o_hi",
                                          "o_lo", "y_mm", "x_new", "v_ok")}
        c4 = {n: m.sem("b4_" + n) for n in ("s_mm", "max", "exp", "p_mm", "p_hi", "p_lo", "o_mm", "k_ok", "zero")}

        with nc.Block() as block:

            @block.gpsimd
            def _(pool):
                def keys(b, c):
                    for h in range(HC):
                        rows = slice(h * DH, (h + 1) * DH)
                        need(pool, c4["k_ok"], HC * (KC * b + c) + h)
                        pool.tensor_copy(kbd[rows, :, c, h, :], g.k1[rows, :, c, bass.ds(b * J, J)]) \
                            .then_inc(c4["k_ok"], 1)

                def values(b):
                    pool.wait_ge(c4["k_ok"], HC * KC * (b + 1))
                    pool.tensor_copy(vst[0:J, :, :], g.v1[0:J, :, b, :]).then_inc(s["v_ok"], 1)
                    pool.wait_ge(s["v_ok"], b + 1)

                pool.memset(kbd[:, :, :, :, :], 0.0).then_inc(c4["zero"], 1)
                pool.wait_ge(c4["zero"], 1)
                for c in range(KC):
                    keys(0, c)
                values(0)

                def step(t, d):
                    u = t - 1
                    if live(u):
                        pool.wait_ge(s["inv"], u + 1)
                        need(pool, s["r_mm"], u)
                        src = rinv[:, (d + 1) % 2, :].rearrange("p (h o) -> p h o", o=1).to_broadcast([P, HEADS, DH])
                        pool.tensor_tensor(wide[:, :].rearrange("p (h o) -> p h o", h=HEADS), src,
                                           g.one[:, :].rearrange("p (h o) -> p h o", h=1).to_broadcast([P, HEADS, DH]),
                                           ALU.mult).then_inc(s["wide"], 1)
                    if live(u) and d == 0 and live(t):
                        pool.wait_ge(c4["o_mm"], KC * u + KC)
                        values(t // TB)
                    u = t + 3
                    if live(u):
                        ln.inverse_root(pool, g, u, (d + 3) % 4)
                    if live(t) and live(t + 1) and d == TB - 1:
                        for c in range(KC):
                            pool.wait_ge(c4["s_mm"], KC * t + c + 1)
                            keys(t // TB + 1, c)
                        pool.wait_ge(c4["k_ok"], HC * KC * (t // TB + 2))
                pipeline(pool, step, 3, 1)

            @block.vector
            def _(dve):
                def maximum(u, d, c):
                    dve.wait_ge(c4["s_mm"], KC * u + c + 1)
                    need(dve, c4["exp"], KC * (u - 2) + c + 1)
                    dve.tensor_reduce(nmax[:, d % 2, c], ps_s[c % 2][:, :, :], AX.X, ALU.max,
                                      negate=True).then_inc(c4["max"], 1)

                def prob_low(u, c):
                    dve.wait_ge(c4["p_hi"], KC * u + c + 1)
                    dve.tensor_tensor(pT[0:J, c, 1], ps_p[c % 2][0:J], pT[0:J, c, 0], ALU.subtract).then_inc(c4["p_lo"], 1)

                def step(t, d):
                    u = t - 1
                    if live(u):
                        q = (d + 1) % 2
                        dve.wait_ge(c4["exp"], KC * u + KC)
                        need(dve, s["wide"], u - 1)
                        dve.reciprocal(rinv[:, q, :], rsum[:, q, :]).then_inc(s["inv"], 1)
                    for c in range(KC):
                        if live(t):
                            maximum(t, d, c)
                        u = t + 1
                        if c == 1 and live(u):
                            q = (d + 1) % 2
                            dve.wait_ge(s["xt_hi"], u + 1)
                            dve.tensor_tensor(xT[:, q, 1], ps_x[:, :, :], xT[:, q, 0], ALU.subtract).then_inc(s["xt_lo"], 1)
                        u = t - 2
                        if c == 2 and live(u):
                            dve.wait_ge(s["y_mm"], u + 1)
                            dve.scalar_tensor_tensor(g.x[:, u, :], ps_y, 1 / WS, g.x[:, u, :], ALU.mult,
                                                     ALU.add).then_inc(s["x_new"], 1)
                        u = t + 1
                        if c == 3 and live(u):
                            q = (d + 1) % 2
                            dve.wait_ge(s["q_hi"], u + 1)
                            dve.scalar_tensor_tensor(qT[:, q, 1], ps_q[:, :, :], SC1 / WS, qT[:, q, 0], ALU.mult,
                                                     ALU.subtract).then_inc(s["q_lo"], 1)
                        if live(t - 1):
                            prob_low(t - 1, c)
                    if live(t + 5) or live(t + 4):
                        ln.statistics(dve, g, t + 5, (d + 1) % 4)
                    if live(t + 2):
                        ln.apply(dve, g, t + 2, (d + 2) % 4, s["xt_mm"])
                    u = t - 1
                    if live(u):
                        q = (d + 1) % 2
                        dve.wait_ge(c4["o_mm"], KC * u + KC)
                        dve.wait_ge(s["rcp"], u + 1)
                        need(dve, s["o_lo"], u)
                        need(dve, s["o_hi"], u)
                        dve.tensor_tensor(of[:, :, :], ps_o[:, :, :], rcp[:, :, :], ALU.mult).then_inc(s["of"], 1)
                        dve.wait_ge(s["of"], u + 1)
                        dve.wait_ge(s["o_hi"], u + 1)
                        dve.tensor_tensor(oT[:, q, 1], of[:, :, :], oT[:, q, 0], ALU.subtract).then_inc(s["o_lo"], 1)
                pipeline(dve, step, 5, 2)

            @block.scalar
            def _(act):
                def prob_high(u, c):
                    act.wait_ge(c4["p_mm"], KC * u + c + 1)
                    need(act, c4["o_mm"], KC * (u - 1) + c + 1)
                    act.activation(pT[0:J, c, 0], ps_p[c % 2][0:J], ACT.Copy).then_inc(c4["p_hi"], 1)

                def exps(u, d, c):
                    act.wait_ge(c4["max"], KC * u + c + 1)
                    need(act, s["inv"], u - 1)
                    need(act, c4["p_mm"], KC * (u - 1) + c + 1)
                    for h in range(HC):
                        n = c * HC + h
                        last = act.activation(prob[:, c, h, :], ps_s[c % 2][:, h, :], ACT.Exp, bias=nmax[:, d % 2, c, h:h + 1],
                                              accum_out=rsum[:, d % 2, n:n + 1])
                    last.then_inc(c4["exp"], 1)

                def step(t, d):
                    for c in range(KC):
                        u = t + 1
                        if c == 3 and live(u):
                            q = (d + 1) % 2
                            act.wait_ge(s["q_mm"], u + 1)
                            need(act, c4["s_mm"], KC * (u - 1))
                            act.activation(qT[:, q, 0], ps_q[:, :, :], ACT.Copy, scale=SC1 / WS).then_inc(s["q_hi"], 1)
                        if live(t - 1):
                            prob_high(t - 1, c)
                        if live(t):
                            exps(t, d, c)
                        u = t + 1
                        if c == 0 and live(u):
                            q = (d + 1) % 2
                            act.wait_ge(s["xt_mm"], u + 1)
                            need(act, s["q_mm"], u - 1)
                            act.activation(xT[:, q, 0], ps_x[:, :, :], ACT.Copy).then_inc(s["xt_hi"], 1)
                    if live(t - 1):
                        act.wait_ge(s["r_mm"], t)
                        need(act, s["of"], t - 1)
                        act.activation(rcp[:, :, :], ps_r[:, :, :], ACT.Copy).then_inc(s["rcp"], 1)
                    u = t - 1
                    if live(u):
                        q = (d + 1) % 2
                        act.wait_ge(s["of"], u + 1)
                        need(act, s["y_mm"], u - 1)
                        act.activation(oT[:, q, 0], of[:, :, :], ACT.Copy).then_inc(s["o_hi"], 1)
                pipeline(act, step, 1, 1)

            @block.tensor
            def _(pe):
                def scores(u, d, c):
                    q = d % 2
                    if c == 0:
                        pe.wait_ge(s["q_lo"], u + 1)
                    if d == 0:
                        pe.wait_ge(c4["k_ok"], KC * HC * (u // TB) + HC * c + HC)
                    need(pe, c4["exp"], KC * u + c - 1)
                    matmuls(pe, ps_s[c % 2][:, :, :], lambda a, _: qT[:, q, a, c, :], lambda a, _: kbd[:, a, c, :, :],
                            ks=(0,)).then_inc(c4["s_mm"], 1)

                def prob_transposed(u, c):
                    pe.wait_ge(c4["exp"], KC * u + c + 1)
                    need(pe, c4["p_lo"], KC * u + c - 1)
                    for h in range(HC):
                        last = pe.transpose(ps_p[c % 2][0:J, h, :], prob[:, c, h, :], g.ident[:, :])
                    last.then_inc(c4["p_mm"], 1)

                def outputs(u, d, c):
                    if c == 0:
                        need(pe, s["of"], u)
                        if d == 0:
                            pe.wait_ge(s["v_ok"], u // TB + 1)
                    pe.wait_ge(c4["p_lo"], KC * u + c + 1)
                    for n, (a, b) in enumerate(PASSES):
                        for h in range(HC):
                            rows = slice(h * DH, (h + 1) * DH)
                            col = (c * HC + h) * DH
                            last = pe.matmul(ps_o[rows, c, :], vst[0:J, a, col:col + DH], pT[0:J, c, b, h, :],
                                      start=n == 0, stop=n == 2)
                    last.then_inc(c4["o_mm"], 1)

                def step(t, d):
                    for c in range(KC):
                        if live(t):
                            scores(t, d, c)
                        if live(t - 1):
                            prob_transposed(t - 1, c)
                        u = t + 1
                        if c == 0 and live(u):
                            pe.wait_ge(ln.ok, u + 1)
                            need(pe, s["xt_lo"], u)
                            for k in range(KC):
                                last = pe.transpose(ps_x[:, k, :], ln.xn[:, (d + 1) % 2, k * P:(k + 1) * P], g.ident[:, :])
                            last.then_inc(s["xt_mm"], 1)
                        u = t - 2
                        if c == 1 and live(u):
                            pe.wait_ge(s["o_lo"], u + 1)
                            pe.wait_ge(s["rcp"], u + 1)
                            matmuls(pe, ps_y, lambda a, k: oT[:, d % 2, a, k, :], lambda a, k: g.wo1[:, a, k, :]) \
                                .then_inc(s["y_mm"], 1)
                        u = t + 1
                        if c == 2 and live(u):
                            pe.wait_ge(s["xt_lo"], u + 1)
                            need(pe, s["q_lo"], u)
                            for mm in range(KC):
                                last = matmuls(pe, ps_q[:, mm, :], lambda a, k: g.wq1[:, a, k, mm * P:(mm + 1) * P],
                                               lambda a, k: xT[:, (d + 1) % 2, a, k, :])
                            last.then_inc(s["q_mm"], 1)
                        if c >= 2 and live(t - 1):
                            outputs(t - 1, (d + 3) % 4, c - 2)
                        u = t - 1
                        if c == 3 and live(u):
                            pe.wait_ge(s["wide"], u + 1)
                            need(pe, s["x_new"], u)
                            for k in range(KC):
                                last = pe.transpose(ps_r[:, k, :], wide[:, k * P:(k + 1) * P], g.ident[:, :])
                            last.then_inc(s["r_mm"], 1)
                    if live(t - 1):
                        outputs(t - 1, (d + 3) % 4, 2)
                        outputs(t - 1, (d + 3) % 4, 3)
                pipeline(pe, step, 2, 2)


def gate(nc, g, io):
    with ExitStack() as ctx:
        m = Scope(nc, ctx, "gate")
        ln = Norm(m, "g")
        xT = m.sb("xT", [P, 2, 2, KC, P], f16)
        raw = m.sb("raw", [P, 2, 4 * IS])
        gwf = m.sb("gwf", [P, KC, E + 1])
        gws = m.sb("gws", [P, 2, KC, E + 1], f16)
        zero = m.sb("zero", [P, D])
        ps_x = [m.ps(f"ps_x{i}", [P, KC, P]) for i in range(2)]
        ps_l = [m.ps(f"ps_l{i}", [P, E + 1]) for i in range(2)]
        s = {n: m.sem(n) for n in ("xt_mm", "xt_hi", "xt_lo", "l_mm", "l_ok", "gw_in", "gw_hi", "gw_lo", "w_hi", "w_lo",
                                   "zero", "zero_out")}
        rows_out = [m.sem(f"rows_out{n}") for n in range(2)]
        xt_out = [m.sem(f"xt_out{n}") for n in range(2)]
        w_in = [m.sem(f"w_in{n}") for n in range(3)]
        srcs = [io["sh_gT"].rearrange("(k p) n -> p k n", p=P), io["sh_uT"].rearrange("(k p) n -> p k n", p=P),
                io["sh_dT"].rearrange("(c p) n -> p c n", p=P)]
        dsts = [g.wg, g.wu, g.wd]

        with nc.Block() as block:

            @block.sync
            def _(sp):
                sp.dma_start(gwf[:, :, :], io["gwT"].rearrange("(k p) n -> p k n", p=P)).then_inc(s["gw_in"], 16)
                for n in range(2):
                    sp.dma_start(raw[:, n].rearrange("p (k n) -> p k n", k=srcs[n].shape[1]), srcs[n]).then_inc(w_in[n], 16)
                sp.wait_ge(s["zero"], 1)
                for n in range(CAP // P):
                    rows = slice(T + n * P, T + (n + 1) * P)
                    sp.dma_start(io["xn_rows"][rows, :], zero[:, :]).then_inc(s["zero_out"], 16)
                    sp.dma_start(io["out"][rows, :], zero[:, :]).then_inc(s["zero_out"], 16)

                def step(t, d):
                    u = t
                    if live(u):
                        sp.wait_ge(ln.ok, u + 1)
                        sp.dma_start(io["xn_rows"][bass.ds(u * P, P), :], ln.xn[:, d % 2]).then_inc(rows_out[d % 2], 16)
                    u = t - 1
                    if live(u):
                        sp.wait_ge(s["xt_lo"], u + 1)
                        sp.dma_start(io["xt_tiles"][u, :, :], xT[:, (d + 1) % 2].rearrange("p q k n -> p (q k n)")) \
                            .then_inc(xt_out[(d + 1) % 2], 16)
                pipeline(sp, step, 0, 1)
                sp.wait_ge(s["w_hi"], 1)
                sp.wait_ge(s["w_lo"], 1)
                sp.dma_start(raw[:, 0].rearrange("p (c n) -> p c n", c=8), srcs[2]).then_inc(w_in[2], 16)
                for n in range(2):
                    sp.wait_ge(rows_out[n], 8 * NT)
                    sp.wait_ge(xt_out[n], 8 * NT)
                sp.wait_ge(s["zero_out"], 32 * (CAP // P))

            @block.gpsimd
            def _(pool):
                pool.memset(zero[:, :], 0.0).then_inc(s["zero"], 1)
                pool.wait_ge(s["zero"], 1)

                def step(t, d):
                    if live(t + 3):
                        ln.inverse_root(pool, g, t + 3, (d + 3) % 4)
                pipeline(pool, step, 3, 0)

            @block.vector
            def _(dve):
                def step(t, d):
                    if live(t + 5) or live(t + 4):
                        ln.statistics(dve, g, t + 5, (d + 1) % 4)
                    if live(t + 3):
                        need(dve, rows_out[(d + 3) % 2], 16 * ((t + 3) // 2))
                        ln.apply(dve, g, t + 3, (d + 3) % 4, s["xt_mm"])
                    u = t + 1
                    if live(u):
                        c = (d + 1) % 2
                        dve.wait_ge(s["xt_hi"], u + 1)
                        dve.tensor_tensor(xT[:, c, 1], ps_x[c][:, :, :], xT[:, c, 0], ALU.subtract).then_inc(s["xt_lo"], 1)
                    if live(t):
                        dve.wait_ge(s["l_mm"], t + 1)
                        dve.tensor_scalar(g.logits[:, t, :], ps_l[d % 2][:, :], 1 / WS, None, ALU.mult).then_inc(s["l_ok"], 1)
                dve.wait_ge(s["gw_hi"], 1)
                dve.scalar_tensor_tensor(gws[:, 1], gwf[:, :, :], WS, gws[:, 0], ALU.mult, ALU.subtract).then_inc(s["gw_lo"], 1)
                pipeline(dve, step, 5, 0)
                for n in range(3):
                    src = raw[:, n % 2].rearrange("p (k n) -> p k n", k=srcs[n].shape[1])
                    dve.wait_ge(s["w_hi"], n + 1)
                    dve.scalar_tensor_tensor(dsts[n][:, 1], src, WS, dsts[n][:, 0], ALU.mult, ALU.subtract).then_inc(s["w_lo"], 1)

            @block.scalar
            def _(act):
                def step(t, d):
                    u = t + 1
                    if live(u):
                        c = (d + 1) % 2
                        act.wait_ge(s["xt_mm"], u + 1)
                        need(act, s["l_mm"], u - 1)
                        need(act, xt_out[c], 16 * (u // 2))
                        act.activation(xT[:, c, 0], ps_x[c][:, :, :], ACT.Copy).then_inc(s["xt_hi"], 1)
                act.wait_ge(s["gw_in"], 16)
                act.activation(gws[:, 0], gwf[:, :, :], ACT.Copy, scale=WS).then_inc(s["gw_hi"], 1)
                pipeline(act, step, 1, 0)
                for n in range(3):
                    act.wait_ge(w_in[n], 16)
                    src = raw[:, n % 2].rearrange("p (k n) -> p k n", k=srcs[n].shape[1])
                    act.activation(dsts[n][:, 0], src, ACT.Copy, scale=WS).then_inc(s["w_hi"], 1)

            @block.tensor
            def _(pe):
                def step(t, d):
                    u = t + 2
                    if live(u):
                        c = d % 2
                        pe.wait_ge(ln.ok, u + 1)
                        need(pe, s["xt_lo"], u - 1)
                        for k in range(KC):
                            last = pe.transpose(ps_x[c][:, k, :], ln.xn[:, c, k * P:(k + 1) * P], g.ident[:, :])
                        last.then_inc(s["xt_mm"], 1)
                    if live(t):
                        pe.wait_ge(s["xt_lo"], t + 1)
                        need(pe, s["l_ok"], t - 1)
                        matmuls(pe, ps_l[d % 2][:, :], lambda a, k: xT[:, d % 2, a, k, :],
                                lambda a, k: gws[:, a, k, :]).then_inc(s["l_mm"], 1)
                pe.wait_ge(s["gw_lo"], 1)
                pipeline(pe, step, 2, 0)


TOPK = 4
TOP_P = 0.75
JITTER2 = 0.2
BIG = 1e30
OFF = float(1 << 20)


class Route:

    def __init__(self, m, g):
        A = lambda name: m.sb(name, [P, NT, E])
        V = lambda name: m.sb(name, [P, NT, 1])
        sm, alive, absl, rev, eq, pr, diff, fac, ex, keep = (
            A(n) for n in ("sm", "alive", "absl", "rev", "eq", "pr", "diff", "fac", "ex", "keep"))
        oh = [A(f"oh{k}") for k in range(TOPK)]
        rw, sel, cum0, cum1, pos, kept, wgt, slot = (A(n) for n in ("rw", "sel", "cum0", "cum1", "pos", "kept", "wgt", "slot"))
        thr = [V(f"thr{k}") for k in range(TOPK)]
        mult = [V(f"mult{k}") for k in range(TOPK)]
        mx, athr, z, z8, csum, pk, valid, rsum, sd, kk, sk = (
            V(n) for n in ("mx", "athr", "z", "z8", "csum", "pk", "valid", "rsum", "sd", "kk", "sk"))
        full = m.sb("full", [P, NT, E + 1])
        selb = m.sb("selb", [P, NT, E], bf16)
        tri = m.sb("tri", [P, P], bf16)
        one = m.sb("one", [P, P], bf16)
        erow = m.sb("erow", [P, NT, E], mybir.dt.int32)
        token = m.sb("token", [P, NT, 1], mybir.dt.int32)
        blank = m.sb("blank", [P, E * CAP // P, 2], mybir.dt.int32)
        load = m.sb("load", [P, NT, TOPK, 2], u32)
        index = m.sb("index", [P, NT, TOPK], u32)
        counts = m.sb("counts", [P, 2, NT, E])
        done = m.sem("done")
        consts, exp_in, exp_out, sel_ok, count_mm, counted, lists, blank_out, listed = (
            m.sem(n) for n in ("consts", "exp_in", "exp_out", "sel_ok", "count_mm", "counted", "lists", "blank_out", "listed"))
        wide = lambda v: v[:, :, 0:1].to_broadcast([P, NT, E])

        def constants(pool, io):
            pool.iota(erow[:, :, :], pattern=[[0, NT], [1, E]], base=0, channel_multiplier=0).then_inc(consts, 1)
            pool.iota(token[:, :, :], pattern=[[P, NT], [0, 1]], base=0, channel_multiplier=1).then_inc(consts, 1)
            pool.iota(blank[:, :, 0:1].rearrange("p (e n) c -> p e n c", e=E),
                      pattern=[[0, E], [P, CAP // P], [0, 1]], base=T, channel_multiplier=1).then_inc(consts, 1)
            pool.memset(blank[:, :, 1:2], 0).then_inc(consts, 1)
            pool.memset(one[:, :], 1.0).then_inc(consts, 1)
            pool.wait_ge(consts, 5)
            pool.affine_select(out=tri[:, :], in_=one[:, :], compare_op=ALU.is_ge, fill=0.0, base=0,
                               pattern=[[1, P]], channel_multiplier=-1).then_inc(consts, 1)
            pool.wait_ge(consts, 6)
            pool.dma_start(io["lists"].rearrange("(n p) c -> p n c", p=P), blank[:, :, :].bitcast(u32)).then_inc(blank_out, 16)
            pool.wait_ge(blank_out, 16)

        def scatter(pool, io):
            pool.wait_ge(lists, 1)
            for t in range(NT):
                for k in range(TOPK):
                    pool.indirect_dma_start(
                        out=io["lists"], out_offset=bass.IndirectOffsetOnAxis(ap=index[:, t, k:k + 1], axis=0),
                        in_=load[:, t, k, :], in_offset=None, bounds_check=E * CAP - 1, oob_is_err=False) \
                        .then_inc(listed, 16)
            pool.wait_ge(listed, 16 * NT * TOPK)

        def exponentials(act, piece):
            if piece < TOPK:
                act.wait_ge(exp_in, piece + 1)
                act.activation(ex[:, :, :], diff[:, :, :], ACT.Exp, scale=-1.0).then_inc(exp_out, 1)
            if piece == TOPK:
                for k in range(1, TOPK):
                    act.wait_ge(exp_in, TOPK + k)
                    act.activation(pk[:, :, :], sk[:, :, :], ACT.Exp).then_inc(exp_out, 1)
            if piece == TOPK + 2:
                act.wait_ge(exp_in, 2 * TOPK)
                act.activation(full[:, :, :], full[:, :, :], ACT.Exp).then_inc(exp_out, 1)

        def count(pe, bank):
            pe.wait_ge(consts, 6)
            pe.wait_ge(sel_ok, 1)
            pe.matmul(bank[:, 0], tri[:, :], selb[:, :, :], start=True, stop=True)
            pe.matmul(bank[:, 1], one[:, :], selb[:, :, :], start=True, stop=True).then_inc(count_mm, 1)

        def counted_wait(pe):
            pe.wait_ge(counted, 1)

        def pieces(dve, bank):
            chained = [0]

            def link(ins):
                chained[0] += 1
                ins.then_inc(done, 1)
                dve.wait_ge(done, chained[0])

            lg = g.logits[:, :, 0:E]
            tt, ts, stt = dve.tensor_tensor, dve.tensor_scalar, dve.scalar_tensor_tensor
            reduce = dve.tensor_reduce
            dve.wait_ge(consts, 6)
            link(dve.memset(alive[:, :, :], 1.0))
            link(dve.tensor_copy(sm[:, :, :], lg))
            link(stt(absl[:, :, :], lg, -1.0, lg, ALU.mult, ALU.max))
            link(ts(rev[:, :, :], erow[:, :, :], -1.0, float(E), ALU.mult, ALU.add))
            for k in range(TOPK):
                link(reduce(thr[k][:, :, :], sm[:, :, :], AX.X, ALU.max))
                link(tt(eq[:, :, :], sm[:, :, :], wide(thr[k]), ALU.is_equal))
                link(tt(pr[:, :, :], eq[:, :, :], rev[:, :, :], ALU.mult))
                link(reduce(mx[:, :, :], pr[:, :, :], AX.X, ALU.max))
                link(tt(oh[k][:, :, :], pr[:, :, :], wide(mx), ALU.is_equal))
                link(tt(fac[:, :, :], wide(thr[k]), lg, ALU.subtract))
                link(stt(athr[:, :, :], thr[k][:, :, :], -1.0, thr[k][:, :, :], ALU.mult, ALU.max))
                link(tt(keep[:, :, :], absl[:, :, :], wide(athr), ALU.max))
                link(stt(keep[:, :, :], keep[:, :, :], JITTER2, fac[:, :, :], ALU.mult, ALU.is_ge))
                link(tt(keep[:, :, :], keep[:, :, :], alive[:, :, :], ALU.mult))
                ts(diff[:, :, :], fac[:, :, :], 0.0, None, ALU.max).then_inc(exp_in, 1)
                dve.wait_ge(exp_out, k + 1)
                if k == 0:
                    link(reduce(z8[:, :, :], ex[:, :, :], AX.X, ALU.add))
                link(tt(keep[:, :, :], keep[:, :, :], ex[:, :, :], ALU.mult))
                link(reduce(z[:, :, :], keep[:, :, :], AX.X, ALU.add))
                link(dve.reciprocal(mult[k][:, :, :], z[:, :, :]))
                link(tt(alive[:, :, :], alive[:, :, :], oh[k][:, :, :], ALU.subtract))
                link(stt(sm[:, :, :], oh[k][:, :, :], -BIG, sm[:, :, :], ALU.mult, ALU.add))
                yield
            link(dve.reciprocal(z8[:, :, :], z8[:, :, :]))
            link(dve.tensor_copy(csum[:, :, :], z8[:, :, :]))
            link(tt(rw[:, :, :], oh[0][:, :, :], wide(mult[0]), ALU.mult))
            link(dve.tensor_copy(rsum[:, :, :], mult[0][:, :, :]))
            link(dve.tensor_copy(sel[:, :, :], oh[0][:, :, :]))
            for k in range(1, TOPK):
                tt(sk[:, :, :], thr[k][:, :, :], thr[0][:, :, :], ALU.subtract).then_inc(exp_in, 1)
                link(ts(valid[:, :, :], csum[:, :, :], TOP_P, None, ALU.is_lt))
                dve.wait_ge(exp_out, TOPK + k)
                link(tt(pk[:, :, :], pk[:, :, :], z8[:, :, :], ALU.mult))
                link(tt(csum[:, :, :], csum[:, :, :], pk[:, :, :], ALU.add))
                link(tt(mult[k][:, :, :], mult[k][:, :, :], valid[:, :, :], ALU.mult))
                link(tt(rsum[:, :, :], rsum[:, :, :], mult[k][:, :, :], ALU.add))
                link(tt(eq[:, :, :], oh[k][:, :, :], wide(mult[k]), ALU.mult))
                link(tt(rw[:, :, :], rw[:, :, :], eq[:, :, :], ALU.add))
                link(tt(eq[:, :, :], oh[k][:, :, :], wide(valid), ALU.mult))
                link(tt(sel[:, :, :], sel[:, :, :], eq[:, :, :], ALU.add))
            dve.tensor_copy(selb[:, :, :], sel[:, :, :]).then_inc(sel_ok, 1)
            link(dve.reciprocal(rsum[:, :, :], rsum[:, :, :]))
            link(tt(rw[:, :, :], rw[:, :, :], wide(rsum), ALU.mult))
            yield
            dve.wait_ge(count_mm, 1)
            dve.tensor_copy(counts[:, :, :, :], bank).then_inc(counted, 1)
            dve.wait_ge(counted, 1)
            link(dve.tensor_copy(cum0[:, :, :], counts[:, 1, :, :]))
            a, b, n = cum0, cum1, 1
            while n < NT:
                link(dve.tensor_copy(b[:, 0:n, :], a[:, 0:n, :]))
                link(tt(b[:, n:NT, :], a[:, n:NT, :], a[:, 0:NT - n, :], ALU.add))
                a, b, n = b, a, 2 * n
            link(tt(pos[:, :, :], a[:, :, :], counts[:, 1, :, :], ALU.subtract))
            link(tt(pos[:, :, :], pos[:, :, :], counts[:, 0, :, :], ALU.add))
            link(stt(kept[:, :, :], pos[:, :, :], float(CAP), sel[:, :, :], ALU.is_le, ALU.mult))
            yield
            link(ts(eq[:, :, :], kept[:, :, :], BIG, -BIG, ALU.mult, ALU.add))
            link(tt(full[:, :, 0:E], lg, eq[:, :, :], ALU.add))
            link(dve.tensor_copy(full[:, :, E:E + 1], g.logits[:, :, E:E + 1]))
            link(reduce(mx[:, :, :], full[:, :, :], AX.X, ALU.max))
            tt(full[:, :, :], full[:, :, :], mx[:, :, 0:1].to_broadcast([P, NT, E + 1]), ALU.subtract).then_inc(exp_in, 1)
            dve.wait_ge(exp_out, 2 * TOPK)
            link(reduce(z[:, :, :], full[:, :, :], AX.X, ALU.add))
            link(reduce(sd[:, :, :], full[:, :, 0:E], AX.X, ALU.add))
            link(dve.reciprocal(z[:, :, :], z[:, :, :]))
            link(ts(z[:, :, :], z[:, :, :], 1 / (WS * HS), None, ALU.mult))
            link(tt(g.gsh[:, :, :], full[:, :, E:E + 1], z[:, :, :], ALU.mult))
            link(tt(sd[:, :, :], sd[:, :, :], z[:, :, :], ALU.mult))
            link(tt(wgt[:, :, :], rw[:, :, :], wide(sd), ALU.mult))
            link(tt(wgt[:, :, :], wgt[:, :, :], kept[:, :, :], ALU.mult))
            yield
            link(stt(slot[:, :, :], erow[:, :, :], float(CAP), pos[:, :, :], ALU.mult, ALU.add))
            link(ts(slot[:, :, :], slot[:, :, :], -1.0 - OFF, None, ALU.add))
            link(tt(slot[:, :, :], slot[:, :, :], kept[:, :, :], ALU.mult))
            for k in range(TOPK):
                link(tt(eq[:, :, :], oh[k][:, :, :], slot[:, :, :], ALU.mult))
                link(reduce(sk[:, :, :], eq[:, :, :], AX.X, ALU.add))
                link(ts(index[:, :, k:k + 1], sk[:, :, :], OFF, None, ALU.add))
                link(tt(eq[:, :, :], oh[k][:, :, :], wgt[:, :, :], ALU.mult))
                link(reduce(load[:, :, k, 1:2].bitcast(f32), eq[:, :, :], AX.X, ALU.add))
                link(dve.tensor_copy(load[:, :, k, 0:1], token[:, :, :]))
            dve.tensor_copy(sk[:, :, :], sk[:, :, :]).then_inc(lists, 1)
            yield

        self.constants, self.scatter, self.exponentials = constants, scatter, exponentials
        self.count, self.counted_wait, self.pieces = count, counted_wait, pieces


def shared(nc, g, io):
    NC = IS // P
    with ExitStack() as ctx:
        m = Scope(nc, ctx, "shared")
        xT = m.sb("xT", [P, 2, 2, KC, S], f16)
        sg = m.sb("sg", [P, 2, S])
        hf = m.sb("hf", [P, 2, S])
        hid = m.sb("hid", [P, 2, 2, S], f16)
        res = m.sb("res", [P, TB, D])
        ps_g = [m.ps(f"ps_g{i}", [P, S]) for i in range(2)]
        ps_u = [m.ps(f"ps_u{i}", [P, S]) for i in range(2)]
        ps_y = [m.ps(f"ps_y{i}", [P, D]) for i in range(TB)]
        s = {n: m.sem(n) for n in ("g_mm", "u_mm", "silu", "hf", "h_hi", "h_lo", "d_mm", "y_ok", "warm")}
        x_in = [m.sem(f"x_in{n}") for n in range(2)]
        out_done = m.sem("out_done")
        routing = Route(m, g)
        bank = ps_u[0][:, :].rearrange("p (a t e) -> p a t e", a=2, e=E)
        BORROW = 6

        def ok(b):
            return not isinstance(b, int) or 0 <= b < B

        with nc.Block() as block:

            @block.sync
            def _(sp):
                def step(b, d):
                    if ok(b + 1):
                        c = (d + 1) % 2
                        need(sp, s["u_mm"], NC * b)
                        for i in range(TB):
                            src = io["xt_tiles"][(b + 1) * TB + i, :, :].rearrange("p (a n) -> p a n", n=P)
                            sp.dma_start(xT[:, c, :, :, i * P:(i + 1) * P].rearrange("p q k n -> p (q k) n"), src) \
                                .then_inc(x_in[c], 16)
                    if ok(b - 1):
                        for i in range(TB):
                            sp.wait_ge(s["y_ok"], TB * (b - 1) + i + 1)
                            sp.dma_start(io["out"][bass.ds(((b - 1) * TB + i) * P, P), :], res[:, i]).then_inc(out_done, 16)
                pipeline(sp, step, 1, 1, B, 2)
                sp.wait_ge(out_done, 16 * NT)

            @block.gpsimd
            def _(pool):
                routing.constants(pool, io)
                routing.scatter(pool, io)

            @block.scalar
            def _(act):
                act.activation(sg[:, 0, 0:1], g.half[:, 0:1], ACT.Silu).then_inc(s["warm"], 1)
                act.wait_ge(s["warm"], 1)

                def step(b, d):
                    for c in range(NC):
                        v = NC * b + c
                        act.wait_ge(s["g_mm"], v + 1)
                        need(act, s["hf"], v - 1)
                        act.activation(sg[:, c % 2], ps_g[c % 2][:, :], ACT.Silu, scale=1 / WS).then_inc(s["silu"], 1)
                        act.wait_ge(s["hf"], v + 1)
                        need(act, s["d_mm"], v - 1)
                        act.activation(hid[:, c % 2, 0], hf[:, c % 2], ACT.Copy).then_inc(s["h_hi"], 1)
                        if isinstance(b, int) and b == 0:
                            routing.exponentials(act, c)
                pipeline(act, step, 0, 0, B, 2)

            @block.vector
            def _(dve):
                pieces = routing.pieces(dve, bank)

                def step(b, d):
                    for c in range(NC):
                        if ok(b):
                            v = NC * b + c
                            dve.wait_ge(s["silu"], v + 1)
                            dve.wait_ge(s["u_mm"], v + 1)
                            need(dve, s["h_hi"], v - 1)
                            need(dve, s["h_lo"], v - 1)
                            dve.scalar_tensor_tensor(hf[:, c % 2], ps_u[c % 2][:, :], HS / WS, sg[:, c % 2], ALU.mult,
                                                     ALU.mult).then_inc(s["hf"], 1)
                            dve.wait_ge(s["h_hi"], v + 1)
                            dve.tensor_tensor(hid[:, c % 2, 1], hf[:, c % 2], hid[:, c % 2, 0], ALU.subtract).then_inc(s["h_lo"], 1)
                            if isinstance(b, int) and b == 0:
                                next(pieces)
                        if c == 0 and ok(b - 1):
                            t0 = (b - 1) * TB
                            dve.wait_ge(s["d_mm"], NC * b)
                            need(dve, out_done, 16 * t0)
                            for i in range(TB):
                                dve.scalar_tensor_tensor(res[:, i], ps_y[i][:, :], g.gsh[:, t0 + i, :], g.x[:, t0 + i, :],
                                                         ALU.mult, ALU.add).then_inc(s["y_ok"], 1)
                pipeline(dve, step, 0, 1, B, 2)

            @block.tensor
            def _(pe):
                def down(v, c):
                    pe.wait_ge(s["h_lo"], v + 1)
                    for n, (a, b) in enumerate(PASSES):
                        for i in range(TB):
                            last = pe.matmul(ps_y[i][:, :], hid[:, c % 2, a, i * P:(i + 1) * P], g.wd[:, b, c, :],
                                             start=c == 0 and n == 0, stop=c == NC - 1 and n == 2)
                    last.then_inc(s["d_mm"], 1)

                def step(b, d):
                    for c in range(NC):
                        v = NC * b + c
                        if ok(b):
                            if c == 0:
                                if isinstance(b, int):
                                    pe.wait_ge(x_in[d % 2], 16 * TB * (b // 2 + 1))
                                else:
                                    pe.wait_ge(x_in[d % 2], 16 * TB * (b // 2 + 1))
                            if isinstance(b, int) and b == 0 and c == BORROW:
                                pe.wait_ge(s["hf"], v - 1)
                                routing.count(pe, bank)
                            need(pe, s["silu"], v - 1)
                            matmuls(pe, ps_g[c % 2][:, :], lambda a, k: g.wg[:, a, k, c * P:(c + 1) * P],
                                    lambda a, k: xT[:, d % 2, a, k, :]).then_inc(s["g_mm"], 1)
                            if isinstance(b, int) and b == 0 and c == BORROW:
                                routing.counted_wait(pe)
                            need(pe, s["hf"], v - 1)
                            matmuls(pe, ps_u[c % 2][:, :], lambda a, k: g.wu[:, a, k, c * P:(c + 1) * P],
                                    lambda a, k: xT[:, d % 2, a, k, :]).then_inc(s["u_mm"], 1)
                        if c == 0 and ok(b - 1):
                            down(v - 1, NC - 1)
                        if c > 0 and ok(b):
                            if c == 1:
                                need(pe, s["y_ok"], TB * b)
                            down(v - 1, c - 1)
                pipeline(pe, step, 0, 1, B, 2)


def experts(nc, g, io):
    CT = CAP // P
    HN = CAP // 2
    NI = IE // P
    WN = 2 * KC * IE + NI * D
    with ExitStack() as ctx:
        m = Scope(nc, ctx, "experts")
        raw = m.sb("raw", [P, 2, WN])
        w = m.sb("w", [P, 2, 2, WN], f16)
        lst = m.sb("lst", [P, E * CT, 2], u32)
        xg = m.sb("xg", [P, 2, CT, D])
        xT = m.sb("xT", [P, 2, 2, KC, CAP], f16)
        sg = m.sb("sg", [P, 2, HN])
        hf = m.sb("hf", [P, 2, HN])
        hid = m.sb("hid", [P, 2, 2, NI, CAP], f16)
        res = m.sb("res", [P, 2, CT, D])
        ps_x = [m.ps(f"ps_x{i}", [P, KC, P]) for i in range(2)]
        ps_g = [m.ps(f"ps_g{i}", [P, HN]) for i in range(2)]
        ps_u = [m.ps(f"ps_u{i}", [P, HN]) for i in range(2)]
        ps_y = [m.ps(f"ps_y{i}", [P, D]) for i in range(2)]
        s = {n: m.sem(n) for n in ("w_hi", "w_lo", "xt_mm", "xt_hi", "xt_lo", "g_mm", "u_mm", "silu", "hf", "h_hi", "h_lo",
                                   "y_mm", "y_ok", "warm", "added")}
        l_in = m.sem("l_in")
        w_in = [m.sem(f"w_in{n}") for n in range(2)]
        x_in = [m.sem(f"x_in{n}") for n in range(2)]
        gk = lambda v, k: v[:, k * IE:(k + 1) * IE]
        UNITS = [(h, i) for h in range(2) for i in range(NI)]

        def ok(e):
            return not isinstance(e, int) or 0 <= e < E

        with nc.Block() as block:

            @block.sync
            def _(sp):
                def step(e, d):
                    u = e + 2
                    if ok(u):
                        c = d % 2
                        need(sp, s["w_hi"], u - 1)
                        need(sp, s["w_lo"], u - 1)
                        sp.dma_start(raw[:, c, 0:KC * IE].rearrange("p (k n) -> p k n", k=KC),
                                     io["dyn_gT"][u, :, :].rearrange("(k p) n -> p k n", p=P)).then_inc(w_in[c], 16)
                        sp.dma_start(raw[:, c, KC * IE:2 * KC * IE].rearrange("p (k n) -> p k n", k=KC),
                                     io["dyn_uT"][u, :, :].rearrange("(k p) n -> p k n", p=P)).then_inc(w_in[c], 16)
                        sp.dma_start(raw[:, c, 2 * KC * IE:WN].rearrange("p (k n) -> p k n", k=NI),
                                     io["dyn_dT"][u, :, :].rearrange("(k p) n -> p k n", p=P)).then_inc(w_in[c], 16)
                sp.dma_start(lst[:, :, :], io["lists"].rearrange("(n p) c -> p n c", p=P)).then_inc(l_in, 16)
                pipeline(sp, step, 2, 0, E, 2)

            @block.gpsimd
            def _(pool):
                def step(e, d):
                    u = e + 2
                    if ok(u):
                        c = d % 2
                        need(pool, s["xt_mm"], CT * (u - 1))
                        for n in range(CT):
                            pool.indirect_dma_start(
                                out=xg[:, c, n, :], out_offset=None, in_=io["xn_rows"],
                                in_offset=bass.IndirectOffsetOnAxis(ap=lst[:, u * CT + n, 0:1], axis=0)).then_inc(x_in[c], 16)
                    u = e - 1
                    if ok(u):
                        c = (d + 1) % 2
                        need(pool, s["added"], 16 * CT * u)
                        for n in range(CT):
                            pool.wait_ge(s["y_ok"], CT * u + n + 1)
                            pool.indirect_dma_start(
                                out=io["out"], out_offset=bass.IndirectOffsetOnAxis(ap=lst[:, u * CT + n, 0:1], axis=0),
                                in_=res[:, c, n, :], in_offset=None, compute_op=ALU.add).then_inc(s["added"], 16)
                pool.wait_ge(l_in, 16)
                for e in range(-2, E + 1):
                    step(e, e % 2)
                pool.wait_ge(s["added"], 16 * CT * E)

            @block.scalar
            def _(act):
                act.activation(sg[:, 0, 0:1], g.half[:, 0:1], ACT.Silu).then_inc(s["warm"], 1)
                act.wait_ge(s["warm"], 1)

                def unit(u, d, n):
                    v = 4 * u + n
                    h, i = UNITS[n]
                    act.wait_ge(s["g_mm"], v + 1)
                    need(act, s["hf"], v - 1)
                    act.activation(sg[:, n % 2], ps_g[n % 2][:, :], ACT.Silu, scale=1 / WS).then_inc(s["silu"], 1)
                    act.wait_ge(s["hf"], v + 1)
                    need(act, s["y_mm"], CT * (u - 1))
                    act.activation(hid[:, d % 2, 0, i, h * HN:(h + 1) * HN], hf[:, n % 2], ACT.Copy).then_inc(s["h_hi"], 1)

                act.wait_ge(l_in, 16)

                def step(e, d):
                    if ok(e):
                        unit(e, d, 0)
                        unit(e, d, 1)
                    u = e - 1
                    if ok(u):
                        c = (d + 1) % 2
                        for n in range(CT):
                            act.wait_ge(s["y_mm"], CT * u + n + 1)
                            if n == 0:
                                need(act, s["added"], 16 * CT * (u - 1))
                            act.activation(res[:, c, n], ps_y[n % 2][:, :], ACT.Copy,
                                           scale=lst[:, u * CT + n, 1:2].bitcast(f32)).then_inc(s["y_ok"], 1)
                    u = e + 1
                    if ok(u):
                        c = (d + 1) % 2
                        act.wait_ge(w_in[c], 48 * (u // 2 + 1))
                        need(act, s["y_mm"], CT * (u - 1))
                        act.activation(w[:, c, 0], raw[:, c], ACT.Copy, scale=WS).then_inc(s["w_hi"], 1)
                    if ok(e):
                        unit(e, d, 2)
                        unit(e, d, 3)
                    u = e + 1
                    if ok(u):
                        c = (d + 1) % 2
                        for n in range(CT):
                            act.wait_ge(s["xt_mm"], CT * u + n + 1)
                            if n == 0:
                                need(act, s["u_mm"], 4 * (u - 1))
                            act.activation(xT[:, c, 0, :, n * P:(n + 1) * P], ps_x[n % 2][:, :, :], ACT.Copy).then_inc(s["xt_hi"], 1)
                pipeline(act, step, 1, 1, E, 2)

            @block.vector
            def _(dve):
                def unit(u, d, n):
                    v = 4 * u + n
                    h, i = UNITS[n]
                    cols = slice(h * HN, (h + 1) * HN)
                    dve.wait_ge(s["silu"], v + 1)
                    dve.wait_ge(s["u_mm"], v + 1)
                    need(dve, s["h_hi"], v - 1)
                    need(dve, s["h_lo"], v - 1)
                    dve.scalar_tensor_tensor(hf[:, n % 2], ps_u[n % 2][:, :], HS / WS, sg[:, n % 2], ALU.mult,
                                             ALU.mult).then_inc(s["hf"], 1)
                    dve.wait_ge(s["h_hi"], v + 1)
                    dve.tensor_tensor(hid[:, d % 2, 1, i, cols], hf[:, n % 2], hid[:, d % 2, 0, i, cols],
                                      ALU.subtract).then_inc(s["h_lo"], 1)

                def step(e, d):
                    if ok(e):
                        for n in range(3):
                            unit(e, d, n)
                    u = e + 1
                    if ok(u):
                        c = (d + 1) % 2
                        dve.wait_ge(s["w_hi"], u + 1)
                        dve.scalar_tensor_tensor(w[:, c, 1], raw[:, c], WS, w[:, c, 0], ALU.mult,
                                                 ALU.subtract).then_inc(s["w_lo"], 1)
                    if ok(e):
                        unit(e, d, 3)
                    u = e + 1
                    if ok(u):
                        c = (d + 1) % 2
                        for n in range(CT):
                            dve.wait_ge(s["xt_hi"], CT * u + n + 1)
                            cols = slice(n * P, (n + 1) * P)
                            dve.tensor_tensor(xT[:, c, 1, :, cols], ps_x[n % 2][:, :, :], xT[:, c, 0, :, cols],
                                              ALU.subtract).then_inc(s["xt_lo"], 1)
                pipeline(dve, step, 1, 0, E, 2)

            @block.tensor
            def _(pe):
                def unit(u, d, n):
                    v = 4 * u + n
                    h, i = UNITS[n]
                    c = d % 2
                    if n == 0:
                        pe.wait_ge(s["w_lo"], u + 1)
                    for bank, sem, read, at in ((ps_g, "g_mm", "silu", 0), (ps_u, "u_mm", "hf", KC * IE)):
                        need(pe, s[read], v - 1)
                        if n % 2 == 0 and at == 0:
                            pe.wait_ge(s["xt_lo"], CT * u + (3 if h == 0 else CT))
                        matmuls(pe, bank[n % 2][:, :],
                                lambda a, k: w[:, c, a, at + k * IE + i * P:at + k * IE + (i + 1) * P],
                                lambda a, k: xT[:, c, a, k, h * HN:(h + 1) * HN]).then_inc(s[sem], 1)

                def step(e, d):
                    if ok(e):
                        unit(e, d, 0)
                        unit(e, d, 1)
                    u = e - 1
                    if ok(u):
                        c = (d + 1) % 2
                        for n in range(CT):
                            pe.wait_ge(s["h_lo"], 4 * u + 4)
                            need(pe, s["y_ok"], CT * u + n - 1)
                            matmuls(pe, ps_y[n % 2][:, :], lambda a, i: hid[:, c, a, i, n * P:(n + 1) * P],
                                    lambda a, i: w[:, c, a, 2 * KC * IE + i * D:2 * KC * IE + (i + 1) * D],
                                    ks=range(NI)).then_inc(s["y_mm"], 1)
                    if ok(e):
                        unit(e, d, 2)
                        unit(e, d, 3)
                    u = e + 1
                    if ok(u):
                        c = (d + 1) % 2
                        pe.wait_ge(x_in[c], 16 * CT * (u // 2 + 1))
                        for n in range(CT):
                            need(pe, s["xt_lo"], CT * u + n - 1)
                            for k in range(KC):
                                last = pe.transpose(ps_x[n % 2][:, k, :], xg[:, c, n, k * P:(k + 1) * P], g.ident[:, :])
                            last.then_inc(s["xt_mm"], 1)
                pipeline(pe, step, 1, 1, E, 2)


class State:
    pass


def program(nc, io, out, stop=9):
    Scope.semaphores = []
    with ExitStack() as ctx:
        m = Scope(nc, ctx, "program")
        g = State()
        g.x = m.sb("x", [P, NT, D])
        g.ident = m.sb("ident", [P, P])
        g.half = m.sb("half", [P, 1])
        g.round_c = m.sb("round_c", [P, 2])
        g.eps = m.sb("eps", [P, 1])
        g.one = m.sb("one", [P, 1])
        g.x_in = m.sem("x_in")
        with ExitStack() as actx:
            a = Scope(nc, actx, "att")
            g.m0 = a.sb("m0", [P, 2, KC, JB], f16)
            g.simb = a.sb("simb", [P, JB])
            g.v0 = a.sb("v0", [P, 2, B, D], f16)
            g.k1 = a.sb("k1", [P, 2, KC, JB], f16)
            g.v1 = a.sb("v1", [P, 2, B, D], f16)
            g.wq1 = a.sb("wq1", [P, 2, KC, D], f16)
            g.wo1 = a.sb("wo1", [P, 2, KC, D], f16)
            g.qr = a.sb("qr", [P, KC, D], bf16)
            g.rs = a.sb("rs", [P, D])
            setup(nc, g, io)
            if stop >= 1:
                attention0(nc, g)
            if stop >= 2:
                quantised(nc, g)
            if stop >= 3:
                attention1(nc, g)
        Scope.clear_semaphores(nc)
        if stop < 4:
            done = m.sem("done")
            with nc.Block() as block:
                @block.sync
                def _(sp):
                    sp.dma_start(out.rearrange("(t p) d -> p t d", p=P), g.x[:, :, :]).then_inc(done, 16)
                    sp.wait_ge(done, 16)
            return
        io = dict(io, out=out)
        io["xn_rows"] = nc.dram_tensor("xn_rows", [T + CAP, D], f32, kind="Internal").ap()
        io["xt_tiles"] = nc.dram_tensor("xt_tiles", [NT, P, 2 * KC * P], f16, kind="Internal").ap()
        io["lists"] = nc.dram_tensor("lists", [E * CAP, 2], u32, kind="Internal").ap()
        with ExitStack() as fctx:
            f = Scope(nc, fctx, "ffn")
            g.logits = f.sb("logits", [P, NT, E + 1])
            g.gsh = f.sb("gsh", [P, NT, 1])
            g.wg = f.sb("wg", [P, 2, KC, IS], f16)
            g.wu = f.sb("wu", [P, 2, KC, IS], f16)
            g.wd = f.sb("wd", [P, 2, IS // P, D], f16)
            gate(nc, g, io)
            shared(nc, g, io)
        experts(nc, g, io)


def layout(a):
    import numpy as np
    c = np.ascontiguousarray

    def chunks(v):
        return c(v.reshape(KC, P).T)

    return {
        "x": c(a["x"].reshape(T, D)),
        "ctxT": c(a["ctx_1024"].reshape(JB, D).T),
        "L0_Wk": c(a["L0_xattn_Wk"]), "L0_Wv": c(a["L0_xattn_Wv"]), "L0_WqT": c(a["L0_xattn_Wq"].T),
        "L0_bq": chunks(a["L0_xattn_bq"]), "L0_bk": chunks(a["L0_xattn_bk"]), "L0_bv": c(a["L0_xattn_bv"]),
        "L0_rhsT": c(a["L0_ffn_rhs"].T),
        "L1_wqT": c(a["L1_xattn_w_q"].T), "L1_wkT": c(a["L1_xattn_w_k"].T),
        "L1_wvT": c(a["L1_xattn_w_v"].T), "L1_woT": c(a["L1_xattn_w_o"].T),
        "gwT": c(a["L1_ffn_gate_w"].T),
        "dyn_gT": c(a["L1_ffn_dyn_gate_w"].transpose(0, 2, 1)), "dyn_uT": c(a["L1_ffn_dyn_up_w"].transpose(0, 2, 1)),
        "dyn_dT": c(a["L1_ffn_dyn_down_w"].transpose(0, 2, 1)),
        "sh_gT": c(a["L1_ffn_sh_gate_w"][0].T), "sh_uT": c(a["L1_ffn_sh_up_w"][0].T),
        "sh_dT": c(a["L1_ffn_sh_down_w"][0].T),
    }


def kernel(**inputs):
    import numpy as np
    import concourse.bacc as bacc
    from concourse.bass_utils import run_bass_kernel_spmd

    nc = bacc.Bacc("TRN2", target_bir_lowering=False, num_devices=1)
    arrays = layout({name: np.asarray(v) for name, v in inputs.items()})
    io = {name: nc.dram_tensor("in_" + name, v.shape, mybir.dt.from_np(v.dtype), kind="ExternalInput").ap()
          for name, v in arrays.items()}
    out = nc.dram_tensor("out_rows", (T + CAP, D), f32, kind="ExternalOutput").ap()
    program(nc, io, out)
    r = run_bass_kernel_spmd(nc, [{"in_" + name: v for name, v in arrays.items()}], core_ids=[0])
    return r.results[0]["out_rows"][0:T].reshape(B, S, D)
```

```python
import concourse.bass as bass
from concourse import mybir
from contextlib import ExitStack

f32 = mybir.dt.float32
f16 = mybir.dt.float16
bf16 = mybir.dt.bfloat16
u32 = mybir.dt.uint32
ALU = mybir.AluOpType
ACT = mybir.ActivationFunctionType
AX = mybir.AxisListType

P = 128
B, S, D = 8, 512, 512
J = 120
T = B * S
NT = T // P
TB = S // P
KC = D // P
JB = B * J
HEADS, DH = 16, 32
HC = P // DH
E = 8
IE, IS = 256, 1024
CAP = 640
EPS = 1e-5
WS = 64.0
HS = 1.0 / 16
CT = CAP // P
WN = 2 * KC * IE + IE // P * D
SC0 = float(D) ** -0.5
SC1 = float(DH) ** -0.5
PASSES = ((0, 0), (1, 0), (0, 1))
ROUND = 1.5 * 2.0 ** 23


def need(eng, sem, n):
    if isinstance(n, int) and n <= 0:
        return
    eng.wait_ge(sem, n)


def live(t):
    return not isinstance(t, int) or 0 <= t < NT


def pipeline(eng, step, lead, lag, n=NT, by=TB, head=None):
    first = (head or by) // by
    end = (n - lead) // by
    for s in range(-lead, first * by):
        step(s, s % by)
    with eng.Fori(first, end) as i:
        for d in range(by):
            step(i * by + d, d)
    for s in range(end * by, n + lag):
        step(s, s % by)


class Scope:

    semaphores: list = []

    def __init__(self, nc, ctx, stage):
        self.nc, self.ctx, self.stage = nc, ctx, stage + "_"

    def sb(self, name, shape, dt=f32):
        return self.ctx.enter_context(self.nc.sbuf_tensor(self.stage + name, shape, dt))

    def ps(self, name, shape, dt=f32):
        return self.ctx.enter_context(self.nc.psum_tensor(self.stage + name, shape, dt))

    def sem(self, name):
        handle = self.nc.alloc_semaphore(self.stage + name)
        Scope.semaphores.append(handle)
        return handle

    @classmethod
    def clear_semaphores(cls, nc):
        nc.clear_and_free_semaphores(cls.semaphores)
        nc.all_engine_barrier()
        cls.semaphores = []


def matmuls(pe, out, lhs, rhs, ks=range(KC)):
    terms = [(k, a, b) for k in ks for a, b in PASSES]
    for n, (k, a, b) in enumerate(terms):
        last = pe.matmul(out, lhs(a, k), rhs(b, k), start=n == 0, stop=n == len(terms) - 1)
    return last


def block_keys(pool, g, b, c):
    for h in range(HC):
        rows = slice(h * DH, (h + 1) * DH)
        need(pool, g.keys_ok, HC * (KC * b + c) + h)
        pool.tensor_copy(g.kbd[rows, :, c, h, :], g.k1[rows, :, c, bass.ds(b * J, J)]).then_inc(g.keys_ok, 1)


def setup(nc, g, io):
    with ExitStack() as ctx:
        m = Scope(nc, ctx, "setup")
        W = ["L0_Wk", "L0_Wv", "L0_WqT", "L1_wkT", "L1_wvT", "L1_wqT", "L1_woT", "L0_rhs"]
        NW = len(W)
        raw = g.x[:, NT - 12:NT, :].rearrange("p (w k) n -> p w k n", w=3)
        ctx_s = m.sb("ctx_s", [P, 2, KC, JB], f16)
        wk = g.x[:, NT - 24:NT - 12, :].rearrange("p (w q k) n -> p w q (k n)", w=3, q=2) \
            .bitcast(f16).rearrange("p w q (k n) -> p w q k n", k=KC)
        k0f = g.x[:, 0:8, :].rearrange("p t n -> p (t n)")[:, 0:KC * JB] \
            .rearrange("p (k n) -> p k n", k=KC)
        ctxf = k0f
        k0 = m.sb("k0", [P, 2, KC, JB], f16)
        fstage = m.sb("fstage", [P, 2, D])
        bvb = m.sb("bvb", [P, D])
        bqk = m.sb("bqk", [P, 2, KC])
        bqb = m.sb("bqb", [P, KC, P])
        ones = m.sb("ones", [P, P])
        qabs = m.sb("qabs", [P, KC])
        qinv = m.sb("qinv", [P, KC])
        rT = k0[:, :, :, :].rearrange("p q k n -> p (q k n)")[:, 0:2 * KC * D].bitcast(f32) \
            .rearrange("p (k n) -> p k n", k=KC)
        dg = bqb
        ring = [m.ps(f"ring{i}", [P, D]) for i in range(4)]
        bps = [m.ps(f"bps{i}", [P, D]) for i in range(2)]
        xp = [m.ps(f"xp{i}", [P, KC, P]) for i in range(2)]

        loaded = [m.sem(f"loaded{n}") for n in range(NW)]
        x_in, ctx_in, bias_in = g.x_in, m.sem("ctx_in"), m.sem("bias_in")
        hi_done, lo_done = m.sem("hi_done"), m.sem("lo_done")
        ctx_hi, ctx_lo = m.sem("ctx_hi"), m.sem("ctx_lo")
        bq_done, ones_done = m.sem("bq_done"), m.sem("ones_done")
        job_mm, job_f, job_hi, job_lo = (m.sem(n) for n in ("job_mm", "job_f", "job_hi", "job_lo"))
        bias_mm, bias_out = m.sem("bias_mm"), m.sem("bias_out")
        id0, id1 = m.sem("id0"), m.sem("id1")
        kbd_zero = m.sem("kbd_zero")
        r_mm, r_abs, r_s1, r_s2, r_q, r_b, r_out, r_dg, r_bc = (
            m.sem(n) for n in ("r_mm", "r_abs", "r_s1", "r_s2", "r_q", "r_b", "r_out", "r_dg", "r_bc"))

        jobs = [("k0", (mm, h)) for mm in range(KC) for h in range(2)]
        jobs += [("v0", b) for b in range(B)]
        jobs += [("m0", (mm, h)) for mm in range(KC) for h in range(2)]
        jobs += [("k1", (mm, h)) for mm in range(KC) for h in range(2)]
        jobs += [("v1", b) for b in range(B)]
        last_job = [8, 16, 24, 32, 40]
        weight_of = {"k0": 0, "v0": 1, "m0": 2, "k1": 3, "v1": 4}
        NH = JB // 2

        def shape(kind):
            return (slice(0, J), slice(0, D)) if kind[0] == "v" else (slice(0, P), slice(0, NH))

        def parts(kind, ix):
            if kind == "v0":
                return g.v0[0:J, 0, ix, :], g.v0[0:J, 1, ix, :]
            if kind == "v1":
                return g.v1[0:J, 0, ix, :], g.v1[0:J, 1, ix, :]
            to = {"k0": k0, "m0": g.m0, "k1": g.k1}[kind]
            mm, h = ix
            return tuple(to[:, q, mm, h * NH:(h + 1) * NH] for q in range(2))

        def f_of(n):
            kind, ix = jobs[n]
            if kind == "k0":
                return k0f[:, ix[0], ix[1] * NH:(ix[1] + 1) * NH]
            rows, cols = shape(kind)
            return fstage[rows, n % 2, cols]

        def w_part(n, q):
            if n < 5:
                return wk[:, n % 3, q]
            return {5: g.wq1, 6: g.wo1}[n][:, q]

        with nc.Block() as block:

            @block.sync
            def _(sp):
                sp.dma_start(ctxf[:, :, :], io["ctxT"].rearrange("(k p) n -> p k n", p=P)).then_inc(ctx_in, 16)
                sp.dma_start(bvb[:, :], io["L0_bv"].partition_broadcast(P)).then_inc(bias_in, 16)
                sp.dma_start(bqk[:, 0, :], io["L0_bq"]).then_inc(bias_in, 16)
                sp.dma_start(bqk[:, 1, :], io["L0_bk"]).then_inc(bias_in, 16)
                for n in range(NW - 1):
                    if n >= 3:
                        sp.wait_ge(hi_done, n - 2)
                        sp.wait_ge(lo_done, n - 2)
                    sp.dma_start(raw[:, n % 3], io[W[n]].rearrange("(k p) n -> p k n", p=P)).then_inc(loaded[n], 16)
                sp.wait_ge(job_mm, 24)
                sp.dma_start(rT[:, :, :], io["L0_rhsT"].rearrange("(k p) n -> p k n", p=P)).then_inc(loaded[NW - 1], 16)
                xs = io["x"].rearrange("(t p) d -> p t d", p=P)
                for t0, t1 in ((0, 8),):
                    sp.dma_start(g.x[:, t0:t1, :], xs[:, t0:t1, :]).then_inc(x_in, 16)
                sp.wait_ge(hi_done, NW - 1)
                sp.wait_ge(lo_done, NW - 1)
                for t0, t1 in ((NT - 12, NT),):
                    sp.dma_start(g.x[:, t0:t1, :], xs[:, t0:t1, :]).then_inc(x_in, 16)
                sp.wait_ge(job_mm, len(jobs))
                for t0, t1 in ((8, NT - 12),):
                    sp.dma_start(g.x[:, t0:t1, :], xs[:, t0:t1, :]).then_inc(x_in, 16)

            @block.gpsimd
            def _(pool):
                pool.memset(g.ident[:, :], 0.0).then_inc(id0, 1)
                pool.memset(ones[:, :], 1.0).then_inc(ones_done, 1)
                pool.memset(g.half[:, :], -0.5).then_inc(id1, 1)
                pool.memset(g.eps[:, :], EPS).then_inc(id1, 1)
                pool.memset(g.one[:, :], 1.0).then_inc(id1, 1)
                pool.memset(g.ws[:, :], WS).then_inc(id1, 1)
                pool.wait_ge(id0, 1)
                pool.affine_select(out=g.ident[:, :], in_=g.ident[:, :], compare_op=ALU.not_equal, fill=1.0,
                                   base=0, pattern=[[-1, P]], channel_multiplier=1).then_inc(id0, 1)
                pool.memset(g.kbd[:, :, :, :, :], 0.0).then_inc(kbd_zero, 1)
                pool.wait_ge(kbd_zero, 1)
                pool.wait_ge(job_hi, 32)
                pool.wait_ge(job_lo, 32)
                for c in range(KC):
                    block_keys(pool, g, 0, c)
                pool.wait_ge(g.keys_ok, HC * KC)

            @block.scalar
            def _(act):
                act.wait_ge(ctx_in, 16)
                act.activation(ctx_s[:, 0], ctxf[:, :, :], ACT.Copy).then_inc(ctx_hi, 1)

                def split(n):
                    act.wait_ge(loaded[n], 16)
                    if 3 <= n < 5:
                        act.wait_ge(job_mm, last_job[n - 3])
                    act.activation(w_part(n, 0), raw[:, n % 3], ACT.Copy, scale=WS).then_inc(hi_done, 1)

                split(0)
                split(1)
                for n, (kind, ix) in enumerate(jobs):
                    act.wait_ge(job_f, n + 1)
                    act.activation(parts(kind, ix)[0], f_of(n), ACT.Copy).then_inc(job_hi, 1)
                    if n % 4 == 3 and n // 4 + 2 < NW - 1:
                        split(n // 4 + 2)
                act.wait_ge(r_s2, 1)
                act.wait_ge(r_abs, 2)
                for k in range(KC):
                    act.activation(rT[:, k, :], rT[:, k, :], ACT.Identity, scale=qinv[:, k:k + 1],
                                   bias=g.round_c[:, 0:1]).then_inc(r_q, 1)

            @block.vector
            def _(dve):
                dve.memset(g.round_c[:, 0:1], ROUND).then_inc(r_abs, 1)
                dve.memset(g.round_c[:, 1:2], -ROUND).then_inc(r_abs, 1)
                dve.wait_ge(ctx_hi, 1)
                dve.tensor_tensor(ctx_s[:, 1], ctxf[:, :, :], ctx_s[:, 0], ALU.subtract).then_inc(ctx_lo, 1)

                def split(n):
                    dve.wait_ge(hi_done, n + 1)
                    dve.scalar_tensor_tensor(w_part(n, 1), raw[:, n % 3], WS, w_part(n, 0), ALU.mult,
                                             ALU.subtract).then_inc(lo_done, 1)

                split(0)
                split(1)
                dve.wait_ge(bias_in, 48)
                dve.wait_ge(ones_done, 1)
                for k in range(KC):
                    dve.tensor_scalar(bqb[:, k, :], ones[:, :], bqk[:, 0, k:k + 1], None, ALU.mult).then_inc(bq_done, 1)
                for n, (kind, ix) in enumerate(jobs):
                    rows, cols = shape(kind)
                    out, bank = f_of(n), ring[n % 4][rows, cols]
                    dve.wait_ge(job_mm, n + 1)
                    need(dve, job_hi, n - 1)
                    need(dve, job_lo, n - 1)
                    if kind == "k0":
                        dve.tensor_scalar(out, bank, 1 / WS, bqk[:, 1, ix[0]:ix[0] + 1], ALU.mult, ALU.add).then_inc(job_f, 1)
                    elif kind == "v0":
                        dve.scalar_tensor_tensor(out, bank, 1 / WS, bvb[rows, :], ALU.mult, ALU.add).then_inc(job_f, 1)
                    else:
                        dve.tensor_scalar(out, bank, 1 / WS, None, ALU.mult).then_inc(job_f, 1)
                    dve.wait_ge(job_hi, n + 1)
                    dve.wait_ge(job_f, n + 1)
                    hi, lo = parts(kind, ix)
                    dve.tensor_tensor(lo, out, hi, ALU.subtract).then_inc(job_lo, 1)
                    if n % 4 == 3 and n // 4 + 2 < NW - 1:
                        split(n // 4 + 2)
                    if n == 15:
                        for h in range(2):
                            dve.wait_ge(bias_mm, h + 1)
                            dve.tensor_scalar(g.simb[:, h * NH:(h + 1) * NH], bps[h][:, 0:NH], SC0, None,
                                              ALU.mult).then_inc(bias_out, 1)
                dve.wait_ge(loaded[NW - 1], 16)
                dve.tensor_reduce(qabs[:, :], rT[:, :, :], AX.X, ALU.max, apply_absolute_value=True).then_inc(r_s1, 1)
                dve.wait_ge(r_s1, 1)
                dve.tensor_scalar(qabs[:, :], qabs[:, :], 1e-12, 1 / 127.0, ALU.max, ALU.mult).then_inc(r_s1, 1)
                dve.wait_ge(r_s1, 2)
                dve.reciprocal(qinv[:, :], qabs[:, :]).then_inc(r_s2, 1)
                dve.wait_ge(id0, 2)
                for k in range(KC):
                    dve.tensor_scalar(dg[:, k, :], g.ident[:, :], qabs[:, k:k + 1], None, ALU.mult).then_inc(r_dg, 1)
                for c in range(KC):
                    dve.wait_ge(r_mm, c + 1)
                    dve.tensor_scalar(g.qr[:, c, :].rearrange("p (k n) -> p k n", k=KC), xp[c % 2][:, :, :], ROUND,
                                      None, ALU.subtract).then_inc(r_out, 1)
                dve.wait_ge(r_bc, 1)
                dve.tensor_copy(g.rs[:, :], bps[0][:, :]).then_inc(r_b, 1)

            @block.tensor
            def _(pe):
                pe.wait_ge(ctx_lo, 1)
                seen = -1
                for n, (kind, ix) in enumerate(jobs):
                    rows, cols = shape(kind)
                    w = weight_of[kind]
                    if w > seen:
                        pe.wait_ge(lo_done, w + 1)
                        pe.wait_ge(hi_done, w + 1)
                        seen = w
                    if n >= 4:
                        pe.wait_ge(job_f, n - 3)
                    out = ring[n % 4][rows, cols]
                    if kind[0] == "v":
                        last = matmuls(pe, out, lambda q, k: ctx_s[:, q, k, ix * J:(ix + 1) * J],
                                       lambda q, k: wk[:, w % 3, q, k, :])
                    else:
                        mm, h = ix
                        if kind == "m0" and n == 16:
                            pe.wait_ge(job_lo, 8)
                        src = k0 if kind == "m0" else ctx_s
                        last = matmuls(pe, out, lambda q, k: wk[:, w % 3, q, k, mm * P:(mm + 1) * P],
                                       lambda q, k: src[:, q, k, h * NH:(h + 1) * NH])
                    last.then_inc(job_mm, 1)
                    if n == 15:
                        pe.wait_ge(bq_done, KC)
                        pe.wait_ge(job_f, 8)
                        for h in range(2):
                            for k in range(KC):
                                last = pe.matmul(bps[h][:, 0:NH], bqb[:, k, :], k0f[:, k, h * NH:(h + 1) * NH],
                                                 start=k == 0, stop=k == KC - 1)
                            last.then_inc(bias_mm, 1)
                pe.wait_ge(id0, 2)
                pe.wait_ge(r_q, KC)
                for c in range(KC):
                    if c >= 2:
                        pe.wait_ge(r_out, c - 1)
                    for k in range(KC):
                        last = pe.transpose(xp[c % 2][:, k, :], rT[:, k, c * P:(c + 1) * P], g.ident[:, :])
                    last.then_inc(r_mm, 1)
                pe.wait_ge(r_dg, KC)
                pe.wait_ge(bias_out, 2)
                for k in range(KC):
                    last = pe.matmul(bps[0][:, k * P:(k + 1) * P], ones[:, :], dg[:, k, :], start=True, stop=True)
                last.then_inc(r_bc, 1)


def attention0(nc, g):
    with ExitStack() as ctx:
        m = Scope(nc, ctx, "attention0")
        ln = Norm(m, "a")
        xn = ln.xn
        xT = m.sb("xT", [P, 2, 2, KC, P], f16)
        sim = m.sb("sim", [P, 2, J])
        nmax = m.sb("nmax", [P, 2, 1])
        prob = m.sb("prob", [P, 2, J])
        y = m.sb("y", [P, 2, D])
        rsum = m.sb("rsum", [P, 4, 1])
        rinv = m.sb("rinv", [P, 4, 1])
        pT = m.sb("pT", [P, 2, 2, P], f16)
        ps_x = [m.ps(f"ps_x{i}", [P, KC, P]) for i in range(2)]
        ps_s = [m.ps(f"ps_s{i}", [P, D]) for i in range(2)]
        ps_p = [m.ps(f"ps_p{i}", [P, D]) for i in range(2)]
        ps_y = [m.ps(f"ps_y{i}", [P, D]) for i in range(2)]
        names = ("xt_mm", "xt_hi", "xt_lo", "sim_mm", "sim_ok",
                 "max_ok", "exp_ok", "sum_ok", "p_mm", "p_hi", "p_lo", "y_mm", "y_ok", "x_new")
        s = {n: m.sem("a0_" + n) for n in names}

        with nc.Block() as block:

            @block.gpsimd
            def _(pool):
                def step(t, d):
                    if live(t + 3):
                        ln.inverse_root(pool, g, t + 3, (d + 3) % 4)
                    u = t - 3
                    if live(u):
                        pool.wait_ge(s["y_ok"], u + 1)
                        pool.tensor_tensor(g.x[:, u, :], g.x[:, u, :], y[:, (d + 1) % 2], ALU.add).then_inc(s["x_new"], 1)
                pipeline(pool, step, 3, 3)

            @block.vector
            def _(dve):
                def step(t, d):
                    if live(t + 5) or live(t + 4):
                        ln.statistics(dve, g, t + 5, (d + 1) % 4)
                    u = t
                    if live(u):
                        c = d % 2
                        dve.wait_ge(s["sim_mm"], u + 1)
                        need(dve, s["exp_ok"], u - 1)
                        dve.scalar_tensor_tensor(sim[:, c], ps_s[c][:, 0:J], SC0, g.simb[:, bass.ds((u // TB) * J, J)],
                                                 ALU.mult, ALU.add).then_inc(s["sim_ok"], 1)
                        dve.wait_ge(s["sim_ok"], u + 1)
                        dve.tensor_reduce(nmax[:, c], sim[:, c], AX.X, ALU.max, negate=True).then_inc(s["max_ok"], 1)
                    u = t + 1
                    if live(u):
                        c = (d + 1) % 2
                        dve.wait_ge(s["xt_hi"], u + 1)
                        dve.tensor_tensor(xT[:, c, 1], ps_x[c][:, :, :], xT[:, c, 0], ALU.subtract).then_inc(s["xt_lo"], 1)
                    u = t - 1
                    if live(u):
                        c = (d + 1) % 2
                        dve.wait_ge(s["p_hi"], u + 1)
                        dve.tensor_tensor(pT[0:J, c, 1], ps_p[c][0:J, 0:P], pT[0:J, c, 0], ALU.subtract).then_inc(s["p_lo"], 1)
                        q = (d + 3) % 4
                        dve.wait_ge(s["exp_ok"], u + 1)
                        dve.reciprocal(rinv[:, q], rsum[:, q]).then_inc(s["sum_ok"], 1)
                    if live(t + 2):
                        ln.apply(dve, g, t + 2, (d + 2) % 4, s["xt_mm"])
                dve.wait_ge(g.x_in, 48)
                pipeline(dve, step, 5, 1)

            @block.scalar
            def _(act):
                def step(t, d):
                    u = t + 1
                    if live(u):
                        c = (d + 1) % 2
                        act.wait_ge(s["xt_mm"], u + 1)
                        need(act, s["sim_mm"], u - 1)
                        act.activation(xT[:, c, 0], ps_x[c][:, :, :], ACT.Copy).then_inc(s["xt_hi"], 1)
                    u = t - 1
                    if live(u):
                        c = (d + 1) % 2
                        act.wait_ge(s["p_mm"], u + 1)
                        need(act, s["y_mm"], u - 1)
                        act.activation(pT[0:J, c, 0], ps_p[c][0:J, 0:P], ACT.Copy).then_inc(s["p_hi"], 1)
                    u = t - 2
                    if live(u):
                        c, q = d % 2, (d + 2) % 4
                        act.wait_ge(s["y_mm"], u + 1)
                        act.wait_ge(s["sum_ok"], u + 1)
                        need(act, s["x_new"], u - 1)
                        act.activation(y[:, c], ps_y[c][:, :], ACT.Copy, scale=rinv[:, q]).then_inc(s["y_ok"], 1)
                    u = t
                    if live(u):
                        c = d % 2
                        act.wait_ge(s["max_ok"], u + 1)
                        need(act, s["p_mm"], u - 1)
                        need(act, s["sum_ok"], u - 3)
                        act.activation(prob[:, c], sim[:, c], ACT.Exp, bias=nmax[:, c],
                                       accum_out=rsum[:, d]).then_inc(s["exp_ok"], 1)
                pipeline(act, step, 1, 2)

            @block.tensor
            def _(pe):
                def step(t, d):
                    u = t
                    if live(u):
                        c = d % 2
                        pe.wait_ge(s["xt_lo"], u + 1)
                        need(pe, s["sim_ok"], u - 1)
                        j0 = (u // TB) * J
                        matmuls(pe, ps_s[c][:, 0:J], lambda q, k: xT[:, c, q, k, :],
                                lambda q, k: g.m0[:, q, k, bass.ds(j0, J)]).then_inc(s["sim_mm"], 1)
                    u = t - 1
                    if live(u):
                        c = (d + 1) % 2
                        pe.wait_ge(s["exp_ok"], u + 1)
                        need(pe, s["p_lo"], u - 1)
                        pe.transpose(ps_p[c][0:J, 0:P], prob[:, c], g.ident[:, :]).then_inc(s["p_mm"], 1)
                    u = t - 2
                    if live(u):
                        c = d % 2
                        pe.wait_ge(s["p_lo"], u + 1)
                        need(pe, s["y_ok"], u - 1)
                        b = u // TB
                        matmuls(pe, ps_y[c][:, :], lambda q, k: pT[0:J, c, q, :],
                                lambda q, k: g.v0[0:J, q, b, :], ks=(0,)).then_inc(s["y_mm"], 1)
                    u = t + 2
                    if live(u):
                        c = d % 2
                        pe.wait_ge(ln.ok, u + 1)
                        need(pe, s["xt_lo"], u - 1)
                        for k in range(KC):
                            last = pe.transpose(ps_x[c][:, k, :], xn[:, c, k * P:(k + 1) * P], g.ident[:, :])
                        last.then_inc(s["xt_mm"], 1)
                pipeline(pe, step, 2, 2)


class Norm:

    def __init__(self, m, name):
        self.st = m.sb(name + "_st", [P, 4, 6])
        self.mv = m.sb(name + "_mv", [P, 4, 2])
        self.ve = m.sb(name + "_ve", [P, 4, 1])
        self.rstd = m.sb(name + "_rstd", [P, 4, 1])
        self.xn = m.sb(name + "_xn", [P, 2, D])
        self.stats, self.aggr, self.var, self.root, self.ok = (
            m.sem(f"{name}_{n}") for n in ("stats", "aggr", "var", "root", "ok"))

    def before(self, dve, u, read=None):
        need(dve, self.stats, u)
        need(dve, read or self.root, u - 4)

    def statistics(self, dve, g, u, d, waits=True):
        if waits:
            self.before(dve, u)
        if live(u):
            dve.bn_stats(self.st[:, d], g.x[:, u, :]).then_inc(self.stats, 1)
        if live(u - 1):
            dve.bn_aggr(self.mv[:, (d + 3) % 4], self.st[:, (d + 3) % 4]).then_inc(self.aggr, 1)

    def inverse_root(self, pool, g, u, d):
        pool.wait_ge(self.aggr, u + 1)
        need(pool, self.ok, u - 3)
        pool.tensor_tensor(self.ve[:, d], self.mv[:, d, 1:2], g.eps[:, :], ALU.add).then_inc(self.var, 1)
        pool.wait_ge(self.var, u + 1)
        pool.tensor_tensor(self.rstd[:, d], self.ve[:, d], g.half[:, :], ALU.pow).then_inc(self.root, 1)

    def apply(self, dve, g, u, d, read, behind=1):
        dve.wait_ge(self.root, u + 1)
        need(dve, read, u - behind)
        dve.tensor_scalar(self.xn[:, d % 2], g.x[:, u, :], self.mv[:, d, 0:1], self.rstd[:, d], ALU.subtract,
                          ALU.mult).then_inc(self.ok, 1)


def quantised(nc, g):
    with ExitStack() as ctx:
        m = Scope(nc, ctx, "quantised")
        ln = Norm(m, "q")
        amax = m.sb("amax", [P, 4, 1])
        scale = m.sb("scale", [P, 4, 1])
        inv = m.sb("inv", [P, 4, 1])
        xr = m.sb("xr", [P, 2, D])
        qT = m.sb("qT", [P, 2, KC, P], bf16)
        y = m.sb("y", [P, 2, D])
        ps_x = [m.ps(f"ps_x{i}", [P, KC, P]) for i in range(2)]
        ps_y = [m.ps(f"ps_y{i}", [P, D]) for i in range(2)]
        s = {n: m.sem("q_" + n) for n in ("amax", "scale", "inv", "xr", "xt_mm", "xt_ok", "y_mm", "y_ok", "x_new")}

        with nc.Block() as block:

            @block.gpsimd
            def _(pool):
                def step(t, d):
                    u = t + 3
                    if live(u):
                        ln.inverse_root(pool, g, u, (d + 3) % 4)
                    u = t - 1
                    if live(u):
                        pool.wait_ge(s["y_ok"], u + 1)
                        pool.tensor_tensor(g.x[:, u, :], g.x[:, u, :], y[:, (d + 1) % 2], ALU.add).then_inc(s["x_new"], 1)
                pipeline(pool, step, 3, 1)

            @block.vector
            def _(dve):
                def step(t, d):
                    u, c = t + 3, (d + 3) % 4
                    if live(u):
                        ln.apply(dve, g, u, c, s["xr"])
                    if live(t + 5) or live(t + 4):
                        ln.statistics(dve, g, t + 5, (d + 1) % 4)
                    if live(u):
                        dve.wait_ge(ln.ok, u + 1)
                        dve.tensor_reduce(amax[:, c], ln.xn[:, c % 2], AX.X, ALU.max,
                                          apply_absolute_value=True).then_inc(s["amax"], 1)
                    if live(t):
                        dve.wait_ge(s["y_mm"], t + 1)
                        need(dve, s["x_new"], t - 1)
                        dve.scalar_tensor_tensor(y[:, d % 2], ps_y[d % 2][:, :], scale[:, d],
                                                 g.rs[:, :], ALU.mult, ALU.mult).then_inc(s["y_ok"], 1)
                    if live(u):
                        dve.wait_ge(s["amax"], u + 1)
                        need(dve, s["y_ok"], u - 3)
                        dve.tensor_scalar(scale[:, c], amax[:, c], 1e-12, 1 / 127.0, ALU.max, ALU.mult).then_inc(s["scale"], 1)
                        dve.wait_ge(s["scale"], u + 1)
                        need(dve, s["xr"], u - 3)
                        dve.reciprocal(inv[:, c], scale[:, c]).then_inc(s["inv"], 1)
                pipeline(dve, step, 5, 0)

            @block.scalar
            def _(act):
                def step(t, d):
                    u = t + 2
                    if live(u):
                        c = (d + 2) % 4
                        act.wait_ge(s["inv"], u + 1)
                        need(act, s["xt_mm"], u - 1)
                        act.activation(xr[:, c % 2], ln.xn[:, c % 2], ACT.Identity, scale=inv[:, c],
                                       bias=g.round_c[:, 0:1]).then_inc(s["xr"], 1)
                    u = t + 1
                    if live(u):
                        c = (d + 1) % 4
                        act.wait_ge(s["xt_mm"], u + 1)
                        need(act, s["y_mm"], u - 1)
                        act.activation(qT[:, c % 2], ps_x[c % 2][:, :, :], ACT.Identity,
                                       bias=g.round_c[:, 1:2]).then_inc(s["xt_ok"], 1)
                pipeline(act, step, 2, 0)

            @block.tensor
            def _(pe):
                def step(t, d):
                    u = t
                    if live(u):
                        pe.wait_ge(s["xt_ok"], u + 1)
                        need(pe, s["y_ok"], u - 1)
                        for k in range(KC):
                            last = pe.matmul(ps_y[d % 2][:, :], qT[:, d % 2, k, :], g.qr[:, k, :], start=k == 0, stop=k == KC - 1)
                        last.then_inc(s["y_mm"], 1)
                    u = t + 2
                    if live(u):
                        c = (d + 2) % 4
                        pe.wait_ge(s["xr"], u + 1)
                        need(pe, s["xt_ok"], u - 1)
                        for k in range(KC):
                            last = pe.transpose(ps_x[c % 2][:, k, :], xr[:, c % 2, k * P:(k + 1) * P], g.ident[:, :])
                        last.then_inc(s["xt_mm"], 1)
                pipeline(pe, step, 2, 0)


def attention1(nc, g, io):
    LEAD, LAG = 5, 9
    HEAD = 12
    with ExitStack() as ctx:
        m = Scope(nc, ctx, "attention1")
        ln = Norm(m, "b")
        xT = m.sb("xT", [P, 2, 2, KC, P], f16)
        qT = m.sb("qT", [P, 2, 2, KC, P], f16)
        nmax = m.sb("nmax", [P, 2, KC, HC])
        prob = m.sb("prob", [P, 4, HC, J])
        pT = m.sb("pT", [P, 4, 2, HC, P], f16)
        rsum = m.sb("rsum", [P, 2, HEADS])
        rinv = m.sb("rinv", [P, 2, HEADS])
        of = m.sb("of", [P, D])
        oT = m.sb("oT", [P, 2, 2, KC, P], f16)
        lg = Norm(m, "g")
        gT = m.sb("gT", [P, 2, 2, KC, P], f16)
        gwf = m.sb("gwf", [P, KC, E + 1])
        gws = m.sb("gws", [P, 2, KC, E + 1], f16)
        raw = g.qr[:, :, :].rearrange("p k n -> p (k n)").bitcast(f32)
        zero = raw[:, 0:D]
        ps_sf = [m.ps(f"ps_s{i}", [P, D]) for i in range(2)]
        ps_s = [v[:, 0:HC * J].rearrange("p (h j) -> p h j", h=HC) for v in ps_sf]
        ps_p = [m.ps(f"ps_p{i}", [P, HC, P]) for i in range(2)]
        ps_x = m.ps("ps_x", [P, KC, P])
        ps_l = ps_x[:, 0, 0:E + 1]
        ps_q = m.ps("ps_q", [P, KC, P])
        ps_o = m.ps("ps_o", [P, D])
        ps_y = m.ps("ps_y", [P, D])
        s = {n: m.sem("b_" + n) for n in ("xt_mm", "xt_hi", "xt_lo", "q_mm", "q_hi", "q_lo", "inv", "of", "o_tr", "o_hi",
                                          "o_lo", "y_mm", "x_new", "g_tr", "g_hi", "g_lo", "l_mm", "l_ok")}
        c4 = {n: m.sem("b4_" + n) for n in ("s_mm", "max", "exp", "p_mm", "p_hi", "p_lo", "o_mm")}
        w_in, w_scaled, w_hi, w_lo = (m.sem(n) for n in ("w_in", "w_scaled", "w_hi", "w_lo"))
        gw_in, gw_hi, gw_lo, zeroed, zero_out = (m.sem(n) for n in ("gw_in", "gw_hi", "gw_lo", "zeroed", "zero_out"))
        centred = m.sem("centred")
        rows_out = [m.sem(f"rows_out{n}") for n in range(2)]
        gt_out = [m.sem(f"gt_out{n}") for n in range(2)]

        def run(eng, step):
            pipeline(eng, step, LEAD, LAG, head=HEAD)

        with nc.Block() as block:

            @block.sync
            def _(sp):
                sp.dma_start(gwf[:, :, :], io["gwT"].rearrange("(k p) n -> p k n", p=P)).then_inc(gw_in, 16)
                sp.wait_ge(zeroed, 1)
                for n in range(CAP // P):
                    rows = slice(T + n * P, T + (n + 1) * P)
                    sp.dma_start(io["xn_rows"][rows, :], zero).then_inc(zero_out, 16)
                    sp.dma_start(io["out"][rows, :], zero).then_inc(zero_out, 16)
                sp.wait_ge(zero_out, 32 * (CAP // P))

                def step(t, d):
                    if live(t) and d == 0:
                        b = t // TB
                        need(sp, w_lo, b)
                        sp.dma_start(raw[:, :], io["sh_guT"][bass.ds(b * P, P), :]).then_inc(w_in, 16)
                    u = t - 7
                    if live(u):
                        sp.wait_ge(lg.ok, u + 1)
                        sp.dma_start(io["xn_rows"][bass.ds(u * P, P), :], lg.xn[:, (d + 1) % 2]).then_inc(rows_out[(d + 1) % 2], 16)
                        sp.wait_ge(s["g_lo"], u + 1)
                        sp.dma_start(io["xt_tiles"][u, :, :], gT[:, (d + 1) % 2].rearrange("p q k n -> p (q k n)")) \
                            .then_inc(gt_out[(d + 1) % 2], 16)
                run(sp, step)
                for n in range(2):
                    sp.wait_ge(rows_out[n], 8 * NT)
                    sp.wait_ge(gt_out[n], 8 * NT)

            @block.gpsimd
            def _(pool):
                pool.memset(zero, 0.0).then_inc(zeroed, 1)

                def step(t, d):
                    u = t + 3
                    if live(u):
                        ln.inverse_root(pool, g, u, (d + 3) % 4)
                    u, q = t - 6, (d + 2) % 4
                    if live(u):
                        lg.inverse_root(pool, g, u, q)
                        need(pool, rows_out[q % 2], 16 * (u // 2))
                        need(pool, s["g_tr"], u - 1)
                        pool.wait_ge(lg.root, u + 1)
                        pool.tensor_tensor(lg.xn[:, q % 2], g.x[:, u, :], lg.mv[:, q, 0:1].to_broadcast([P, D]),
                                           ALU.subtract).then_inc(centred, 1)
                        pool.wait_ge(centred, u + 1)
                        pool.tensor_tensor(lg.xn[:, q % 2], lg.xn[:, q % 2], lg.rstd[:, q].to_broadcast([P, D]),
                                           ALU.mult).then_inc(lg.ok, 1)
                    if live(t) and d == 1:
                        b = t // TB
                        pool.wait_ge(w_in, 16 * (b + 1))
                        pool.tensor_tensor(raw[:, :], raw[:, :], g.ws[:, :].to_broadcast([P, IS]), ALU.mult).then_inc(w_scaled, 1)
                        pool.wait_ge(w_scaled, b + 1)
                        pool.tensor_tensor(g.wgu[:, b, 0, :], raw[:, :], g.one[:, :].to_broadcast([P, IS]), ALU.mult).then_inc(w_hi, 1)
                        pool.wait_ge(w_hi, b + 1)
                        pool.tensor_tensor(g.wgu[:, b, 1, :], raw[:, :], g.wgu[:, b, 0, :], ALU.subtract).then_inc(w_lo, 1)
                    if live(t) and live(t + 1) and d == TB - 1:
                        b = t // TB
                        for c in range(KC):
                            pool.wait_ge(c4["s_mm"], KC * t + c + 1)
                            block_keys(pool, g, b + 1, c)
                        pool.wait_ge(g.keys_ok, HC * KC * (b + 2))
                run(pool, step)

            @block.vector
            def _(dve):
                def maximum(u, d, c):
                    dve.wait_ge(c4["s_mm"], KC * u + c + 1)
                    need(dve, c4["exp"], KC * (u - 2) + c + 1)
                    dve.tensor_reduce(nmax[:, d % 2, c], ps_s[c % 2][:, :, :], AX.X, ALU.max,
                                      negate=True).then_inc(c4["max"], 1)

                def prob_low(u, c):
                    dve.wait_ge(c4["p_hi"], KC * u + c + 1)
                    dve.tensor_tensor(pT[0:J, c, 1], ps_p[c % 2][0:J], pT[0:J, c, 0], ALU.subtract).then_inc(c4["p_lo"], 1)

                def step(t, d):
                    if live(t):
                        maximum(t, d, 0)
                    u = t - 4
                    if live(u):
                        dve.wait_ge(s["y_mm"], u + 1)
                        dve.scalar_tensor_tensor(g.x[:, u, :], ps_y[:, :], 1 / WS, g.x[:, u, :], ALU.mult,
                                                 ALU.add).then_inc(s["x_new"], 1)
                    u, q = t - 1, (d + 1) % 2
                    if live(u):
                        prob_low(u, 0)
                        dve.wait_ge(c4["exp"], KC * u + KC)
                        need(dve, s["of"], u - 1)
                        dve.reciprocal(rinv[:, q, :], rsum[:, q, :]).then_inc(s["inv"], 1)
                    u, q = t - 2, d % 2
                    if live(u):
                        dve.wait_ge(c4["o_mm"], KC * u + KC)
                        dve.wait_ge(s["inv"], u + 1)
                        need(dve, s["o_tr"], u)
                        dve.tensor_tensor(of[:, :].rearrange("p (h o) -> p h o", h=HEADS),
                                          ps_o[:, :].rearrange("p (h o) -> p h o", h=HEADS),
                                          rinv[:, q, :].rearrange("p (h o) -> p h o", o=1).to_broadcast([P, HEADS, DH]),
                                          ALU.mult).then_inc(s["of"], 1)
                    u, q = t + 1, (d + 1) % 2
                    if live(u):
                        dve.wait_ge(s["xt_hi"], u + 1)
                        dve.tensor_tensor(xT[:, q, 1], ps_x[:, :, :], xT[:, q, 0], ALU.subtract).then_inc(s["xt_lo"], 1)
                    if live(t):
                        maximum(t, d, 1)
                    if live(t - 4):
                        dve.wait_ge(s["x_new"], t - 3)
                    if live(t - 4) or live(t - 5):
                        lg.before(dve, t - 4, lg.ok)
                    if live(t - 1):
                        prob_low(t - 1, 1)
                    u = t - 8
                    if live(u):
                        dve.wait_ge(s["l_mm"], u + 1)
                        dve.tensor_scalar(g.logits[:, u, :], ps_l, 1 / WS, None, ALU.mult).then_inc(s["l_ok"], 1)
                    if live(t - 4) or live(t - 5):
                        lg.statistics(dve, g, t - 4, d, waits=False)
                    if live(t + 2):
                        ln.apply(dve, g, t + 2, (d + 2) % 4, s["xt_mm"])
                    if live(t):
                        maximum(t, d, 2)
                    if live(t - 1):
                        prob_low(t - 1, 2)
                    if live(t + 5) or live(t + 4):
                        ln.before(dve, t + 5)
                    u, q = t - 2, d % 2
                    if live(u):
                        dve.wait_ge(s["o_hi"], u + 1)
                        dve.tensor_tensor(oT[:, q, 1], ps_x[:, :, :], oT[:, q, 0], ALU.subtract).then_inc(s["o_lo"], 1)
                    if live(t + 5) or live(t + 4):
                        ln.statistics(dve, g, t + 5, (d + 1) % 4, waits=False)
                    if live(t):
                        maximum(t, d, 3)
                    u, q = t + 1, (d + 1) % 2
                    if live(u):
                        dve.wait_ge(s["q_hi"], u + 1)
                        dve.scalar_tensor_tensor(qT[:, q, 1], ps_q[:, :, :], SC1 / WS, qT[:, q, 0], ALU.mult,
                                                 ALU.subtract).then_inc(s["q_lo"], 1)
                    u, q = t - 7, (d + 1) % 2
                    if live(u):
                        dve.wait_ge(s["g_hi"], u + 1)
                        dve.tensor_tensor(gT[:, q, 1], ps_x[:, :, :], gT[:, q, 0], ALU.subtract).then_inc(s["g_lo"], 1)
                    if live(t - 1):
                        prob_low(t - 1, 3)
                dve.wait_ge(gw_hi, 1)
                dve.scalar_tensor_tensor(gws[:, 1], gwf[:, :, :], WS, gws[:, 0], ALU.mult, ALU.subtract).then_inc(gw_lo, 1)
                run(dve, step)

            @block.scalar
            def _(act):
                def prob_high(u, c):
                    act.wait_ge(c4["p_mm"], KC * u + c + 1)
                    need(act, c4["o_mm"], KC * (u - 1) + c + 1)
                    act.activation(pT[0:J, c, 0], ps_p[c % 2][0:J], ACT.Copy).then_inc(c4["p_hi"], 1)

                def exps(u, d, c):
                    act.wait_ge(c4["max"], KC * u + c + 1)
                    need(act, s["inv"], u - 1)
                    need(act, c4["p_mm"], KC * (u - 1) + c + 1)
                    for h in range(HC):
                        n = c * HC + h
                        last = act.activation(prob[:, c, h, :], ps_s[c % 2][:, h, :], ACT.Exp, bias=nmax[:, d % 2, c, h:h + 1],
                                              accum_out=rsum[:, d % 2, n:n + 1])
                    last.then_inc(c4["exp"], 1)

                def step(t, d):
                    for c in range(KC):
                        u, q = t + 1, (d + 1) % 2
                        if c == 3 and live(u):
                            act.wait_ge(s["q_mm"], u + 1)
                            need(act, c4["s_mm"], KC * (u - 1))
                            act.activation(qT[:, q, 0], ps_q[:, :, :], ACT.Copy, scale=SC1 / WS).then_inc(s["q_hi"], 1)
                        u, q = t - 7, (d + 1) % 2
                        if c == 3 and live(u):
                            act.wait_ge(s["g_tr"], u + 1)
                            need(act, s["l_mm"], u - 1)
                            need(act, gt_out[q], 16 * (u // 2))
                            act.activation(gT[:, q, 0], ps_x[:, :, :], ACT.Copy).then_inc(s["g_hi"], 1)
                        if live(t - 1):
                            prob_high(t - 1, c)
                        u, q = t - 2, d % 2
                        if c == 2 and live(u):
                            act.wait_ge(s["o_tr"], u + 1)
                            need(act, s["y_mm"], u - 1)
                            act.activation(oT[:, q, 0], ps_x[:, :, :], ACT.Copy).then_inc(s["o_hi"], 1)
                        if live(t):
                            exps(t, d, c)
                        u, q = t + 1, (d + 1) % 2
                        if c == 0 and live(u):
                            act.wait_ge(s["xt_mm"], u + 1)
                            need(act, s["q_mm"], u - 1)
                            act.activation(xT[:, q, 0], ps_x[:, :, :], ACT.Copy).then_inc(s["xt_hi"], 1)
                act.wait_ge(gw_in, 16)
                act.activation(gws[:, 0], gwf[:, :, :], ACT.Copy, scale=WS).then_inc(gw_hi, 1)
                run(act, step)

            @block.tensor
            def _(pe):
                def scores(u, d, c):
                    if c == 0:
                        pe.wait_ge(s["q_lo"], u + 1)
                    if d == 0:
                        pe.wait_ge(g.keys_ok, KC * HC * (u // TB) + HC * c + HC)
                    need(pe, c4["exp"], KC * u + c - 1)
                    matmuls(pe, ps_s[c % 2][:, :, :], lambda a, _: qT[:, d % 2, a, c, :], lambda a, _: g.kbd[:, a, c, :, :],
                            ks=(0,)).then_inc(c4["s_mm"], 1)

                def prob_transposed(u, c):
                    pe.wait_ge(c4["exp"], KC * u + c + 1)
                    need(pe, c4["p_lo"], KC * u + c - 1)
                    for h in range(HC):
                        last = pe.transpose(ps_p[c % 2][0:J, h, :], prob[:, c, h, :], g.ident[:, :])
                    last.then_inc(c4["p_mm"], 1)

                def outputs(u, c):
                    if c == 0:
                        need(pe, s["of"], u)
                    pe.wait_ge(c4["p_lo"], KC * u + c + 1)
                    for h in range(HC):
                        cols = slice((c * HC + h) * DH, (c * HC + h + 1) * DH)
                        for n, (a, b) in enumerate(((0, 0), (0, 1), (1, 0))):
                            last = pe.matmul(ps_o[:, cols], pT[0:J, c, a, h, :], g.v1[0:J, b, u // TB, cols],
                                             start=n == 0, stop=n == 2)
                    last.then_inc(c4["o_mm"], 1)

                def transposed(to, src):
                    for k in range(KC):
                        last = pe.transpose(to[:, k, :], src[:, k * P:(k + 1) * P], g.ident[:, :])
                    return last

                def queries(u, d, mms):
                    for mm in mms:
                        last = matmuls(pe, ps_q[:, mm, :], lambda a, k: g.wq1[:, a, k, mm * P:(mm + 1) * P],
                                       lambda a, k: xT[:, d % 2, a, k, :])
                    return last

                def product(u, d, ks):
                    for k in ks:
                        for n, (a, b) in enumerate(PASSES):
                            last = pe.matmul(ps_y[:, :], oT[:, d % 2, a, k, :], g.wo1[:, b, k, :],
                                             start=k == 0 and n == 0, stop=k == KC - 1 and n == 2)
                    return last

                def step(t, d):
                    if live(t):
                        scores(t, d, 0)
                    if live(t - 1):
                        prob_transposed(t - 1, 0)
                    if live(t - 2):
                        outputs(t - 2, 3)
                    u = t + 1
                    if live(u):
                        pe.wait_ge(ln.ok, u + 1)
                        need(pe, s["xt_lo"], u)
                        need(pe, s["o_lo"], t - 2)
                        need(pe, s["g_lo"], t - 7)
                        transposed(ps_x, ln.xn[:, (d + 1) % 2]).then_inc(s["xt_mm"], 1)
                    u = t - 3
                    if live(u):
                        pe.wait_ge(s["o_lo"], u + 1)
                        need(pe, s["x_new"], u)
                        product(u, d + 1, (0, 1))
                    if live(t):
                        scores(t, d, 1)
                    if live(t - 1):
                        prob_transposed(t - 1, 1)
                    u = t - 8
                    if live(u):
                        pe.wait_ge(s["g_lo"], u + 1)
                        pe.wait_ge(s["xt_lo"], min(t + 2, NT) if isinstance(t, int) else t + 2)
                        matmuls(pe, ps_l, lambda a, k: gT[:, d % 2, a, k, :], lambda a, k: gws[:, a, k, :]).then_inc(s["l_mm"], 1)
                    u = t + 1
                    if live(u):
                        pe.wait_ge(s["xt_lo"], u + 1)
                        need(pe, s["q_lo"], u)
                        queries(u, d + 1, (0, 1))
                    if live(t - 1):
                        outputs(t - 1, 0)
                    if live(t):
                        scores(t, d, 2)
                    if live(t - 1):
                        prob_transposed(t - 1, 2)
                        outputs(t - 1, 1)
                    u = t - 2
                    if live(u):
                        pe.wait_ge(s["of"], u + 1)
                        need(pe, s["xt_lo"], min(t + 2, NT) if isinstance(t, int) else t + 2)
                        need(pe, s["l_ok"], t - 7)
                        transposed(ps_x, of).then_inc(s["o_tr"], 1)
                    u = t + 1
                    if live(u):
                        queries(u, d + 1, (2, 3)).then_inc(s["q_mm"], 1)
                    u = t - 7
                    if live(u):
                        pe.wait_ge(lg.ok, u + 1)
                        pe.wait_ge(s["o_lo"], min(t - 1, NT) if isinstance(t, int) else t - 1)
                        need(pe, s["l_ok"], t - 7)
                        transposed(ps_x, lg.xn[:, (d + 1) % 2]).then_inc(s["g_tr"], 1)
                    if live(t):
                        scores(t, d, 3)
                    if live(t - 1):
                        prob_transposed(t - 1, 3)
                        outputs(t - 1, 2)
                    u = t - 3
                    if live(u):
                        product(u, d + 1, (2, 3)).then_inc(s["y_mm"], 1)
                pe.wait_ge(gw_lo, 1)
                run(pe, step)


TOPK = 4
TOP_P = 0.75
JITTER2 = 0.2
BIG = 1e30
OFF = float(1 << 20)


class Route:

    def __init__(self, m, g):
        A = lambda name: m.sb(name, [P, NT, E])
        V = lambda name: m.sb(name, [P, NT, 1])
        sm, alive, absl, rev, eq, pr, diff, fac, ex, keep = (
            A(n) for n in ("sm", "alive", "absl", "rev", "eq", "pr", "diff", "fac", "ex", "keep"))
        oh = [A(f"oh{k}") for k in range(TOPK)]
        rw, sel, cum0, cum1, pos, kept, wgt, slot = (A(n) for n in ("rw", "sel", "cum0", "cum1", "pos", "kept", "wgt", "slot"))
        thr = [V(f"thr{k}") for k in range(TOPK)]
        mult = [V(f"mult{k}") for k in range(TOPK)]
        mx, athr, z, z8, csum, pk, valid, rsum, sd, kk, sk = (
            V(n) for n in ("mx", "athr", "z", "z8", "csum", "pk", "valid", "rsum", "sd", "kk", "sk"))
        full = m.sb("full", [P, NT, E + 1])
        selb = m.sb("selb", [P, NT, E], bf16)
        tri = m.sb("tri", [P, P], bf16)
        one = m.sb("one", [P, P], bf16)
        erow = m.sb("erow", [P, NT, E], mybir.dt.int32)
        token = m.sb("token", [P, NT, 1], mybir.dt.int32)
        blank = m.sb("blank", [P, E * CAP // P, 2], mybir.dt.int32)
        load = m.sb("load", [P, NT, TOPK, 2], u32)
        index = m.sb("index", [P, NT, TOPK], u32)
        counts = m.sb("counts", [P, 2, NT, E])
        done = m.sem("done")
        consts, exp_in, exp_out, sel_ok, count_mm, counted, lists, blank_out, listed = (
            m.sem(n) for n in ("consts", "exp_in", "exp_out", "sel_ok", "count_mm", "counted", "lists", "blank_out", "listed"))
        wide = lambda v: v[:, :, 0:1].to_broadcast([P, NT, E])

        def constants(pool, io):
            pool.iota(erow[:, :, :], pattern=[[0, NT], [1, E]], base=0, channel_multiplier=0).then_inc(consts, 1)
            pool.iota(token[:, :, :], pattern=[[P, NT], [0, 1]], base=0, channel_multiplier=1).then_inc(consts, 1)
            pool.iota(blank[:, :, 0:1].rearrange("p (e n) c -> p e n c", e=E),
                      pattern=[[0, E], [P, CAP // P], [0, 1]], base=T, channel_multiplier=1).then_inc(consts, 1)
            pool.memset(blank[:, :, 1:2], 0).then_inc(consts, 1)
            pool.memset(one[:, :], 1.0).then_inc(consts, 1)
            pool.wait_ge(consts, 5)
            pool.affine_select(out=tri[:, :], in_=one[:, :], compare_op=ALU.is_ge, fill=0.0, base=0,
                               pattern=[[1, P]], channel_multiplier=-1).then_inc(consts, 1)
            pool.wait_ge(consts, 6)
            pool.dma_start(io["lists"].rearrange("(n p) c -> p n c", p=P), blank[:, :, :].bitcast(u32)).then_inc(blank_out, 16)
            pool.wait_ge(blank_out, 16)

        def scatter(pool, io):
            pool.wait_ge(lists, 1)
            for t in range(NT):
                for k in range(TOPK):
                    pool.indirect_dma_start(
                        out=io["lists"], out_offset=bass.IndirectOffsetOnAxis(ap=index[:, t, k:k + 1], axis=0),
                        in_=load[:, t, k, :], in_offset=None, bounds_check=E * CAP - 1, oob_is_err=False) \
                        .then_inc(listed, 16)
            pool.wait_ge(listed, 16 * NT * TOPK)

        def exponentials(act, piece):
            if piece < TOPK:
                act.wait_ge(exp_in, piece + 1)
                act.activation(ex[:, :, :], diff[:, :, :], ACT.Exp, scale=-1.0).then_inc(exp_out, 1)
            if piece == TOPK:
                for k in range(1, TOPK):
                    act.wait_ge(exp_in, TOPK + k)
                    act.activation(pk[:, :, :], sk[:, :, :], ACT.Exp).then_inc(exp_out, 1)
            if piece == TOPK + 2:
                act.wait_ge(exp_in, 2 * TOPK)
                act.activation(full[:, :, :], full[:, :, :], ACT.Exp).then_inc(exp_out, 1)

        def count(pe, bank):
            pe.wait_ge(consts, 6)
            pe.wait_ge(sel_ok, 1)
            pe.matmul(bank[:, 0], tri[:, :], selb[:, :, :], start=True, stop=True)
            pe.matmul(bank[:, 1], one[:, :], selb[:, :, :], start=True, stop=True).then_inc(count_mm, 1)

        def counted_wait(pe):
            pe.wait_ge(counted, 1)

        def pieces(dve, bank):
            chained = [0]

            def link(ins):
                chained[0] += 1
                ins.then_inc(done, 1)
                dve.wait_ge(done, chained[0])

            lg = g.logits[:, :, 0:E]
            tt, ts, stt = dve.tensor_tensor, dve.tensor_scalar, dve.scalar_tensor_tensor
            reduce = dve.tensor_reduce
            dve.wait_ge(consts, 6)
            link(dve.memset(alive[:, :, :], 1.0))
            link(dve.tensor_copy(sm[:, :, :], lg))
            link(stt(absl[:, :, :], lg, -1.0, lg, ALU.mult, ALU.max))
            link(ts(rev[:, :, :], erow[:, :, :], -1.0, float(E), ALU.mult, ALU.add))
            for k in range(TOPK):
                link(reduce(thr[k][:, :, :], sm[:, :, :], AX.X, ALU.max))
                link(tt(eq[:, :, :], sm[:, :, :], wide(thr[k]), ALU.is_equal))
                link(tt(pr[:, :, :], eq[:, :, :], rev[:, :, :], ALU.mult))
                link(reduce(mx[:, :, :], pr[:, :, :], AX.X, ALU.max))
                link(tt(oh[k][:, :, :], pr[:, :, :], wide(mx), ALU.is_equal))
                link(tt(fac[:, :, :], wide(thr[k]), lg, ALU.subtract))
                link(stt(athr[:, :, :], thr[k][:, :, :], -1.0, thr[k][:, :, :], ALU.mult, ALU.max))
                link(tt(keep[:, :, :], absl[:, :, :], wide(athr), ALU.max))
                link(stt(keep[:, :, :], keep[:, :, :], JITTER2, fac[:, :, :], ALU.mult, ALU.is_ge))
                link(tt(keep[:, :, :], keep[:, :, :], alive[:, :, :], ALU.mult))
                ts(diff[:, :, :], fac[:, :, :], 0.0, None, ALU.max).then_inc(exp_in, 1)
                dve.wait_ge(exp_out, k + 1)
                if k == 0:
                    link(reduce(z8[:, :, :], ex[:, :, :], AX.X, ALU.add))
                link(tt(keep[:, :, :], keep[:, :, :], ex[:, :, :], ALU.mult))
                link(reduce(z[:, :, :], keep[:, :, :], AX.X, ALU.add))
                link(dve.reciprocal(mult[k][:, :, :], z[:, :, :]))
                link(tt(alive[:, :, :], alive[:, :, :], oh[k][:, :, :], ALU.subtract))
                link(stt(sm[:, :, :], oh[k][:, :, :], -BIG, sm[:, :, :], ALU.mult, ALU.add))
                yield
            link(dve.reciprocal(z8[:, :, :], z8[:, :, :]))
            link(dve.tensor_copy(csum[:, :, :], z8[:, :, :]))
            link(tt(rw[:, :, :], oh[0][:, :, :], wide(mult[0]), ALU.mult))
            link(dve.tensor_copy(rsum[:, :, :], mult[0][:, :, :]))
            link(dve.tensor_copy(sel[:, :, :], oh[0][:, :, :]))
            for k in range(1, TOPK):
                tt(sk[:, :, :], thr[k][:, :, :], thr[0][:, :, :], ALU.subtract).then_inc(exp_in, 1)
                link(ts(valid[:, :, :], csum[:, :, :], TOP_P, None, ALU.is_lt))
                dve.wait_ge(exp_out, TOPK + k)
                link(tt(pk[:, :, :], pk[:, :, :], z8[:, :, :], ALU.mult))
                link(tt(csum[:, :, :], csum[:, :, :], pk[:, :, :], ALU.add))
                link(tt(mult[k][:, :, :], mult[k][:, :, :], valid[:, :, :], ALU.mult))
                link(tt(rsum[:, :, :], rsum[:, :, :], mult[k][:, :, :], ALU.add))
                link(tt(eq[:, :, :], oh[k][:, :, :], wide(mult[k]), ALU.mult))
                link(tt(rw[:, :, :], rw[:, :, :], eq[:, :, :], ALU.add))
                link(tt(eq[:, :, :], oh[k][:, :, :], wide(valid), ALU.mult))
                link(tt(sel[:, :, :], sel[:, :, :], eq[:, :, :], ALU.add))
            dve.tensor_copy(selb[:, :, :], sel[:, :, :]).then_inc(sel_ok, 1)
            link(dve.reciprocal(rsum[:, :, :], rsum[:, :, :]))
            link(tt(rw[:, :, :], rw[:, :, :], wide(rsum), ALU.mult))
            yield
            dve.wait_ge(count_mm, 1)
            dve.tensor_copy(counts[:, :, :, :], bank).then_inc(counted, 1)
            dve.wait_ge(counted, 1)
            link(dve.tensor_copy(cum0[:, :, :], counts[:, 1, :, :]))
            a, b, n = cum0, cum1, 1
            while n < NT:
                link(dve.tensor_copy(b[:, 0:n, :], a[:, 0:n, :]))
                link(tt(b[:, n:NT, :], a[:, n:NT, :], a[:, 0:NT - n, :], ALU.add))
                a, b, n = b, a, 2 * n
            link(tt(pos[:, :, :], a[:, :, :], counts[:, 1, :, :], ALU.subtract))
            link(tt(pos[:, :, :], pos[:, :, :], counts[:, 0, :, :], ALU.add))
            link(stt(kept[:, :, :], pos[:, :, :], float(CAP), sel[:, :, :], ALU.is_le, ALU.mult))
            yield
            link(ts(eq[:, :, :], kept[:, :, :], BIG, -BIG, ALU.mult, ALU.add))
            link(tt(full[:, :, 0:E], lg, eq[:, :, :], ALU.add))
            link(dve.tensor_copy(full[:, :, E:E + 1], g.logits[:, :, E:E + 1]))
            link(reduce(mx[:, :, :], full[:, :, :], AX.X, ALU.max))
            tt(full[:, :, :], full[:, :, :], mx[:, :, 0:1].to_broadcast([P, NT, E + 1]), ALU.subtract).then_inc(exp_in, 1)
            dve.wait_ge(exp_out, 2 * TOPK)
            link(reduce(z[:, :, :], full[:, :, :], AX.X, ALU.add))
            link(reduce(sd[:, :, :], full[:, :, 0:E], AX.X, ALU.add))
            link(dve.reciprocal(z[:, :, :], z[:, :, :]))
            link(ts(z[:, :, :], z[:, :, :], 1 / (WS * HS), None, ALU.mult))
            link(tt(g.gsh[:, :, :], full[:, :, E:E + 1], z[:, :, :], ALU.mult))
            link(tt(sd[:, :, :], sd[:, :, :], z[:, :, :], ALU.mult))
            link(tt(wgt[:, :, :], rw[:, :, :], wide(sd), ALU.mult))
            link(tt(wgt[:, :, :], wgt[:, :, :], kept[:, :, :], ALU.mult))
            yield
            link(stt(slot[:, :, :], erow[:, :, :], float(CAP), pos[:, :, :], ALU.mult, ALU.add))
            link(ts(slot[:, :, :], slot[:, :, :], -1.0 - OFF, None, ALU.add))
            link(tt(slot[:, :, :], slot[:, :, :], kept[:, :, :], ALU.mult))
            for k in range(TOPK):
                link(tt(eq[:, :, :], oh[k][:, :, :], slot[:, :, :], ALU.mult))
                link(reduce(sk[:, :, :], eq[:, :, :], AX.X, ALU.add))
                link(ts(index[:, :, k:k + 1], sk[:, :, :], OFF, None, ALU.add))
                link(tt(eq[:, :, :], oh[k][:, :, :], wgt[:, :, :], ALU.mult))
                link(reduce(load[:, :, k, 1:2].bitcast(f32), eq[:, :, :], AX.X, ALU.add))
                link(dve.tensor_copy(load[:, :, k, 0:1], token[:, :, :]))
            dve.tensor_copy(sk[:, :, :], sk[:, :, :]).then_inc(lists, 1)
            yield

        self.constants, self.scatter, self.exponentials = constants, scatter, exponentials
        self.count, self.counted_wait, self.pieces = count, counted_wait, pieces


def expert_weights(sp, g, io, e, c):
    to, done = g.ex_raw[:, c], g.ex_w_in[c]
    sp.dma_start(to[:, 0:KC * IE].rearrange("p (k n) -> p k n", k=KC),
                 io["dyn_gT"][e, :, :].rearrange("(k p) n -> p k n", p=P)).then_inc(done, 16)
    sp.dma_start(to[:, KC * IE:2 * KC * IE].rearrange("p (k n) -> p k n", k=KC),
                 io["dyn_uT"][e, :, :].rearrange("(k p) n -> p k n", p=P)).then_inc(done, 16)
    sp.dma_start(to[:, 2 * KC * IE:WN].rearrange("p (k n) -> p k n", k=IE // P),
                 io["dyn_dT"][e, :, :].rearrange("(k p) n -> p k n", p=P)).then_inc(done, 16)


def gather_rows(pool, g, io, e):
    for n in range(CT):
        pool.indirect_dma_start(
            out=g.ex_rows[:, e % 2, n, :], out_offset=None, in_=io["xn_rows"],
            in_offset=bass.IndirectOffsetOnAxis(ap=g.ex_slots[:, e * CT + n, 0:1], axis=0)).then_inc(g.ex_x_in[e % 2], 16)


def shared(nc, g, io):
    NC = IS // P
    with ExitStack() as ctx:
        m = Scope(nc, ctx, "shared")
        xT = m.sb("xT", [P, 2, 2, KC, S], f16)
        sg = m.sb("sg", [P, 2, S])
        hf = m.sb("hf", [P, 2, S])
        hid = m.sb("hid", [P, 2, 2, S], f16)
        res = m.sb("res", [P, TB, D])
        gsh = m.sb("gsh", [P, NT, 1])
        wd = m.sb("wd", [P, 2, NC, D], f16)
        wd_raw = m.sb("wd_raw", [P, NC, D])
        g.gsh = gsh
        ps_g = [m.ps(f"ps_g{i}", [P, S]) for i in range(2)]
        ps_u = [m.ps(f"ps_u{i}", [P, S]) for i in range(2)]
        ps_y = [m.ps(f"ps_y{i}", [P, D]) for i in range(TB)]
        s = {n: m.sem(n) for n in ("g_mm", "u_mm", "silu", "hf", "h_hi", "h_lo", "d_mm", "y_ok", "warm", "wd_hi", "wd_lo")}
        wd_in = [m.sem(f"wd_in{n}") for n in range(2)]
        x_in = [m.sem(f"x_in{n}") for n in range(2)]
        out_done, slots_in = m.sem("out_done"), m.sem("slots_in")
        routing = Route(m, g)
        bank = ps_u[0][:, :].rearrange("p (a t e) -> p a t e", a=2, e=E)
        BORROW = 6

        def ok(b):
            return not isinstance(b, int) or 0 <= b < B

        with nc.Block() as block:

            @block.sync
            def _(sp):
                def step(b, d):
                    if ok(b + 1):
                        c = (d + 1) % 2
                        need(sp, s["u_mm"], NC * b)
                        for i in range(TB):
                            src = io["xt_tiles"][(b + 1) * TB + i, :, :].rearrange("p (a n) -> p a n", n=P)
                            sp.dma_start(xT[:, c, :, :, i * P:(i + 1) * P].rearrange("p q k n -> p (q k) n"), src) \
                                .then_inc(x_in[c], 16)
                    if isinstance(b, int) and b == -1:
                        down_rows = io["sh_dT"].rearrange("(c p) n -> p c n", p=P)
                        for n in range(2):
                            cs = slice(n * NC // 2, (n + 1) * NC // 2)
                            sp.dma_start(wd_raw[:, cs], down_rows[:, cs]).then_inc(wd_in[n], 16)
                    if ok(b - 1):
                        for i in range(TB):
                            sp.wait_ge(s["y_ok"], TB * (b - 1) + i + 1)
                            sp.dma_start(io["out"][bass.ds(((b - 1) * TB + i) * P, P), :], res[:, i]).then_inc(out_done, 16)
                    if isinstance(b, int) and b == B - 2:
                        for e in range(2):
                            expert_weights(sp, g, io, e, e)
                pipeline(sp, step, 1, 1, B, 2)
                sp.wait_ge(out_done, 16 * NT)

            @block.gpsimd
            def _(pool):
                routing.constants(pool, io)
                routing.scatter(pool, io)
                pool.dma_start(g.ex_slots[:, :, :], io["lists"].rearrange("(n p) c -> p n c", p=P)).then_inc(slots_in, 16)
                pool.wait_ge(slots_in, 16)
                pool.wait_ge(s["y_ok"], NT - 2 * TB)
                for e in range(2):
                    gather_rows(pool, g, io, e)

            @block.scalar
            def _(act):
                act.activation(sg[:, 0, 0:1], g.half[:, 0:1], ACT.Silu).then_inc(s["warm"], 1)
                act.wait_ge(s["warm"], 1)

                def step(b, d):
                    for c in range(NC):
                        v = NC * b + c
                        act.wait_ge(s["g_mm"], v + 1)
                        need(act, s["hf"], v - 1)
                        act.activation(sg[:, c % 2], ps_g[c % 2][:, :], ACT.Silu, scale=1 / WS).then_inc(s["silu"], 1)
                        act.wait_ge(s["hf"], v + 1)
                        need(act, s["d_mm"], v - 1)
                        act.activation(hid[:, c % 2, 0], hf[:, c % 2], ACT.Copy).then_inc(s["h_hi"], 1)
                        if isinstance(b, int) and b == 0:
                            act.wait_ge(wd_in[2 * c // NC], 16)
                            act.activation(wd[:, 0, c], wd_raw[:, c], ACT.Copy, scale=WS).then_inc(s["wd_hi"], 1)
                            routing.exponentials(act, c)
                pipeline(act, step, 0, 0, B, 2)

            @block.vector
            def _(dve):
                pieces = routing.pieces(dve, bank)

                def step(b, d):
                    for c in range(NC):
                        if ok(b):
                            v = NC * b + c
                            dve.wait_ge(s["silu"], v + 1)
                            dve.wait_ge(s["u_mm"], v + 1)
                            need(dve, s["h_hi"], v - 1)
                            need(dve, s["h_lo"], v - 1)
                            dve.scalar_tensor_tensor(hf[:, c % 2], ps_u[c % 2][:, :], HS / WS, sg[:, c % 2], ALU.mult,
                                                     ALU.mult).then_inc(s["hf"], 1)
                            dve.wait_ge(s["h_hi"], v + 1)
                            dve.tensor_tensor(hid[:, c % 2, 1], hf[:, c % 2], hid[:, c % 2, 0], ALU.subtract).then_inc(s["h_lo"], 1)
                            if isinstance(b, int) and b == 0:
                                dve.wait_ge(s["wd_hi"], c + 1)
                                dve.scalar_tensor_tensor(wd[:, 1, c], wd_raw[:, c], WS, wd[:, 0, c], ALU.mult,
                                                         ALU.subtract).then_inc(s["wd_lo"], 1)
                                next(pieces)
                        if c == 0 and ok(b - 1):
                            t0 = (b - 1) * TB
                            dve.wait_ge(s["d_mm"], NC * b)
                            need(dve, out_done, 16 * t0)
                            for i in range(TB):
                                dve.scalar_tensor_tensor(res[:, i], ps_y[i][:, :], g.gsh[:, t0 + i, :], g.x[:, t0 + i, :],
                                                         ALU.mult, ALU.add).then_inc(s["y_ok"], 1)
                pipeline(dve, step, 0, 1, B, 2)

            @block.tensor
            def _(pe):
                def down(v, c):
                    pe.wait_ge(s["h_lo"], v + 1)
                    if isinstance(v, int) and v < NC:
                        pe.wait_ge(s["wd_lo"], c + 1)
                    for n, (a, b) in enumerate(PASSES):
                        for i in range(TB):
                            last = pe.matmul(ps_y[i][:, :], hid[:, c % 2, a, i * P:(i + 1) * P], wd[:, b, c, :],
                                             start=c == 0 and n == 0, stop=c == NC - 1 and n == 2)
                    last.then_inc(s["d_mm"], 1)

                def step(b, d):
                    for c in range(NC):
                        v = NC * b + c
                        if ok(b):
                            if c == 0:
                                pe.wait_ge(x_in[d % 2], 16 * TB * (b // 2 + 1))
                            if isinstance(b, int) and b == 0 and c == BORROW:
                                pe.wait_ge(s["hf"], v - 1)
                                routing.count(pe, bank)
                            need(pe, s["silu"], v - 1)
                            matmuls(pe, ps_g[c % 2][:, :], lambda a, k: g.wgu[:, k, a, c * P:(c + 1) * P],
                                    lambda a, k: xT[:, d % 2, a, k, :]).then_inc(s["g_mm"], 1)
                            if isinstance(b, int) and b == 0 and c == BORROW:
                                routing.counted_wait(pe)
                            need(pe, s["hf"], v - 1)
                            matmuls(pe, ps_u[c % 2][:, :], lambda a, k: g.wgu[:, KC + k, a, c * P:(c + 1) * P],
                                    lambda a, k: xT[:, d % 2, a, k, :]).then_inc(s["u_mm"], 1)
                        if c == 0 and ok(b - 1):
                            down(v - 1, NC - 1)
                        if c > 0 and ok(b):
                            if c == 1:
                                need(pe, s["y_ok"], TB * b)
                            down(v - 1, c - 1)
                pipeline(pe, step, 0, 1, B, 2)


def experts(nc, g, io):
    HN = CAP // 2
    NI = IE // P
    with ExitStack() as ctx:
        m = Scope(nc, ctx, "experts")
        raw, xg, res, lst = g.ex_raw, g.ex_rows, g.ex_res, g.ex_slots
        w = m.sb("w", [P, 2, 2, WN], f16)
        xT = m.sb("xT", [P, 2, 2, KC, CAP], f16)
        sg = m.sb("sg", [P, 2, HN])
        hf = m.sb("hf", [P, 2, HN])
        hid = m.sb("hid", [P, 2, 2, NI, CAP], f16)
        ps_x = [m.ps(f"ps_x{i}", [P, KC, P]) for i in range(2)]
        ps_g = [m.ps(f"ps_g{i}", [P, HN]) for i in range(2)]
        ps_u = [m.ps(f"ps_u{i}", [P, HN]) for i in range(2)]
        ps_y = [m.ps(f"ps_y{i}", [P, D]) for i in range(2)]
        s = {n: m.sem(n) for n in ("w_hi", "w_lo", "xt_mm", "xt_hi", "xt_lo", "g_mm", "u_mm", "silu", "hf", "h_hi", "h_lo",
                                   "y_mm", "y_ok", "warm", "added")}
        w_in, x_in = g.ex_w_in, g.ex_x_in
        PARTS = [slice(n * WN // 3, (n + 1) * WN // 3) for n in range(3)]
        UNITS = [(h, i) for h in range(2) for i in range(NI)]

        def ok(e):
            return not isinstance(e, int) or 0 <= e < E

        with nc.Block() as block:

            @block.sync
            def _(sp):
                def step(e, d):
                    u = e + 2
                    if ok(u):
                        sp.wait_ge(s["w_hi"], 3 * (u - 1))
                        sp.wait_ge(s["w_lo"], 3 * (u - 1))
                        expert_weights(sp, g, io, u, d % 2)
                pipeline(sp, step, 0, 0, E - 2, 2)

            @block.gpsimd
            def _(pool):
                def step(e, d):
                    u = e + 2
                    if ok(u):
                        pool.wait_ge(s["xt_mm"], CT * (u - 1))
                        gather_rows(pool, g, io, u)
                    u = e - 1
                    if ok(u):
                        c = (d + 1) % 2
                        need(pool, s["added"], 16 * CT * u)
                        for n in range(CT):
                            pool.wait_ge(s["y_ok"], CT * u + n + 1)
                            pool.indirect_dma_start(
                                out=io["out"], out_offset=bass.IndirectOffsetOnAxis(ap=lst[:, u * CT + n, 0:1], axis=0),
                                in_=res[:, c, n, :], in_offset=None, compute_op=ALU.add).then_inc(s["added"], 16)
                for e in range(E + 1):
                    step(e, e % 2)
                pool.wait_ge(s["added"], 16 * CT * E)

            @block.scalar
            def _(act):
                act.activation(sg[:, 0, 0:1], g.half[:, 0:1], ACT.Silu).then_inc(s["warm"], 1)
                act.wait_ge(s["warm"], 1)

                def silu(u, n):
                    v = 4 * u + n
                    act.wait_ge(s["g_mm"], v + 1)
                    need(act, s["hf"], v - 1)
                    act.activation(sg[:, n % 2], ps_g[n % 2][:, :], ACT.Silu, scale=1 / WS).then_inc(s["silu"], 1)

                def hidden_high(u, d, n):
                    v = 4 * u + n
                    h, i = UNITS[n]
                    act.wait_ge(s["hf"], v + 1)
                    need(act, s["y_mm"], CT * (u - 1))
                    act.activation(hid[:, d % 2, 0, i, h * HN:(h + 1) * HN], hf[:, n % 2], ACT.Copy).then_inc(s["h_hi"], 1)

                def rows_high(u, c, n):
                    act.wait_ge(s["xt_mm"], CT * u + n + 1)
                    if n == 0:
                        need(act, s["u_mm"], 4 * (u - 1))
                    act.activation(xT[:, c, 0, :, n * P:(n + 1) * P], ps_x[n % 2][:, :, :], ACT.Copy).then_inc(s["xt_hi"], 1)

                def weights_high(u, c, n):
                    act.wait_ge(w_in[c], 48 * (u // 2 + 1))
                    if n == 0:
                        need(act, s["u_mm"], 4 * (u - 1))
                    if n == 2:
                        need(act, s["y_mm"], CT * (u - 1))
                    act.activation(w[:, c, 0, PARTS[n]], raw[:, c, PARTS[n]], ACT.Copy, scale=WS).then_inc(s["w_hi"], 1)

                def step(e, d):
                    after = (d + 1) % 2
                    for n in range(4):
                        if ok(e):
                            silu(e, n)
                        if n < 3 and ok(e + 1):
                            weights_high(e + 1, after, n)
                        if ok(e):
                            hidden_high(e, d, n)
                        u = e + 1
                        if ok(u):
                            rows_high(u, after, n)
                            if n == 3:
                                rows_high(u, after, 4)
                        u = e - 1
                        if n == 0 and ok(u):
                            for i in range(CT):
                                act.wait_ge(s["y_mm"], CT * u + i + 1)
                                if i == 0:
                                    need(act, s["added"], 16 * CT * (u - 1))
                                act.activation(res[:, after, i], ps_y[i % 2][:, :], ACT.Copy,
                                               scale=lst[:, u * CT + i, 1:2].bitcast(f32)).then_inc(s["y_ok"], 1)
                pipeline(act, step, 1, 1, E, 2)

            @block.vector
            def _(dve):
                def unit(u, d, n):
                    v = 4 * u + n
                    h, i = UNITS[n]
                    cols = slice(h * HN, (h + 1) * HN)
                    dve.wait_ge(s["silu"], v + 1)
                    dve.wait_ge(s["u_mm"], v + 1)
                    need(dve, s["h_hi"], v - 1)
                    need(dve, s["h_lo"], v - 1)
                    dve.scalar_tensor_tensor(hf[:, n % 2], ps_u[n % 2][:, :], HS / WS, sg[:, n % 2], ALU.mult,
                                             ALU.mult).then_inc(s["hf"], 1)
                    dve.wait_ge(s["h_hi"], v + 1)
                    dve.tensor_tensor(hid[:, d % 2, 1, i, cols], hf[:, n % 2], hid[:, d % 2, 0, i, cols],
                                      ALU.subtract).then_inc(s["h_lo"], 1)

                def rows_low(u, c, n):
                    dve.wait_ge(s["xt_hi"], CT * u + n + 1)
                    cols = slice(n * P, (n + 1) * P)
                    dve.tensor_tensor(xT[:, c, 1, :, cols], ps_x[n % 2][:, :, :], xT[:, c, 0, :, cols],
                                      ALU.subtract).then_inc(s["xt_lo"], 1)

                def weights_low(u, c, n):
                    dve.wait_ge(s["w_hi"], 3 * u + n + 1)
                    dve.scalar_tensor_tensor(w[:, c, 1, PARTS[n]], raw[:, c, PARTS[n]], WS, w[:, c, 0, PARTS[n]], ALU.mult,
                                             ALU.subtract).then_inc(s["w_lo"], 1)

                def step(e, d):
                    after = (d + 1) % 2
                    for n in range(4):
                        if ok(e):
                            unit(e, d, n)
                        if ok(e + 1):
                            rows_low(e + 1, after, n)
                            if n < 3:
                                weights_low(e + 1, after, n)
                            else:
                                rows_low(e + 1, after, 4)
                pipeline(dve, step, 1, 0, E, 2)

            @block.tensor
            def _(pe):
                def unit(u, d, n):
                    v = 4 * u + n
                    h, i = UNITS[n]
                    c = d % 2
                    if n == 0:
                        pe.wait_ge(s["w_lo"], 3 * u + 2)
                    for bank, sem, read, at in ((ps_g, "g_mm", "silu", 0), (ps_u, "u_mm", "hf", KC * IE)):
                        need(pe, s[read], v - 1)
                        if n % 2 == 0 and at == 0:
                            pe.wait_ge(s["xt_lo"], CT * u + (3 if h == 0 else CT))
                        matmuls(pe, bank[n % 2][:, :],
                                lambda a, k: w[:, c, a, at + k * IE + i * P:at + k * IE + (i + 1) * P],
                                lambda a, k: xT[:, c, a, k, h * HN:(h + 1) * HN]).then_inc(s[sem], 1)

                def rows_transposed(u, c, n):
                    if n == 0:
                        pe.wait_ge(x_in[c], 16 * CT * (u // 2 + 1))
                    need(pe, s["xt_lo"], CT * u + max(n - 1, 0))
                    for k in range(KC):
                        last = pe.transpose(ps_x[n % 2][:, k, :], xg[:, c, n, k * P:(k + 1) * P], g.ident[:, :])
                    last.then_inc(s["xt_mm"], 1)

                def step(e, d):
                    after = (d + 1) % 2
                    for n in range(4):
                        if ok(e):
                            unit(e, d, n)
                        if ok(e + 1):
                            rows_transposed(e + 1, after, n)
                            if n == 3:
                                rows_transposed(e + 1, after, 4)
                        u = e - 1
                        if n == 0 and ok(u):
                            for i in range(CT):
                                pe.wait_ge(s["h_lo"], 4 * u + 4)
                                pe.wait_ge(s["w_lo"], 3 * u + 3)
                                need(pe, s["y_ok"], CT * u + max(i - 1, 0))
                                matmuls(pe, ps_y[i % 2][:, :], lambda a, j: hid[:, after, a, j, i * P:(i + 1) * P],
                                        lambda a, j: w[:, after, a, 2 * KC * IE + j * D:2 * KC * IE + (j + 1) * D],
                                        ks=range(NI)).then_inc(s["y_mm"], 1)
                pipeline(pe, step, 1, 1, E, 2)


class State:
    pass


def program(nc, io, out, stop=9):
    Scope.semaphores = []
    with ExitStack() as ctx:
        m = Scope(nc, ctx, "program")
        g = State()
        g.x = m.sb("x", [P, NT, D])
        g.ident = m.sb("ident", [P, P])
        g.half = m.sb("half", [P, 1])
        g.round_c = m.sb("round_c", [P, 2])
        g.eps = m.sb("eps", [P, 1])
        g.one = m.sb("one", [P, 1])
        g.ws = m.sb("ws", [P, 1])
        g.logits = m.sb("logits", [P, NT, E + 1])
        g.wgu = m.sb("wgu", [P, 2 * KC, 2, IS], f16)
        half = g.wgu[:, 0:KC].rearrange("p k q n -> p (k q n)"), g.wgu[:, KC:2 * KC].rearrange("p k q n -> p (k q n)")
        g.m0 = half[0][:, 0:2 * KC * JB].rearrange("p (q k n) -> p q k n", q=2, k=KC)
        g.v0 = half[1][:, 0:2 * B * D].rearrange("p (q b n) -> p q b n", q=2, b=B)
        g.x_in = m.sem("x_in")
        g.keys_ok = m.sem("keys_ok")
        io = dict(io, out=out)
        io["xn_rows"] = nc.dram_tensor("xn_rows", [T + CAP, D], f32, kind="Internal").ap()
        io["xt_tiles"] = nc.dram_tensor("xt_tiles", [NT, P, 2 * KC * P], f16, kind="Internal").ap()
        io["lists"] = nc.dram_tensor("lists", [E * CAP, 2], u32, kind="Internal").ap()
        with ExitStack() as actx:
            a = Scope(nc, actx, "att")
            g.simb = a.sb("simb", [P, JB])
            g.k1 = a.sb("k1", [P, 2, KC, JB], f16)
            g.v1 = a.sb("v1", [P, 2, B, D], f16)
            g.wq1 = a.sb("wq1", [P, 2, KC, D], f16)
            g.wo1 = a.sb("wo1", [P, 2, KC, D], f16)
            g.qr = a.sb("qr", [P, KC, D], bf16)
            g.rs = a.sb("rs", [P, D])
            g.kbd = a.sb("kbd", [P, 2, KC, HC, J], f16)
            setup(nc, g, io)
            if stop >= 1:
                attention0(nc, g)
            if stop >= 2:
                quantised(nc, g)
            if stop >= 3:
                attention1(nc, g, io)
        Scope.clear_semaphores(nc)
        if stop < 4:
            done = m.sem("done")
            with nc.Block() as block:
                @block.sync
                def _(sp):
                    sp.dma_start(out[0:T].rearrange("(t p) d -> p t d", p=P), g.x[:, :, :]).then_inc(done, 16)
                    sp.wait_ge(done, 16)
            return
        place = g.x[:, :, :].rearrange("p t n -> p (t n)")
        g.ex_raw = place[:, 0:2 * WN].rearrange("p (s n) -> p s n", s=2)
        g.ex_rows, g.ex_res = (place[:, o:o + 2 * CT * D].rearrange("p (s c n) -> p s c n", s=2, c=CT)
                               for o in (2 * WN, 2 * WN + 2 * CT * D))
        g.ex_slots = m.sb("ex_slots", [P, E * CT, 2], u32)
        g.ex_w_in = [m.sem(f"ex_w_in{n}") for n in range(2)]
        g.ex_x_in = [m.sem(f"ex_x_in{n}") for n in range(2)]
        shared(nc, g, io)
        experts(nc, g, io)


def layout(a):
    import numpy as np
    c = np.ascontiguousarray

    def chunks(v):
        return c(v.reshape(KC, P).T)

    return {
        "x": c(a["x"].reshape(T, D)),
        "ctxT": c(a["ctx_1024"].reshape(JB, D).T),
        "L0_Wk": c(a["L0_xattn_Wk"]), "L0_Wv": c(a["L0_xattn_Wv"]), "L0_WqT": c(a["L0_xattn_Wq"].T),
        "L0_bq": chunks(a["L0_xattn_bq"]), "L0_bk": chunks(a["L0_xattn_bk"]), "L0_bv": c(a["L0_xattn_bv"]),
        "L0_rhsT": c(a["L0_ffn_rhs"].T),
        "L1_wqT": c(a["L1_xattn_w_q"].T), "L1_wkT": c(a["L1_xattn_w_k"].T),
        "L1_wvT": c(a["L1_xattn_w_v"].T), "L1_woT": c(a["L1_xattn_w_o"].T),
        "gwT": c(a["L1_ffn_gate_w"].T),
        "dyn_gT": c(a["L1_ffn_dyn_gate_w"].transpose(0, 2, 1)), "dyn_uT": c(a["L1_ffn_dyn_up_w"].transpose(0, 2, 1)),
        "dyn_dT": c(a["L1_ffn_dyn_down_w"].transpose(0, 2, 1)),
        "sh_guT": c(np.concatenate([a["L1_ffn_sh_gate_w"][0].T, a["L1_ffn_sh_up_w"][0].T])),
        "sh_dT": c(a["L1_ffn_sh_down_w"][0].T),
    }


def kernel(**inputs):
    import numpy as np
    import concourse.bacc as bacc
    from concourse.bass_utils import run_bass_kernel_spmd

    nc = bacc.Bacc("TRN2", target_bir_lowering=False, num_devices=1)
    arrays = layout({name: np.asarray(v) for name, v in inputs.items()})
    io = {name: nc.dram_tensor("in_" + name, v.shape, mybir.dt.from_np(v.dtype), kind="ExternalInput").ap()
          for name, v in arrays.items()}
    out = nc.dram_tensor("out_rows", (T + CAP, D), f32, kind="ExternalOutput").ap()
    program(nc, io, out)
    r = run_bass_kernel_spmd(nc, [{"in_" + name: v for name, v in arrays.items()}], core_ids=[0])
    return r.results[0]["out_rows"][0:T].reshape(B, S, D)
```

```python
import concourse.bass as bass
from concourse import mybir
from contextlib import ExitStack

f32 = mybir.dt.float32
f16 = mybir.dt.float16
bf16 = mybir.dt.bfloat16
u32 = mybir.dt.uint32
ALU = mybir.AluOpType
ACT = mybir.ActivationFunctionType
AX = mybir.AxisListType

P = 128
B, S, D = 8, 512, 512
J = 120
T = B * S
NT = T // P
TB = S // P
KC = D // P
JB = B * J
HEADS, DH = 16, 32
HC = P // DH
E = 8
IE, IS = 256, 1024
CAP = 640
EPS = 1e-5
WS = 64.0
HS = 1.0 / 16
CT = CAP // P
WN = 2 * KC * IE + IE // P * D
PARTS = [slice(n * WN // 3, (n + 1) * WN // 3) for n in range(3)]
SC0 = float(D) ** -0.5
SC1 = float(DH) ** -0.5
PASSES = ((0, 0), (1, 0), (0, 1))
ROUND = 1.5 * 2.0 ** 23


def need(eng, sem, n):
    if isinstance(n, int) and n <= 0:
        return
    eng.wait_ge(sem, n)


def live(t):
    return not isinstance(t, int) or 0 <= t < NT


def pipeline(eng, step, lead, lag, n=NT, by=TB, head=None, tail=0):
    first = (head or by) // by
    end = (n - max(lead, tail)) // by
    for s in range(-lead, first * by):
        step(s, s % by)
    with eng.Fori(first, end) as i:
        for d in range(by):
            step(i * by + d, d)
    for s in range(end * by, n + lag):
        step(s, s % by)


class Scope:

    semaphores: list = []

    def __init__(self, nc, ctx, stage):
        self.nc, self.ctx, self.stage = nc, ctx, stage + "_"

    def sb(self, name, shape, dt=f32):
        return self.ctx.enter_context(self.nc.sbuf_tensor(self.stage + name, shape, dt))

    def ps(self, name, shape, dt=f32):
        return self.ctx.enter_context(self.nc.psum_tensor(self.stage + name, shape, dt))

    def sem(self, name):
        handle = self.nc.alloc_semaphore(self.stage + name)
        Scope.semaphores.append(handle)
        return handle

    @classmethod
    def clear_semaphores(cls, nc):
        nc.clear_and_free_semaphores(cls.semaphores)
        nc.all_engine_barrier()
        cls.semaphores = []


def matmuls(pe, out, lhs, rhs, ks=range(KC)):
    terms = [(k, a, b) for k in ks for a, b in PASSES]
    for n, (k, a, b) in enumerate(terms):
        last = pe.matmul(out, lhs(a, k), rhs(b, k), start=n == 0, stop=n == len(terms) - 1)
    return last


def block_keys(pool, g, b, c):
    for h in range(HC):
        rows = slice(h * DH, (h + 1) * DH)
        need(pool, g.keys_ok, HC * (KC * b + c) + h)
        pool.tensor_copy(g.kbd[rows, :, c, h, :], g.k1[rows, :, c, bass.ds(b * J, J)]).then_inc(g.keys_ok, 1)


def setup(nc, g, io):
    with ExitStack() as ctx:
        m = Scope(nc, ctx, "setup")
        W = ["L0_Wk", "L0_Wv", "L0_WqT", "L1_wkT", "L1_wvT", "L1_wqT", "L1_woT", "L0_rhs"]
        NW = len(W)
        raw = g.x[:, NT - 12:NT, :].rearrange("p (w k) n -> p w k n", w=3)
        ctx_s = m.sb("ctx_s", [P, 2, KC, JB], f16)
        wk = g.x[:, NT - 24:NT - 12, :].rearrange("p (w q k) n -> p w q (k n)", w=3, q=2) \
            .bitcast(f16).rearrange("p w q (k n) -> p w q k n", k=KC)
        k0f = g.x[:, 0:8, :].rearrange("p t n -> p (t n)")[:, 0:KC * JB] \
            .rearrange("p (k n) -> p k n", k=KC)
        ctxf = k0f
        k0 = m.sb("k0", [P, 2, KC, JB], f16)
        fstage = m.sb("fstage", [P, 2, D])
        bvb = m.sb("bvb", [P, D])
        bqk = m.sb("bqk", [P, 2, KC])
        bqb = m.sb("bqb", [P, KC, P])
        ones = m.sb("ones", [P, P])
        qabs = m.sb("qabs", [P, KC])
        qinv = m.sb("qinv", [P, KC])
        rT = k0[:, :, :, :].rearrange("p q k n -> p (q k n)")[:, 0:2 * KC * D].bitcast(f32) \
            .rearrange("p (k n) -> p k n", k=KC)
        dg = bqb
        ring = [m.ps(f"ring{i}", [P, D]) for i in range(4)]
        bps = [m.ps(f"bps{i}", [P, D]) for i in range(2)]
        xp = [m.ps(f"xp{i}", [P, KC, P]) for i in range(2)]

        loaded = [m.sem(f"loaded{n}") for n in range(NW)]
        x_in, ctx_in, bias_in = g.x_in, [m.sem(f"ctx_in{n}") for n in range(2)], m.sem("bias_in")
        hi_done, lo_done = m.sem("hi_done"), m.sem("lo_done")
        ctx_hi, ctx_lo = m.sem("ctx_hi"), m.sem("ctx_lo")
        bq_done, ones_done = m.sem("bq_done"), m.sem("ones_done")
        job_mm, job_f, job_hi, job_lo = (m.sem(n) for n in ("job_mm", "job_f", "job_hi", "job_lo"))
        bias_mm, bias_out = m.sem("bias_mm"), m.sem("bias_out")
        id0, id1 = m.sem("id0"), m.sem("id1")
        kbd_zero = m.sem("kbd_zero")
        r_mm, r_abs, r_s1, r_s2, r_q, r_b, r_out, r_dg, r_bc = (
            m.sem(n) for n in ("r_mm", "r_abs", "r_s1", "r_s2", "r_q", "r_b", "r_out", "r_dg", "r_bc"))

        jobs = [("k0", (mm, h)) for h in range(2) for mm in range(KC)]
        jobs += [("v0", b) for b in range(B)]
        jobs += [("m0", (mm, h)) for mm in range(KC) for h in range(2)]
        jobs += [("k1", (mm, h)) for mm in range(KC) for h in range(2)]
        jobs += [("v1", b) for b in range(B)]
        last_job = [8, 16, 24, 32, 40]
        weight_of = {"k0": 0, "v0": 1, "m0": 2, "k1": 3, "v1": 4}
        NH = JB // 2

        def shape(kind):
            return (slice(0, J), slice(0, D)) if kind[0] == "v" else (slice(0, P), slice(0, NH))

        def parts(kind, ix):
            if kind == "v0":
                return g.v0[0:J, 0, ix, :], g.v0[0:J, 1, ix, :]
            if kind == "v1":
                return g.v1[0:J, 0, ix, :], g.v1[0:J, 1, ix, :]
            to = {"k0": k0, "m0": g.m0, "k1": g.k1}[kind]
            mm, h = ix
            return tuple(to[:, q, mm, h * NH:(h + 1) * NH] for q in range(2))

        def f_of(n):
            kind, ix = jobs[n]
            if kind == "k0":
                return k0f[:, ix[0], ix[1] * NH:(ix[1] + 1) * NH]
            rows, cols = shape(kind)
            return fstage[rows, n % 2, cols]

        def w_part(n, q):
            if n < 5:
                return wk[:, n % 3, q]
            return {5: g.wq1, 6: g.wo1}[n][:, q]

        with nc.Block() as block:

            @block.sync
            def _(sp):
                def context(h):
                    cols = slice(h * NH, (h + 1) * NH)
                    sp.dma_start(ctxf[:, :, cols], io["ctxT"].rearrange("(k p) n -> p k n", p=P)[:, :, cols]).then_inc(ctx_in[h], 16)

                def weight(n):
                    sp.dma_start(raw[:, n % 3], io[W[n]].rearrange("(k p) n -> p k n", p=P)).then_inc(loaded[n], 16)

                context(0)
                weight(0)
                context(1)
                weight(1)
                sp.dma_start(bvb[:, :], io["L0_bv"].partition_broadcast(P)).then_inc(bias_in, 16)
                sp.dma_start(bqk[:, 0, :], io["L0_bq"]).then_inc(bias_in, 16)
                sp.dma_start(bqk[:, 1, :], io["L0_bk"]).then_inc(bias_in, 16)
                for n in range(2, NW - 1):
                    if n >= 3:
                        sp.wait_ge(hi_done, n - 2)
                        sp.wait_ge(lo_done, n - 2)
                    weight(n)
                sp.wait_ge(job_mm, 24)
                sp.dma_start(rT[:, :, :], io["L0_rhsT"].rearrange("(k p) n -> p k n", p=P)).then_inc(loaded[NW - 1], 16)
                xs = io["x"].rearrange("(t p) d -> p t d", p=P)
                sp.dma_start(g.x[:, 0:8, :], xs[:, 0:8, :]).then_inc(x_in[0], 16)
                sp.wait_ge(hi_done, NW - 1)
                sp.wait_ge(lo_done, NW - 1)
                sp.dma_start(g.x[:, NT - 12:NT, :], xs[:, NT - 12:NT, :]).then_inc(x_in[1], 16)
                sp.wait_ge(job_mm, len(jobs))
                sp.dma_start(g.x[:, 8:NT - 12, :], xs[:, 8:NT - 12, :]).then_inc(x_in[2], 16)

            @block.gpsimd
            def _(pool):
                pool.memset(g.ident[:, :], 0.0).then_inc(id0, 1)
                pool.memset(ones[:, :], 1.0).then_inc(ones_done, 1)
                pool.memset(g.half[:, :], -0.5).then_inc(id1, 1)
                pool.memset(g.eps[:, :], EPS).then_inc(id1, 1)
                pool.memset(g.one[:, :], 1.0).then_inc(id1, 1)
                pool.memset(g.ws[:, :], WS).then_inc(id1, 1)
                pool.wait_ge(id0, 1)
                pool.affine_select(out=g.ident[:, :], in_=g.ident[:, :], compare_op=ALU.not_equal, fill=1.0,
                                   base=0, pattern=[[-1, P]], channel_multiplier=1).then_inc(id0, 1)
                pool.memset(g.kbd[:, :, :, :, :], 0.0).then_inc(kbd_zero, 1)
                pool.wait_ge(kbd_zero, 1)
                pool.wait_ge(job_hi, 32)
                pool.wait_ge(job_lo, 32)
                for c in range(KC):
                    block_keys(pool, g, 0, c)
                pool.wait_ge(g.keys_ok, HC * KC)

            @block.scalar
            def _(act):
                def context(h):
                    cols = slice(h * NH, (h + 1) * NH)
                    act.wait_ge(ctx_in[h], 16)
                    act.activation(ctx_s[:, 0, :, cols], ctxf[:, :, cols], ACT.Copy).then_inc(ctx_hi, 1)

                def split(n):
                    act.wait_ge(loaded[n], 16)
                    if 3 <= n < 5:
                        act.wait_ge(job_mm, last_job[n - 3])
                    act.activation(w_part(n, 0), raw[:, n % 3], ACT.Copy, scale=WS).then_inc(hi_done, 1)

                context(0)
                split(0)
                context(1)
                split(1)
                for n, (kind, ix) in enumerate(jobs):
                    act.wait_ge(job_f, n + 1)
                    act.activation(parts(kind, ix)[0], f_of(n), ACT.Copy).then_inc(job_hi, 1)
                    if n % 4 == 3 and n // 4 + 2 < NW - 1:
                        split(n // 4 + 2)
                    if 32 <= n < 32 + KC:
                        act.wait_ge(r_s2, 1)
                        act.wait_ge(r_abs, 2)
                        k = n - 32
                        act.activation(rT[:, k, :], rT[:, k, :], ACT.Identity, scale=qinv[:, k:k + 1],
                                       bias=g.round_c[:, 0:1]).then_inc(r_q, 1)

            @block.vector
            def _(dve):
                dve.memset(g.round_c[:, 0:1], ROUND).then_inc(r_abs, 1)
                dve.memset(g.round_c[:, 1:2], -ROUND).then_inc(r_abs, 1)

                def context(h):
                    cols = slice(h * NH, (h + 1) * NH)
                    dve.wait_ge(ctx_hi, h + 1)
                    dve.tensor_tensor(ctx_s[:, 1, :, cols], ctxf[:, :, cols], ctx_s[:, 0, :, cols], ALU.subtract) \
                        .then_inc(ctx_lo, 1)

                def split(n):
                    dve.wait_ge(hi_done, n + 1)
                    dve.scalar_tensor_tensor(w_part(n, 1), raw[:, n % 3], WS, w_part(n, 0), ALU.mult,
                                             ALU.subtract).then_inc(lo_done, 1)

                context(0)
                split(0)
                context(1)
                dve.wait_ge(bias_in, 48)
                for n, (kind, ix) in enumerate(jobs):
                    if n == 2:
                        split(1)
                    if n == 4:
                        dve.wait_ge(ones_done, 1)
                        for k in range(KC):
                            dve.tensor_scalar(bqb[:, k, :], ones[:, :], bqk[:, 0, k:k + 1], None, ALU.mult).then_inc(bq_done, 1)
                    rows, cols = shape(kind)
                    out, bank = f_of(n), ring[n % 4][rows, cols]
                    dve.wait_ge(job_mm, n + 1)
                    need(dve, job_hi, n - 1)
                    need(dve, job_lo, n - 1)
                    if kind == "k0":
                        dve.tensor_scalar(out, bank, 1 / WS, bqk[:, 1, ix[0]:ix[0] + 1], ALU.mult, ALU.add).then_inc(job_f, 1)
                    elif kind == "v0":
                        dve.scalar_tensor_tensor(out, bank, 1 / WS, bvb[rows, :], ALU.mult, ALU.add).then_inc(job_f, 1)
                    else:
                        dve.tensor_scalar(out, bank, 1 / WS, None, ALU.mult).then_inc(job_f, 1)
                    dve.wait_ge(job_hi, n + 1)
                    dve.wait_ge(job_f, n + 1)
                    hi, lo = parts(kind, ix)
                    dve.tensor_tensor(lo, out, hi, ALU.subtract).then_inc(job_lo, 1)
                    if n % 4 == 3 and n // 4 + 2 < NW - 1:
                        split(n // 4 + 2)
                    if n == 30:
                        dve.wait_ge(loaded[NW - 1], 16)
                        dve.tensor_reduce(qabs[:, :], rT[:, :, :], AX.X, ALU.max, apply_absolute_value=True).then_inc(r_s1, 1)
                        dve.wait_ge(r_s1, 1)
                        dve.tensor_scalar(qabs[:, :], qabs[:, :], 1e-12, 1 / 127.0, ALU.max, ALU.mult).then_inc(r_s1, 1)
                        dve.wait_ge(r_s1, 2)
                        dve.reciprocal(qinv[:, :], qabs[:, :]).then_inc(r_s2, 1)
                        dve.wait_ge(id0, 2)
                        for k in range(KC):
                            dve.tensor_scalar(dg[:, k, :], g.ident[:, :], qabs[:, k:k + 1], None, ALU.mult).then_inc(r_dg, 1)
                    if n == 15:
                        for h in range(2):
                            dve.wait_ge(bias_mm, h + 1)
                            dve.tensor_scalar(g.simb[:, h * NH:(h + 1) * NH], bps[h][:, 0:NH], SC0, None,
                                              ALU.mult).then_inc(bias_out, 1)
                for c in range(KC):
                    dve.wait_ge(r_mm, c + 1)
                    dve.tensor_scalar(g.qr[:, c, :].rearrange("p (k n) -> p k n", k=KC), xp[c % 2][:, :, :], ROUND,
                                      None, ALU.subtract).then_inc(r_out, 1)
                dve.wait_ge(r_bc, 1)
                dve.tensor_copy(g.rs[:, :], bps[0][:, :]).then_inc(r_b, 1)

            @block.tensor
            def _(pe):
                seen = -1
                for n, (kind, ix) in enumerate(jobs):
                    rows, cols = shape(kind)
                    w = weight_of[kind]
                    if w > seen:
                        pe.wait_ge(lo_done, w + 1)
                        pe.wait_ge(hi_done, w + 1)
                        seen = w
                    if n in (0, KC):
                        pe.wait_ge(ctx_lo, n // KC + 1)
                    if n >= 4:
                        pe.wait_ge(job_f, n - 3)
                    out = ring[n % 4][rows, cols]
                    if kind[0] == "v":
                        last = matmuls(pe, out, lambda q, k: ctx_s[:, q, k, ix * J:(ix + 1) * J],
                                       lambda q, k: wk[:, w % 3, q, k, :])
                    else:
                        mm, h = ix
                        if kind == "m0" and n == 16:
                            pe.wait_ge(job_lo, 8)
                        src = k0 if kind == "m0" else ctx_s
                        last = matmuls(pe, out, lambda q, k: wk[:, w % 3, q, k, mm * P:(mm + 1) * P],
                                       lambda q, k: src[:, q, k, h * NH:(h + 1) * NH])
                    last.then_inc(job_mm, 1)
                    if n == 15:
                        pe.wait_ge(bq_done, KC)
                        pe.wait_ge(job_f, 8)
                        for h in range(2):
                            for k in range(KC):
                                last = pe.matmul(bps[h][:, 0:NH], bqb[:, k, :], k0f[:, k, h * NH:(h + 1) * NH],
                                                 start=k == 0, stop=k == KC - 1)
                            last.then_inc(bias_mm, 1)
                pe.wait_ge(id0, 2)
                pe.wait_ge(r_q, KC)
                for c in range(KC):
                    if c >= 2:
                        pe.wait_ge(r_out, c - 1)
                    for k in range(KC):
                        last = pe.transpose(xp[c % 2][:, k, :], rT[:, k, c * P:(c + 1) * P], g.ident[:, :])
                    last.then_inc(r_mm, 1)
                pe.wait_ge(r_dg, KC)
                pe.wait_ge(bias_out, 2)
                for k in range(KC):
                    last = pe.matmul(bps[0][:, k * P:(k + 1) * P], ones[:, :], dg[:, k, :], start=True, stop=True)
                last.then_inc(r_bc, 1)


class Norm:

    def __init__(self, m, name):
        self.st = m.sb(name + "_st", [P, 4, 6])
        self.mv = m.sb(name + "_mv", [P, 4, 2])
        self.ve = m.sb(name + "_ve", [P, 4, 1])
        self.rstd = m.sb(name + "_rstd", [P, 4, 1])
        self.xn = m.sb(name + "_xn", [P, 2, D])
        self.stats, self.aggr, self.var, self.root, self.ok = (
            m.sem(f"{name}_{n}") for n in ("stats", "aggr", "var", "root", "ok"))

    def before(self, dve, u, read=None):
        need(dve, self.stats, u)
        need(dve, read or self.root, u - 4)

    def statistics(self, dve, g, u, d, waits=True):
        if waits:
            self.before(dve, u)
        if live(u):
            dve.bn_stats(self.st[:, d], g.x[:, u, :]).then_inc(self.stats, 1)
        if live(u - 1):
            dve.bn_aggr(self.mv[:, (d + 3) % 4], self.st[:, (d + 3) % 4]).then_inc(self.aggr, 1)

    def inverse_root(self, pool, g, u, d):
        pool.wait_ge(self.aggr, u + 1)
        need(pool, self.ok, u - 3)
        pool.tensor_tensor(self.ve[:, d], self.mv[:, d, 1:2], g.eps[:, :], ALU.add).then_inc(self.var, 1)
        pool.wait_ge(self.var, u + 1)
        pool.tensor_tensor(self.rstd[:, d], self.ve[:, d], g.half[:, :], ALU.pow).then_inc(self.root, 1)

    def apply(self, dve, g, u, d, read, behind=1):
        dve.wait_ge(self.root, u + 1)
        need(dve, read, u - behind)
        dve.tensor_scalar(self.xn[:, d % 2], g.x[:, u, :], self.mv[:, d, 0:1], self.rstd[:, d], ALU.subtract,
                          ALU.mult).then_inc(self.ok, 1)


def layer0(nc, g):
    LEAD, LAG = 5, 10
    HEAD = 12
    with ExitStack() as ctx:
        m = Scope(nc, ctx, "layer0")
        ln = Norm(m, "a")
        xT = m.sb("xT", [P, 2, 2, KC, P], f16)
        sim = m.sb("sim", [P, 2, J])
        nmax = m.sb("nmax", [P, 2, 1])
        prob = m.sb("prob", [P, 2, J])
        y = m.sb("y", [P, 2, D])
        rsum = m.sb("rsum", [P, 4, 1])
        rinv = m.sb("rinv", [P, 4, 1])
        pT = m.sb("pT", [P, 2, 2, P], f16)
        lq = Norm(m, "q")
        amax = m.sb("amax", [P, 4, 1])
        scale = m.sb("scale", [P, 4, 1])
        inv = m.sb("inv", [P, 4, 1])
        xr = m.sb("xr", [P, 2, D])
        qT = m.sb("qT", [P, 2, KC, P], bf16)
        yq = m.sb("yq", [P, 2, D])
        ps_x = [m.ps(f"ps_x{i}", [P, KC, P]) for i in range(2)]
        ps_s, ps_p, ps_y, ps_qy = (m.ps(n, [P, D]) for n in ("ps_s", "ps_p", "ps_y", "ps_qy"))
        ps_qx = [m.ps(f"ps_qx{i}", [P, KC, P]) for i in range(2)]
        s = {n: m.sem("a0_" + n) for n in ("xt_mm", "xt_hi", "xt_lo", "sim_mm", "sim_ok", "max_ok", "exp_ok", "sum_ok", "p_mm",
                                           "p_hi", "p_lo", "y_mm", "y_ok", "x_new")}
        q = {n: m.sem("q_" + n) for n in ("amax", "scale", "inv", "xr", "xt_mm", "xt_ok", "y_mm", "y_ok", "x_new")}

        def run(eng, step):
            pipeline(eng, step, LEAD, LAG, head=HEAD)

        with nc.Block() as block:

            @block.gpsimd
            def _(pool):
                def step(t, d):
                    if live(t + 3):
                        ln.inverse_root(pool, g, t + 3, (d + 3) % 4)
                    u, c = t - 10, d % 2
                    if live(u):
                        pool.wait_ge(q["y_ok"], u + 1)
                        pool.tensor_tensor(g.x[:, u, :], g.x[:, u, :], yq[:, c], ALU.add).then_inc(q["x_new"], 1)
                    u, c = t - 3, (d + 1) % 2
                    if live(u):
                        pool.wait_ge(s["y_ok"], u + 1)
                        pool.tensor_tensor(g.x[:, u, :], g.x[:, u, :], y[:, c], ALU.add).then_inc(s["x_new"], 1)
                    u = t - 5
                    if live(u):
                        lq.inverse_root(pool, g, u, (d + 3) % 4)
                run(pool, step)

            @block.vector
            def _(dve):
                def step(t, d):
                    w, e = t - 6, (d + 2) % 4
                    if live(w):
                        lq.apply(dve, g, w, e, q["xr"])
                    u, c = t, d % 2
                    if live(u):
                        dve.wait_ge(s["sim_mm"], u + 1)
                        need(dve, s["exp_ok"], u - 1)
                        dve.scalar_tensor_tensor(sim[:, c], ps_s[:, 0:J], SC0, g.simb[:, bass.ds((u // TB) * J, J)],
                                                 ALU.mult, ALU.add).then_inc(s["sim_ok"], 1)
                        dve.wait_ge(s["sim_ok"], u + 1)
                        dve.tensor_reduce(nmax[:, c], sim[:, c], AX.X, ALU.max, negate=True).then_inc(s["max_ok"], 1)
                    if live(t - 4):
                        dve.wait_ge(s["x_new"], t - 3)
                    if live(t - 4) or live(t - 5):
                        lq.before(dve, t - 4)
                    u, c = t + 1, (d + 1) % 2
                    if live(u):
                        dve.wait_ge(s["xt_hi"], u + 1)
                        dve.tensor_tensor(xT[:, c, 1], ps_x[c][:, :, :], xT[:, c, 0], ALU.subtract).then_inc(s["xt_lo"], 1)
                    if live(t - 4) or live(t - 5):
                        lq.statistics(dve, g, t - 4, d, waits=False)
                    if live(t + 2):
                        ln.apply(dve, g, t + 2, (d + 2) % 4, s["xt_mm"])
                    if live(w):
                        dve.wait_ge(lq.ok, w + 1)
                        dve.tensor_reduce(amax[:, e], lq.xn[:, e % 2], AX.X, ALU.max,
                                          apply_absolute_value=True).then_inc(q["amax"], 1)
                    u, c = t - 1, (d + 1) % 2
                    if live(u):
                        dve.wait_ge(s["p_hi"], u + 1)
                        dve.tensor_tensor(pT[0:J, c, 1], ps_p[0:J, 0:P], pT[0:J, c, 0], ALU.subtract).then_inc(s["p_lo"], 1)
                        r = (d + 3) % 4
                        dve.wait_ge(s["exp_ok"], u + 1)
                        dve.reciprocal(rinv[:, r], rsum[:, r]).then_inc(s["sum_ok"], 1)
                    if live(w):
                        dve.wait_ge(q["amax"], w + 1)
                        need(dve, q["y_ok"], w - 3)
                        dve.tensor_scalar(scale[:, e], amax[:, e], 1e-12, 1 / 127.0, ALU.max, ALU.mult).then_inc(q["scale"], 1)
                    if isinstance(t, int) and t + 5 == 8:
                        dve.wait_ge(g.x_in[1], 16)
                        dve.wait_ge(g.x_in[2], 16)
                    if live(t + 5) or live(t + 4):
                        ln.before(dve, t + 5)
                    u, c = t - 9, (d + 3) % 4
                    if live(u):
                        dve.wait_ge(q["y_mm"], u + 1)
                        need(dve, q["x_new"], u - 1)
                        dve.scalar_tensor_tensor(yq[:, c % 2], ps_qy[:, :], scale[:, c], g.rs[:, :], ALU.mult,
                                                 ALU.mult).then_inc(q["y_ok"], 1)
                    if live(w):
                        dve.wait_ge(q["scale"], w + 1)
                        need(dve, q["xr"], w - 3)
                        dve.reciprocal(inv[:, e], scale[:, e]).then_inc(q["inv"], 1)
                    if live(t + 5) or live(t + 4):
                        ln.statistics(dve, g, t + 5, (d + 1) % 4, waits=False)
                dve.wait_ge(g.x_in[0], 16)
                run(dve, step)

            @block.scalar
            def _(act):
                def step(t, d):
                    u, c = t + 1, (d + 1) % 2
                    if live(u):
                        act.wait_ge(s["xt_mm"], u + 1)
                        need(act, s["sim_mm"], u - 1)
                        act.activation(xT[:, c, 0], ps_x[c][:, :, :], ACT.Copy).then_inc(s["xt_hi"], 1)
                    u, c = t - 7, (d + 1) % 4
                    if live(u):
                        act.wait_ge(q["inv"], u + 1)
                        need(act, q["xt_mm"], u - 1)
                        act.activation(xr[:, c % 2], lq.xn[:, c % 2], ACT.Identity, scale=inv[:, c],
                                       bias=g.round_c[:, 0:1]).then_inc(q["xr"], 1)
                    u, c = t - 1, (d + 1) % 2
                    if live(u):
                        act.wait_ge(s["p_mm"], u + 1)
                        need(act, s["y_mm"], u - 1)
                        act.activation(pT[0:J, c, 0], ps_p[0:J, 0:P], ACT.Copy).then_inc(s["p_hi"], 1)
                    u, c = t - 8, d % 2
                    if live(u):
                        act.wait_ge(q["xt_mm"], u + 1)
                        need(act, q["y_mm"], u - 1)
                        act.activation(qT[:, c], ps_qx[c][:, :, :], ACT.Identity, bias=g.round_c[:, 1:2]).then_inc(q["xt_ok"], 1)
                    u, c, r = t - 2, d % 2, (d + 2) % 4
                    if live(u):
                        act.wait_ge(s["y_mm"], u + 1)
                        act.wait_ge(s["sum_ok"], u + 1)
                        need(act, s["x_new"], u - 1)
                        act.activation(y[:, c], ps_y[:, :], ACT.Copy, scale=rinv[:, r]).then_inc(s["y_ok"], 1)
                    u, c = t, d % 2
                    if live(u):
                        act.wait_ge(s["max_ok"], u + 1)
                        need(act, s["p_mm"], u - 1)
                        need(act, s["sum_ok"], u - 3)
                        act.activation(prob[:, c], sim[:, c], ACT.Exp, bias=nmax[:, c],
                                       accum_out=rsum[:, d]).then_inc(s["exp_ok"], 1)
                run(act, step)

            @block.tensor
            def _(pe):
                def transposed(to, src):
                    for k in range(KC):
                        last = pe.transpose(to[:, k, :], src[:, k * P:(k + 1) * P], g.ident[:, :])
                    return last

                def step(t, d):
                    u, c = t, d % 2
                    if live(u):
                        pe.wait_ge(s["xt_lo"], u + 1)
                        need(pe, s["sim_ok"], u)
                        j0 = (u // TB) * J
                        matmuls(pe, ps_s[:, 0:J], lambda a, k: xT[:, c, a, k, :],
                                lambda a, k: g.m0[:, a, k, bass.ds(j0, J)]).then_inc(s["sim_mm"], 1)
                    u, c = t - 1, (d + 1) % 2
                    if live(u):
                        pe.wait_ge(s["exp_ok"], u + 1)
                        need(pe, s["p_lo"], u)
                        pe.transpose(ps_p[0:J, 0:P], prob[:, c], g.ident[:, :]).then_inc(s["p_mm"], 1)
                    u, c = t - 9, (d + 1) % 2
                    if live(u):
                        pe.wait_ge(q["xt_ok"], u + 1)
                        need(pe, q["y_ok"], u)
                        for k in range(KC):
                            last = pe.matmul(ps_qy[:, :], qT[:, c, k, :], g.qr[:, k, :], start=k == 0, stop=k == KC - 1)
                        last.then_inc(q["y_mm"], 1)
                    u, c = t - 2, d % 2
                    if live(u):
                        pe.wait_ge(s["p_lo"], u + 1)
                        need(pe, s["y_ok"], u)
                        b = u // TB
                        matmuls(pe, ps_y[:, :], lambda a, k: pT[0:J, c, a, :], lambda a, k: g.v0[0:J, a, b, :],
                                ks=(0,)).then_inc(s["y_mm"], 1)
                    u, c = t + 2, d % 2
                    if live(u):
                        pe.wait_ge(ln.ok, u + 1)
                        need(pe, s["xt_lo"], u - 1)
                        transposed(ps_x[c], ln.xn[:, c]).then_inc(s["xt_mm"], 1)
                    u, c = t - 7, (d + 1) % 2
                    if live(u):
                        pe.wait_ge(q["xr"], u + 1)
                        need(pe, q["xt_ok"], u - 1)
                        transposed(ps_qx[c], xr[:, c]).then_inc(q["xt_mm"], 1)
                run(pe, step)


def tokens(eng, g, io, b, c, done):
    for i in range(TB):
        src = io["xt_tiles"][b * TB + i, :, :].rearrange("p (a n) -> p a n", n=P)
        eng.dma_start(g.xs[:, c, :, :, i * P:(i + 1) * P].rearrange("p q k n -> p (q k) n"), src).then_inc(done, 16)


def attention1(nc, g, io):
    LEAD, LAG = 5, 9
    HEAD = 12
    with ExitStack() as ctx:
        m = Scope(nc, ctx, "attention1")
        ln = Norm(m, "b")
        xT = m.sb("xT", [P, 2, 2, KC, P], f16)
        qT = m.sb("qT", [P, 2, 2, KC, P], f16)
        nmax = m.sb("nmax", [P, 2, KC, HC])
        prob = m.sb("prob", [P, 4, HC, J])
        pT = m.sb("pT", [P, 4, 2, HC, P], f16)
        rsum = m.sb("rsum", [P, 2, HEADS])
        rinv = m.sb("rinv", [P, 2, HEADS])
        of = m.sb("of", [P, D])
        oT = m.sb("oT", [P, 2, 2, KC, P], f16)
        lg = Norm(m, "g")
        gT = m.sb("gT", [P, 2, 2, KC, P], f16)
        gwf = m.sb("gwf", [P, KC, E + 1])
        gws = m.sb("gws", [P, 2, KC, E + 1], f16)
        raw = g.qr[:, :, :].rearrange("p k n -> p (k n)").bitcast(f32)
        zero = raw[:, 0:D]
        ps_sf = [m.ps(f"ps_s{i}", [P, D]) for i in range(2)]
        ps_s = [v[:, 0:HC * J].rearrange("p (h j) -> p h j", h=HC) for v in ps_sf]
        ps_p = [m.ps(f"ps_p{i}", [P, HC, P]) for i in range(2)]
        ps_x = m.ps("ps_x", [P, KC, P])
        ps_l = ps_x[:, 0, 0:E + 1]
        ps_q = m.ps("ps_q", [P, KC, P])
        ps_o = m.ps("ps_o", [P, D])
        ps_y = m.ps("ps_y", [P, D])
        s = {n: m.sem("b_" + n) for n in ("xt_mm", "xt_hi", "xt_lo", "q_mm", "q_hi", "q_lo", "inv", "of", "o_tr", "o_hi",
                                          "o_lo", "y_mm", "x_new", "g_tr", "g_hi", "g_lo", "l_mm", "l_ok")}
        c4 = {n: m.sem("b4_" + n) for n in ("s_mm", "max", "exp", "p_mm", "p_hi", "p_lo", "o_mm")}
        w_in, w_scaled, w_hi, w_lo = (m.sem(n) for n in ("w_in", "w_scaled", "w_hi", "w_lo"))
        gw_in, gw_hi, gw_lo, zeroed, zero_out = (m.sem(n) for n in ("gw_in", "gw_hi", "gw_lo", "zeroed", "zero_out"))
        centred, xs_in = m.sem("centred"), m.sem("xs_in")
        rows_out = [m.sem(f"rows_out{n}") for n in range(2)]
        gt_out = [m.sem(f"gt_out{n}") for n in range(2)]

        def run(eng, step):
            pipeline(eng, step, LEAD, LAG, head=HEAD)

        def past(t, n):
            return isinstance(t, int) and t >= NT + n

        def bank_y(u):
            if isinstance(u, int) and u >= NT - 2:
                return ps_p[u % 2][:, :, :].rearrange("p h n -> p (h n)")
            return ps_y[:, :]

        def bank_g(t):
            if past(t, 2):
                return (ps_q, ps_o[:, :].rearrange("p (k n) -> p k n", k=KC))[t % 2]
            return ps_x

        with nc.Block() as block:

            @block.sync
            def _(sp):
                sp.dma_start(gwf[:, :, :], io["gwT"].rearrange("(k p) n -> p k n", p=P)).then_inc(gw_in, 16)
                sp.wait_ge(zeroed, 1)
                for n in range(CAP // P):
                    rows = slice(T + n * P, T + (n + 1) * P)
                    sp.dma_start(io["xn_rows"][rows, :], zero).then_inc(zero_out, 16)
                    sp.dma_start(io["out"][rows, :], zero).then_inc(zero_out, 16)
                sp.wait_ge(zero_out, 32 * (CAP // P))

                def step(t, d):
                    if live(t) and d == 0:
                        b = t // TB
                        need(sp, w_lo, b)
                        sp.dma_start(raw[:, :], io["sh_guT"][bass.ds(b * P, P), :]).then_inc(w_in, 16)
                    u = t - 7
                    if live(u):
                        sp.wait_ge(lg.ok, u + 1)
                        sp.dma_start(io["xn_rows"][bass.ds(u * P, P), :], lg.xn[:, (d + 1) % 2]).then_inc(rows_out[(d + 1) % 2], 16)
                        sp.wait_ge(s["g_lo"], u + 1)
                        sp.dma_start(io["xt_tiles"][u, :, :], gT[:, (d + 1) % 2].rearrange("p q k n -> p (q k n)")) \
                            .then_inc(gt_out[(d + 1) % 2], 16)
                run(sp, step)
                for n in range(2):
                    sp.wait_ge(rows_out[n], 8 * NT)
                    sp.wait_ge(gt_out[n], 8 * NT)

            @block.gpsimd
            def _(pool):
                pool.memset(zero, 0.0).then_inc(zeroed, 1)

                def step(t, d):
                    u = t + 3
                    if live(u):
                        ln.inverse_root(pool, g, u, (d + 3) % 4)
                    u, q = t - 6, (d + 2) % 4
                    if live(u):
                        lg.inverse_root(pool, g, u, q)
                    if live(u) and not past(t, 1):
                        need(pool, rows_out[q % 2], 16 * (u // 2))
                        need(pool, s["g_tr"], u - 1)
                        pool.wait_ge(lg.root, u + 1)
                        pool.tensor_tensor(lg.xn[:, q % 2], g.x[:, u, :], lg.mv[:, q, 0:1].to_broadcast([P, D]),
                                           ALU.subtract).then_inc(centred, 1)
                        pool.wait_ge(centred, u + 1)
                        pool.tensor_tensor(lg.xn[:, q % 2], lg.xn[:, q % 2], lg.rstd[:, q].to_broadcast([P, D]),
                                           ALU.mult).then_inc(lg.ok, 1)
                    if live(t) and d == 1:
                        b = t // TB
                        pool.wait_ge(w_in, 16 * (b + 1))
                        pool.tensor_tensor(raw[:, :], raw[:, :], g.ws[:, :].to_broadcast([P, IS]), ALU.mult).then_inc(w_scaled, 1)
                        pool.wait_ge(w_scaled, b + 1)
                        pool.tensor_tensor(g.wgu[:, b, 0, :], raw[:, :], g.one[:, :].to_broadcast([P, IS]), ALU.mult).then_inc(w_hi, 1)
                        pool.wait_ge(w_hi, b + 1)
                        pool.tensor_tensor(g.wgu[:, b, 1, :], raw[:, :], g.wgu[:, b, 0, :], ALU.subtract).then_inc(w_lo, 1)
                    if live(t) and live(t + 1) and d == TB - 1:
                        b = t // TB
                        for c in range(KC):
                            pool.wait_ge(c4["s_mm"], KC * t + c + 1)
                            block_keys(pool, g, b + 1, c)
                        pool.wait_ge(g.keys_ok, HC * KC * (b + 2))
                run(pool, step)

            @block.vector
            def _(dve):
                def maximum(u, d, c):
                    dve.wait_ge(c4["s_mm"], KC * u + c + 1)
                    need(dve, c4["exp"], KC * (u - 2) + c + 1)
                    dve.tensor_reduce(nmax[:, d % 2, c], ps_s[c % 2][:, :, :], AX.X, ALU.max,
                                      negate=True).then_inc(c4["max"], 1)

                def prob_low(u, c):
                    dve.wait_ge(c4["p_hi"], KC * u + c + 1)
                    dve.tensor_tensor(pT[0:J, c, 1], ps_p[c % 2][0:J], pT[0:J, c, 0], ALU.subtract).then_inc(c4["p_lo"], 1)

                def step(t, d):
                    if live(t):
                        maximum(t, d, 0)
                    u = t - 4
                    if live(u):
                        dve.wait_ge(s["y_mm"], u + 1)
                        dve.scalar_tensor_tensor(g.x[:, u, :], bank_y(u), 1 / WS, g.x[:, u, :], ALU.mult,
                                                 ALU.add).then_inc(s["x_new"], 1)
                    u, q = t - 1, (d + 1) % 2
                    if live(u):
                        prob_low(u, 0)
                        dve.wait_ge(c4["exp"], KC * u + KC)
                        need(dve, s["of"], u - 1)
                        dve.reciprocal(rinv[:, q, :], rsum[:, q, :]).then_inc(s["inv"], 1)
                    u, q = t - 2, d % 2
                    if live(u):
                        dve.wait_ge(c4["o_mm"], KC * u + KC)
                        dve.wait_ge(s["inv"], u + 1)
                        need(dve, s["o_tr"], u)
                        dve.tensor_tensor(of[:, :].rearrange("p (h o) -> p h o", h=HEADS),
                                          ps_o[:, :].rearrange("p (h o) -> p h o", h=HEADS),
                                          rinv[:, q, :].rearrange("p (h o) -> p h o", o=1).to_broadcast([P, HEADS, DH]),
                                          ALU.mult).then_inc(s["of"], 1)
                    u, q = t + 1, (d + 1) % 2
                    if live(u):
                        dve.wait_ge(s["xt_hi"], u + 1)
                        dve.tensor_tensor(xT[:, q, 1], ps_x[:, :, :], xT[:, q, 0], ALU.subtract).then_inc(s["xt_lo"], 1)
                    if live(t):
                        maximum(t, d, 1)
                    if live(t - 4):
                        dve.wait_ge(s["x_new"], t - 3)
                    if live(t - 4) or live(t - 5):
                        lg.before(dve, t - 4, lg.ok)
                    if live(t - 1):
                        prob_low(t - 1, 1)
                    u = t - 8
                    if live(u):
                        dve.wait_ge(s["l_mm"], u + 1)
                        dve.tensor_scalar(g.logits[:, u, :], ps_l, 1 / WS, None, ALU.mult).then_inc(s["l_ok"], 1)
                    if live(t - 4) or live(t - 5):
                        lg.statistics(dve, g, t - 4, d, waits=False)
                    if live(t + 2):
                        ln.apply(dve, g, t + 2, (d + 2) % 4, s["xt_mm"])
                    if live(t):
                        maximum(t, d, 2)
                    if live(t - 1):
                        prob_low(t - 1, 2)
                    if live(t + 5) or live(t + 4):
                        ln.before(dve, t + 5)
                    u, q = t - 2, d % 2
                    if live(u):
                        dve.wait_ge(s["o_hi"], u + 1)
                        dve.tensor_tensor(oT[:, q, 1], ps_x[:, :, :], oT[:, q, 0], ALU.subtract).then_inc(s["o_lo"], 1)
                    if live(t + 5) or live(t + 4):
                        ln.statistics(dve, g, t + 5, (d + 1) % 4, waits=False)
                    if live(t):
                        maximum(t, d, 3)
                    u, q = t + 1, (d + 1) % 2
                    if live(u):
                        dve.wait_ge(s["q_hi"], u + 1)
                        dve.scalar_tensor_tensor(qT[:, q, 1], ps_q[:, :, :], SC1 / WS, qT[:, q, 0], ALU.mult,
                                                 ALU.subtract).then_inc(s["q_lo"], 1)
                    u, q = t - 7, (d + 1) % 2
                    if live(u):
                        dve.wait_ge(s["g_hi"], u + 1)
                        dve.tensor_tensor(gT[:, q, 1], bank_g(t)[:, :, :], gT[:, q, 0], ALU.subtract).then_inc(s["g_lo"], 1)
                    if live(t - 1):
                        prob_low(t - 1, 3)
                    u, q = t - 6, (d + 2) % 4
                    if live(u) and past(t, 1):
                        dve.wait_ge(lg.ok, u)
                        need(dve, rows_out[q % 2], 16 * (u // 2))
                        lg.apply(dve, g, u, q, s["g_tr"])
                    if isinstance(t, int) and t == 2:
                        dve.wait_ge(gw_hi, 1)
                        dve.scalar_tensor_tensor(gws[:, 1], gwf[:, :, :], WS, gws[:, 0], ALU.mult,
                                                 ALU.subtract).then_inc(gw_lo, 1)
                run(dve, step)

            @block.scalar
            def _(act):
                def prob_high(u, c):
                    act.wait_ge(c4["p_mm"], KC * u + c + 1)
                    need(act, c4["o_mm"], KC * (u - 1) + c + 1)
                    act.activation(pT[0:J, c, 0], ps_p[c % 2][0:J], ACT.Copy).then_inc(c4["p_hi"], 1)

                def exps(u, d, c):
                    act.wait_ge(c4["max"], KC * u + c + 1)
                    need(act, s["inv"], u - 1)
                    need(act, c4["p_mm"], KC * (u - 1) + c + 1)
                    for h in range(HC):
                        n = c * HC + h
                        last = act.activation(prob[:, c, h, :], ps_s[c % 2][:, h, :], ACT.Exp, bias=nmax[:, d % 2, c, h:h + 1],
                                              accum_out=rsum[:, d % 2, n:n + 1])
                    last.then_inc(c4["exp"], 1)

                def step(t, d):
                    for c in range(KC):
                        u, q = t + 1, (d + 1) % 2
                        if c == 3 and live(u):
                            act.wait_ge(s["q_mm"], u + 1)
                            need(act, c4["s_mm"], KC * (u - 1))
                            act.activation(qT[:, q, 0], ps_q[:, :, :], ACT.Copy, scale=SC1 / WS).then_inc(s["q_hi"], 1)
                        u, q = t - 7, (d + 1) % 2
                        if c == 3 and live(u):
                            act.wait_ge(s["g_tr"], u + 1)
                            need(act, s["l_mm"], u - 1)
                            need(act, gt_out[q], 16 * (u // 2))
                            act.activation(gT[:, q, 0], bank_g(t)[:, :, :], ACT.Copy).then_inc(s["g_hi"], 1)
                        if live(t - 1):
                            prob_high(t - 1, c)
                        u, q = t - 2, d % 2
                        if c == 2 and live(u):
                            act.wait_ge(s["o_tr"], u + 1)
                            need(act, s["y_mm"], u - 1)
                            act.activation(oT[:, q, 0], ps_x[:, :, :], ACT.Copy).then_inc(s["o_hi"], 1)
                        if live(t):
                            exps(t, d, c)
                        u, q = t + 1, (d + 1) % 2
                        if c == 0 and live(u):
                            act.wait_ge(s["xt_mm"], u + 1)
                            need(act, s["q_mm"], u - 1)
                            act.activation(xT[:, q, 0], ps_x[:, :, :], ACT.Copy).then_inc(s["xt_hi"], 1)
                    if isinstance(t, int) and t == NT + 1:
                        act.wait_ge(g.keys_ok, B * KC * HC)
                        tokens(act, g, io, 0, 0, xs_in)
                    if isinstance(t, int) and t == 1:
                        act.wait_ge(gw_in, 16)
                        act.activation(gws[:, 0], gwf[:, :, :], ACT.Copy, scale=WS).then_inc(gw_hi, 1)
                run(act, step)
                act.wait_ge(xs_in, 16 * TB)

            @block.tensor
            def _(pe):
                def scores(u, d, c):
                    if c == 0:
                        pe.wait_ge(s["q_lo"], u + 1)
                    if d == 0:
                        pe.wait_ge(g.keys_ok, KC * HC * (u // TB) + HC * c + HC)
                    need(pe, c4["exp"], KC * u + c - 1)
                    matmuls(pe, ps_s[c % 2][:, :, :], lambda a, _: qT[:, d % 2, a, c, :], lambda a, _: g.kbd[:, a, c, :, :],
                            ks=(0,)).then_inc(c4["s_mm"], 1)

                def prob_transposed(u, c):
                    pe.wait_ge(c4["exp"], KC * u + c + 1)
                    need(pe, c4["p_lo"], KC * u + c - 1)
                    for h in range(HC):
                        last = pe.transpose(ps_p[c % 2][0:J, h, :], prob[:, c, h, :], g.ident[:, :])
                    last.then_inc(c4["p_mm"], 1)

                def outputs(u, c):
                    if c == 0:
                        need(pe, s["of"], u)
                    pe.wait_ge(c4["p_lo"], KC * u + c + 1)
                    for h in range(HC):
                        cols = slice((c * HC + h) * DH, (c * HC + h + 1) * DH)
                        for n, (a, b) in enumerate(((0, 0), (0, 1), (1, 0))):
                            last = pe.matmul(ps_o[:, cols], pT[0:J, c, a, h, :], g.v1[0:J, b, u // TB, cols],
                                             start=n == 0, stop=n == 2)
                    last.then_inc(c4["o_mm"], 1)

                def transposed(to, src):
                    for k in range(KC):
                        last = pe.transpose(to[:, k, :], src[:, k * P:(k + 1) * P], g.ident[:, :])
                    return last

                def queries(u, d, mms):
                    for mm in mms:
                        last = matmuls(pe, ps_q[:, mm, :], lambda a, k: g.wq1[:, a, k, mm * P:(mm + 1) * P],
                                       lambda a, k: xT[:, d % 2, a, k, :])
                    return last

                def product(u, d, ks):
                    for k in ks:
                        for n, (a, b) in enumerate(PASSES):
                            last = pe.matmul(bank_y(u), oT[:, d % 2, a, k, :], g.wo1[:, b, k, :],
                                             start=k == 0 and n == 0, stop=k == KC - 1 and n == 2)
                    return last

                def gate_transposed(t, d):
                    u = t - 7
                    if live(u):
                        pe.wait_ge(lg.ok, u + 1)
                        if past(t, 2):
                            pe.wait_ge(s["g_lo"], u - 1)
                        else:
                            pe.wait_ge(s["o_lo"], min(t - 1, NT) if isinstance(t, int) else t - 1)
                            need(pe, s["l_ok"], t - 7)
                        transposed(bank_g(t), lg.xn[:, (d + 1) % 2]).then_inc(s["g_tr"], 1)

                def step(t, d):
                    if past(t, 2):
                        gate_transposed(t, d)
                    if live(t):
                        scores(t, d, 0)
                    if live(t - 1):
                        prob_transposed(t - 1, 0)
                    if live(t - 2):
                        outputs(t - 2, 3)
                    u = t + 1
                    if live(u):
                        pe.wait_ge(ln.ok, u + 1)
                        need(pe, s["xt_lo"], u)
                        need(pe, s["o_lo"], t - 2)
                        need(pe, s["g_lo"], t - 7)
                        transposed(ps_x, ln.xn[:, (d + 1) % 2]).then_inc(s["xt_mm"], 1)
                    u = t - 3
                    if live(u):
                        pe.wait_ge(s["o_lo"], u + 1)
                        if not past(t, 1):
                            need(pe, s["x_new"], u)
                        product(u, d + 1, (0, 1))
                    if live(t):
                        scores(t, d, 1)
                    if live(t - 1):
                        prob_transposed(t - 1, 1)
                    u = t - 8
                    if live(u):
                        pe.wait_ge(s["g_lo"], u + 1)
                        pe.wait_ge(s["xt_lo"], min(t + 2, NT) if isinstance(t, int) else t + 2)
                        need(pe, s["l_ok"], u)
                        if isinstance(t, int):
                            pe.wait_ge(gw_lo, 1)
                        if past(t, 0):
                            pe.wait_ge(s["o_lo"], min(t - 2, NT))
                        matmuls(pe, ps_l, lambda a, k: gT[:, d % 2, a, k, :], lambda a, k: gws[:, a, k, :]).then_inc(s["l_mm"], 1)
                    u = t + 1
                    if live(u):
                        pe.wait_ge(s["xt_lo"], u + 1)
                        need(pe, s["q_lo"], u)
                        queries(u, d + 1, (0, 1))
                    if live(t - 1):
                        outputs(t - 1, 0)
                    if live(t):
                        scores(t, d, 2)
                    if live(t - 1):
                        prob_transposed(t - 1, 2)
                        outputs(t - 1, 1)
                    u = t - 2
                    if live(u):
                        pe.wait_ge(s["of"], u + 1)
                        need(pe, s["xt_lo"], min(t + 2, NT) if isinstance(t, int) else t + 2)
                        need(pe, s["l_ok"], t - 7)
                        transposed(ps_x, of).then_inc(s["o_tr"], 1)
                    u = t + 1
                    if live(u):
                        queries(u, d + 1, (2, 3)).then_inc(s["q_mm"], 1)
                    if not past(t, 2):
                        gate_transposed(t, d)
                    if live(t):
                        scores(t, d, 3)
                    if live(t - 1):
                        prob_transposed(t - 1, 3)
                        outputs(t - 1, 2)
                    u = t - 3
                    if live(u):
                        product(u, d + 1, (2, 3)).then_inc(s["y_mm"], 1)
                run(pe, step)


TOPK = 4
TOP_P = 0.75
JITTER2 = 0.2
BIG = 1e30
OFF = float(1 << 20)


class Route:

    def __init__(self, m, g):
        A = lambda name: m.sb(name, [P, NT, E])
        V = lambda name: m.sb(name, [P, NT, 1])
        sm, alive, absl, rev, eq, pr, diff, fac, ex, keep = (
            A(n) for n in ("sm", "alive", "absl", "rev", "eq", "pr", "diff", "fac", "ex", "keep"))
        oh = [A(f"oh{k}") for k in range(TOPK)]
        rw, sel, pos, kept, wgt, slot = (A(n) for n in ("rw", "sel", "pos", "kept", "wgt", "slot"))
        cum0, cum1 = sm, absl
        thr = [V(f"thr{k}") for k in range(TOPK)]
        mult = [V(f"mult{k}") for k in range(TOPK)]
        mx, athr, z, z8, csum, valid, rsum, sd, sk = (
            V(n) for n in ("mx", "athr", "z", "z8", "csum", "valid", "rsum", "sd", "sk"))
        pk = [V(f"pk{k}") for k in range(1, TOPK)]
        full = m.sb("full", [P, NT, E + 1])
        selb = m.sb("selb", [P, NT, E], bf16)
        tri = m.sb("tri", [P, P], bf16)
        one = m.sb("one", [P, P], bf16)
        erow = m.sb("erow", [P, NT, E], mybir.dt.int32)
        token = m.sb("token", [P, NT, 1], mybir.dt.int32)
        blank = m.sb("blank", [P, E * CAP // P, 2], mybir.dt.int32)
        load = m.sb("load", [P, NT, TOPK, 2], u32)
        index = m.sb("index", [P, NT, TOPK], u32)
        counts = m.sb("counts", [P, 2, NT, E])
        done = m.sem("done")
        consts, exp_in, exp_out, sel_ok, count_mm, counted, lists, blank_out, listed = (
            m.sem(n) for n in ("consts", "exp_in", "exp_out", "sel_ok", "count_mm", "counted", "lists", "blank_out", "listed"))
        wide = lambda v: v[:, :, 0:1].to_broadcast([P, NT, E])

        def constants(pool, io):
            pool.iota(erow[:, :, :], pattern=[[0, NT], [1, E]], base=0, channel_multiplier=0).then_inc(consts, 1)
            pool.iota(token[:, :, :], pattern=[[P, NT], [0, 1]], base=0, channel_multiplier=1).then_inc(consts, 1)
            pool.iota(blank[:, :, 0:1].rearrange("p (e n) c -> p e n c", e=E),
                      pattern=[[0, E], [P, CAP // P], [0, 1]], base=T, channel_multiplier=1).then_inc(consts, 1)
            pool.memset(blank[:, :, 1:2], 0).then_inc(consts, 1)
            pool.memset(one[:, :], 1.0).then_inc(consts, 1)
            pool.wait_ge(consts, 5)
            pool.affine_select(out=tri[:, :], in_=one[:, :], compare_op=ALU.is_ge, fill=0.0, base=0,
                               pattern=[[1, P]], channel_multiplier=-1).then_inc(consts, 1)
            pool.wait_ge(consts, 6)
            pool.dma_start(io["lists"].rearrange("(n p) c -> p n c", p=P), blank[:, :, :].bitcast(u32)).then_inc(blank_out, 16)
            pool.wait_ge(blank_out, 16)

        def scatter(pool, io):
            pool.wait_ge(lists, 1)
            for t in range(NT):
                for k in range(TOPK):
                    pool.indirect_dma_start(
                        out=io["lists"], out_offset=bass.IndirectOffsetOnAxis(ap=index[:, t, k:k + 1], axis=0),
                        in_=load[:, t, k, :], in_offset=None, bounds_check=E * CAP - 1, oob_is_err=False) \
                        .then_inc(listed, 16)
            pool.wait_ge(listed, 16 * NT * TOPK)

        def exponentials(act, unit):
            if unit % 2 == 1 and unit < 2 * TOPK:
                act.wait_ge(exp_in, unit // 2 + 1)
                act.activation(ex[:, :, :], diff[:, :, :], ACT.Exp, scale=-1.0).then_inc(exp_out, 1)
            if unit == 2 * TOPK:
                for k in range(1, TOPK):
                    act.wait_ge(exp_in, TOPK + k)
                    act.activation(pk[k - 1][:, :, :], pk[k - 1][:, :, :], ACT.Exp).then_inc(exp_out, 1)
            if unit == 2 * TOPK + 5:
                act.wait_ge(exp_in, 2 * TOPK)
                act.activation(full[:, :, :], full[:, :, :], ACT.Exp).then_inc(exp_out, 1)

        def count(pe, bank):
            pe.wait_ge(consts, 6)
            pe.wait_ge(sel_ok, 1)
            pe.matmul(bank[:, 0], tri[:, :], selb[:, :, :], start=True, stop=True)
            pe.matmul(bank[:, 1], one[:, :], selb[:, :, :], start=True, stop=True).then_inc(count_mm, 1)

        def counted_wait(pe):
            pe.wait_ge(counted, 1)

        def pieces(dve, bank):
            chained = [0]

            def link(ins):
                chained[0] += 1
                ins.then_inc(done, 1)
                dve.wait_ge(done, chained[0])

            lg = g.logits[:, :, 0:E]
            tt, ts, stt = dve.tensor_tensor, dve.tensor_scalar, dve.scalar_tensor_tensor
            reduce = dve.tensor_reduce
            dve.wait_ge(consts, 6)
            link(dve.memset(alive[:, :, :], 1.0))
            link(dve.tensor_copy(sm[:, :, :], lg))
            link(stt(absl[:, :, :], lg, -1.0, lg, ALU.mult, ALU.max))
            link(ts(rev[:, :, :], erow[:, :, :], -1.0, float(E), ALU.mult, ALU.add))
            for k in range(TOPK):
                link(reduce(thr[k][:, :, :], sm[:, :, :], AX.X, ALU.max))
                link(tt(eq[:, :, :], sm[:, :, :], wide(thr[k]), ALU.is_equal))
                link(tt(pr[:, :, :], eq[:, :, :], rev[:, :, :], ALU.mult))
                link(reduce(mx[:, :, :], pr[:, :, :], AX.X, ALU.max))
                link(tt(oh[k][:, :, :], pr[:, :, :], wide(mx), ALU.is_equal))
                link(tt(fac[:, :, :], wide(thr[k]), lg, ALU.subtract))
                link(stt(athr[:, :, :], thr[k][:, :, :], -1.0, thr[k][:, :, :], ALU.mult, ALU.max))
                link(tt(keep[:, :, :], absl[:, :, :], wide(athr), ALU.max))
                link(stt(keep[:, :, :], keep[:, :, :], JITTER2, fac[:, :, :], ALU.mult, ALU.is_ge))
                link(tt(keep[:, :, :], keep[:, :, :], alive[:, :, :], ALU.mult))
                ts(diff[:, :, :], fac[:, :, :], 0.0, None, ALU.max).then_inc(exp_in, 1)
                yield
                dve.wait_ge(exp_out, k + 1)
                if k == 0:
                    link(reduce(z8[:, :, :], ex[:, :, :], AX.X, ALU.add))
                link(tt(keep[:, :, :], keep[:, :, :], ex[:, :, :], ALU.mult))
                link(reduce(z[:, :, :], keep[:, :, :], AX.X, ALU.add))
                link(dve.reciprocal(mult[k][:, :, :], z[:, :, :]))
                link(tt(alive[:, :, :], alive[:, :, :], oh[k][:, :, :], ALU.subtract))
                link(stt(sm[:, :, :], oh[k][:, :, :], -BIG, sm[:, :, :], ALU.mult, ALU.add))
                if k < TOPK - 1:
                    yield
            for k in range(1, TOPK):
                tt(pk[k - 1][:, :, :], thr[k][:, :, :], thr[0][:, :, :], ALU.subtract).then_inc(exp_in, 1)
            yield
            link(dve.reciprocal(z8[:, :, :], z8[:, :, :]))
            link(dve.tensor_copy(csum[:, :, :], z8[:, :, :]))
            link(tt(rw[:, :, :], oh[0][:, :, :], wide(mult[0]), ALU.mult))
            link(dve.tensor_copy(rsum[:, :, :], mult[0][:, :, :]))
            link(dve.tensor_copy(sel[:, :, :], oh[0][:, :, :]))
            for k in range(1, TOPK):
                link(ts(valid[:, :, :], csum[:, :, :], TOP_P, None, ALU.is_lt))
                dve.wait_ge(exp_out, TOPK + k)
                link(tt(pk[k - 1][:, :, :], pk[k - 1][:, :, :], z8[:, :, :], ALU.mult))
                link(tt(csum[:, :, :], csum[:, :, :], pk[k - 1][:, :, :], ALU.add))
                link(tt(mult[k][:, :, :], mult[k][:, :, :], valid[:, :, :], ALU.mult))
                link(tt(rsum[:, :, :], rsum[:, :, :], mult[k][:, :, :], ALU.add))
                link(tt(eq[:, :, :], oh[k][:, :, :], wide(mult[k]), ALU.mult))
                link(tt(rw[:, :, :], rw[:, :, :], eq[:, :, :], ALU.add))
                link(tt(eq[:, :, :], oh[k][:, :, :], wide(valid), ALU.mult))
                link(tt(sel[:, :, :], sel[:, :, :], eq[:, :, :], ALU.add))
                if k < TOPK - 1:
                    yield
            dve.tensor_copy(selb[:, :, :], sel[:, :, :]).then_inc(sel_ok, 1)
            link(dve.reciprocal(rsum[:, :, :], rsum[:, :, :]))
            link(tt(rw[:, :, :], rw[:, :, :], wide(rsum), ALU.mult))
            yield
            dve.wait_ge(count_mm, 1)
            dve.tensor_copy(counts[:, :, :, :], bank).then_inc(counted, 1)
            dve.wait_ge(counted, 1)
            link(dve.tensor_copy(cum0[:, :, :], counts[:, 1, :, :]))
            a, b, n = cum0, cum1, 1
            while n < NT:
                link(dve.tensor_copy(b[:, 0:n, :], a[:, 0:n, :]))
                link(tt(b[:, n:NT, :], a[:, n:NT, :], a[:, 0:NT - n, :], ALU.add))
                a, b, n = b, a, 2 * n
            link(tt(pos[:, :, :], a[:, :, :], counts[:, 1, :, :], ALU.subtract))
            link(tt(pos[:, :, :], pos[:, :, :], counts[:, 0, :, :], ALU.add))
            link(stt(kept[:, :, :], pos[:, :, :], float(CAP), sel[:, :, :], ALU.is_le, ALU.mult))
            yield
            link(ts(eq[:, :, :], kept[:, :, :], BIG, -BIG, ALU.mult, ALU.add))
            link(tt(full[:, :, 0:E], lg, eq[:, :, :], ALU.add))
            link(dve.tensor_copy(full[:, :, E:E + 1], g.logits[:, :, E:E + 1]))
            link(reduce(mx[:, :, :], full[:, :, :], AX.X, ALU.max))
            tt(full[:, :, :], full[:, :, :], mx[:, :, 0:1].to_broadcast([P, NT, E + 1]), ALU.subtract).then_inc(exp_in, 1)
            yield
            dve.wait_ge(exp_out, 2 * TOPK)
            link(reduce(z[:, :, :], full[:, :, :], AX.X, ALU.add))
            link(reduce(sd[:, :, :], full[:, :, 0:E], AX.X, ALU.add))
            link(dve.reciprocal(z[:, :, :], z[:, :, :]))
            link(ts(z[:, :, :], z[:, :, :], 1 / (WS * HS), None, ALU.mult))
            link(tt(g.gsh[:, :, :], full[:, :, E:E + 1], z[:, :, :], ALU.mult))
            link(tt(sd[:, :, :], sd[:, :, :], z[:, :, :], ALU.mult))
            link(tt(wgt[:, :, :], rw[:, :, :], wide(sd), ALU.mult))
            link(tt(wgt[:, :, :], wgt[:, :, :], kept[:, :, :], ALU.mult))
            yield
            link(stt(slot[:, :, :], erow[:, :, :], float(CAP), pos[:, :, :], ALU.mult, ALU.add))
            link(ts(slot[:, :, :], slot[:, :, :], -1.0 - OFF, None, ALU.add))
            link(tt(slot[:, :, :], slot[:, :, :], kept[:, :, :], ALU.mult))
            for k in range(TOPK):
                if k == TOPK // 2:
                    yield
                link(tt(eq[:, :, :], oh[k][:, :, :], slot[:, :, :], ALU.mult))
                link(reduce(sk[:, :, :], eq[:, :, :], AX.X, ALU.add))
                link(ts(index[:, :, k:k + 1], sk[:, :, :], OFF, None, ALU.add))
                link(tt(eq[:, :, :], oh[k][:, :, :], wgt[:, :, :], ALU.mult))
                link(reduce(load[:, :, k, 1:2].bitcast(f32), eq[:, :, :], AX.X, ALU.add))
                link(dve.tensor_copy(load[:, :, k, 0:1], token[:, :, :]))
            dve.tensor_copy(sk[:, :, :], sk[:, :, :]).then_inc(lists, 1)
            yield

        self.constants, self.scatter, self.exponentials = constants, scatter, exponentials
        self.count, self.counted_wait, self.pieces = count, counted_wait, pieces


def expert_weights(sp, g, io, e, c):
    to, done = g.ex_raw[:, c], g.ex_w_in[c]
    sp.dma_start(to[:, 0:KC * IE].rearrange("p (k n) -> p k n", k=KC),
                 io["dyn_gT"][e, :, :].rearrange("(k p) n -> p k n", p=P)).then_inc(done, 16)
    sp.dma_start(to[:, KC * IE:2 * KC * IE].rearrange("p (k n) -> p k n", k=KC),
                 io["dyn_uT"][e, :, :].rearrange("(k p) n -> p k n", p=P)).then_inc(done, 16)
    sp.dma_start(to[:, 2 * KC * IE:WN].rearrange("p (k n) -> p k n", k=IE // P),
                 io["dyn_dT"][e, :, :].rearrange("(k p) n -> p k n", p=P)).then_inc(done, 16)


def gather_rows(pool, g, io, e):
    for n in range(CT):
        pool.indirect_dma_start(
            out=g.ex_rows[:, e % 2, n, :], out_offset=None, in_=io["xn_rows"],
            in_offset=bass.IndirectOffsetOnAxis(ap=g.ex_slots[:, e * CT + n, 0:1], axis=0)).then_inc(g.ex_x_in[e % 2], 16)


def shared(nc, g, io):
    NC = IS // P
    with ExitStack() as ctx:
        m = Scope(nc, ctx, "shared")
        xT = g.xs
        sg = m.sb("sg", [P, 2, S])
        hf = m.sb("hf", [P, 2, S])
        hid = m.sb("hid", [P, 2, 2, S], f16)
        res = g.res
        gsh = m.sb("gsh", [P, NT, 1])
        wd = m.sb("wd", [P, 2, NC, D], f16)
        wd_raw = m.sb("wd_raw", [P, NC, D])
        g.gsh = gsh
        ps_g = [m.ps(f"ps_g{i}", [P, S]) for i in range(2)]
        ps_u = [m.ps(f"ps_u{i}", [P, S]) for i in range(2)]
        ps_y = [m.ps(f"ps_y{i}", [P, D]) for i in range(TB)]
        s = {n: m.sem(n) for n in ("g_mm", "u_mm", "silu", "hf", "h_hi", "h_lo", "d_mm", "y_ok", "warm", "wd_hi", "wd_lo", "kept", "w0_hi", "w0_lo")}
        wd_in = [m.sem(f"wd_in{n}") for n in range(2)]
        x_in = [m.sem(f"x_in{n}") for n in range(2)]
        out_done, slots_in = g.out_done, m.sem("slots_in")
        routing = Route(m, g)
        bank = ps_u[0][:, :].rearrange("p (a t e) -> p a t e", a=2, e=E)
        BORROW = NC + 4
        kept = wd_raw[:, 0:TB]

        def ok(b):
            return not isinstance(b, int) or 0 <= b < B

        with nc.Block() as block:

            @block.sync
            def _(sp):
                def step(b, d):
                    if ok(b + 1) and not (isinstance(b, int) and b < 0):
                        c = (d + 1) % 2
                        need(sp, s["u_mm"], NC * b)
                        tokens(sp, g, io, b + 1, c, x_in[c])
                    if isinstance(b, int) and b == -1:
                        down_rows = io["sh_dT"].rearrange("(c p) n -> p c n", p=P)
                        for n in range(2):
                            cs = slice(n * NC // 2, (n + 1) * NC // 2)
                            sp.dma_start(wd_raw[:, cs], down_rows[:, cs]).then_inc(wd_in[n], 16)
                    if ok(b - 1):
                        for i in range(TB):
                            sp.wait_ge(s["y_ok"], TB * (b - 1) + i + 1)
                            sp.dma_start(io["out"][bass.ds(((b - 1) * TB + i) * P, P), :], res[:, i]).then_inc(out_done, 16)
                    if isinstance(b, int) and b == B - 2:
                        for e in range(2):
                            expert_weights(sp, g, io, e, e)
                pipeline(sp, step, 1, 1, B, 2)

            @block.gpsimd
            def _(pool):
                routing.constants(pool, io)
                routing.scatter(pool, io)
                pool.dma_start(g.ex_slots[:, :, :], io["lists"].rearrange("(n p) c -> p n c", p=P)).then_inc(slots_in, 16)
                pool.wait_ge(slots_in, 16)
                pool.wait_ge(s["y_ok"], NT - 2 * TB)
                for e in range(2):
                    gather_rows(pool, g, io, e)

            @block.scalar
            def _(act):
                act.activation(sg[:, 0, 0:1], g.half[:, 0:1], ACT.Silu).then_inc(s["warm"], 1)
                act.wait_ge(s["warm"], 1)

                def step(b, d):
                    for c in range(NC):
                        v = NC * b + c
                        act.wait_ge(s["g_mm"], v + 1)
                        need(act, s["hf"], v - 1)
                        act.activation(sg[:, c % 2], ps_g[c % 2][:, :], ACT.Silu, scale=1 / WS).then_inc(s["silu"], 1)
                        if isinstance(b, int) and b < 2:
                            routing.exponentials(act, v)
                        act.wait_ge(s["hf"], v + 1)
                        need(act, s["d_mm"], v - 1)
                        act.activation(hid[:, c % 2, 0], hf[:, c % 2], ACT.Copy).then_inc(s["h_hi"], 1)
                        if isinstance(b, int) and b == 0:
                            act.wait_ge(wd_in[2 * c // NC], 16)
                            act.activation(wd[:, 0, c], wd_raw[:, c], ACT.Copy, scale=WS).then_inc(s["wd_hi"], 1)
                        if isinstance(b, int) and b == B - 1 and c < 3:
                            act.wait_ge(g.ex_w_in[0], 48)
                            act.activation(g.ex_w0[:, 0, PARTS[c]], g.ex_raw[:, 0, PARTS[c]], ACT.Copy, scale=WS).then_inc(s["w0_hi"], 1)
                        if isinstance(b, int) and b == 1 and c == 0:
                            act.wait_ge(s["d_mm"], NC)
                            act.wait_ge(s["wd_lo"], NC)
                            for i in range(TB):
                                act.activation(kept[:, i], ps_y[i][:, :], ACT.Copy).then_inc(s["kept"], 1)
                pipeline(act, step, 0, 0, B, 2, tail=1)

            @block.vector
            def _(dve):
                pieces = routing.pieces(dve, bank)

                def step(b, d):
                    for c in range(NC):
                        if ok(b):
                            v = NC * b + c
                            dve.wait_ge(s["silu"], v + 1)
                            dve.wait_ge(s["u_mm"], v + 1)
                            need(dve, s["h_hi"], v - 1)
                            need(dve, s["h_lo"], v - 1)
                            dve.scalar_tensor_tensor(hf[:, c % 2], ps_u[c % 2][:, :], HS / WS, sg[:, c % 2], ALU.mult,
                                                     ALU.mult).then_inc(s["hf"], 1)
                            dve.wait_ge(s["h_hi"], v + 1)
                            dve.tensor_tensor(hid[:, c % 2, 1], hf[:, c % 2], hid[:, c % 2, 0], ALU.subtract).then_inc(s["h_lo"], 1)
                            if isinstance(b, int) and b == 0:
                                dve.wait_ge(s["wd_hi"], c + 1)
                                dve.scalar_tensor_tensor(wd[:, 1, c], wd_raw[:, c], WS, wd[:, 0, c], ALU.mult,
                                                         ALU.subtract).then_inc(s["wd_lo"], 1)
                            if isinstance(b, int) and b == B - 1 and c < 3:
                                dve.wait_ge(s["w0_hi"], c + 1)
                                dve.scalar_tensor_tensor(g.ex_w0[:, 1, PARTS[c]], g.ex_raw[:, 0, PARTS[c]], WS,
                                                         g.ex_w0[:, 0, PARTS[c]], ALU.mult, ALU.subtract).then_inc(s["w0_lo"], 1)
                            if isinstance(b, int) and b < 2:
                                next(pieces)
                        if isinstance(b, int) and b == 1:
                            if c == NC - 1:
                                dve.wait_ge(s["kept"], TB)
                                for i in range(TB):
                                    dve.scalar_tensor_tensor(res[:, i], kept[:, i], g.gsh[:, i, :], g.x[:, i, :],
                                                             ALU.mult, ALU.add).then_inc(s["y_ok"], 1)
                            continue
                        if c == 0 and ok(b - 1):
                            t0 = (b - 1) * TB
                            dve.wait_ge(s["d_mm"], NC * b)
                            need(dve, out_done, 16 * t0)
                            for i in range(TB):
                                dve.scalar_tensor_tensor(res[:, i], ps_y[i][:, :], g.gsh[:, t0 + i, :], g.x[:, t0 + i, :],
                                                         ALU.mult, ALU.add).then_inc(s["y_ok"], 1)
                pipeline(dve, step, 0, 1, B, 2, tail=1)

            @block.tensor
            def _(pe):
                def down(v, c):
                    pe.wait_ge(s["h_lo"], v + 1)
                    if isinstance(v, int) and v < NC:
                        pe.wait_ge(s["wd_lo"], c + 1)
                    for n, (a, b) in enumerate(PASSES):
                        for i in range(TB):
                            last = pe.matmul(ps_y[i][:, :], hid[:, c % 2, a, i * P:(i + 1) * P], wd[:, b, c, :],
                                             start=c == 0 and n == 0, stop=c == NC - 1 and n == 2)
                    last.then_inc(s["d_mm"], 1)

                def step(b, d):
                    for c in range(NC):
                        v = NC * b + c
                        if ok(b):
                            if c == 0:
                                need(pe, x_in[d % 2], 16 * TB * (b // 2 + d % 2))
                            if isinstance(b, int) and v == BORROW:
                                pe.wait_ge(s["hf"], v - 1)
                                routing.count(pe, bank)
                            need(pe, s["silu"], v - 1)
                            matmuls(pe, ps_g[c % 2][:, :], lambda a, k: g.wgu[:, k, a, c * P:(c + 1) * P],
                                    lambda a, k: xT[:, d % 2, a, k, :]).then_inc(s["g_mm"], 1)
                            if isinstance(b, int) and v == BORROW:
                                routing.counted_wait(pe)
                            need(pe, s["hf"], v - 1)
                            matmuls(pe, ps_u[c % 2][:, :], lambda a, k: g.wgu[:, KC + k, a, c * P:(c + 1) * P],
                                    lambda a, k: xT[:, d % 2, a, k, :]).then_inc(s["u_mm"], 1)
                        if c == 0 and ok(b - 1):
                            down(v - 1, NC - 1)
                        if c > 0 and ok(b):
                            if c == 1:
                                if isinstance(b, int) and b == 1:
                                    pe.wait_ge(s["kept"], TB)
                                else:
                                    need(pe, s["y_ok"], TB * b)
                            down(v - 1, c - 1)
                pipeline(pe, step, 0, 1, B, 2)


def experts(nc, g, io):
    HN = CAP // 2
    NI = IE // P
    with ExitStack() as ctx:
        m = Scope(nc, ctx, "experts")
        raw, xg, res, lst = g.ex_raw, g.ex_rows, g.ex_res, g.ex_slots
        w = [g.ex_w0, m.sb("w1", [P, 2, WN], f16)]
        xT = m.sb("xT", [P, 2, 2, KC, CAP], f16)
        sg = m.sb("sg", [P, 2, HN])
        hf = m.sb("hf", [P, 2, HN])
        hid = m.sb("hid", [P, 2, 2, NI, CAP], f16)
        ps_x = [m.ps(f"ps_x{i}", [P, KC, P]) for i in range(2)]
        ps_g = [m.ps(f"ps_g{i}", [P, HN]) for i in range(2)]
        ps_u = [m.ps(f"ps_u{i}", [P, HN]) for i in range(2)]
        ps_y = [m.ps(f"ps_y{i}", [P, D]) for i in range(2)]
        s = {n: m.sem(n) for n in ("w_hi", "w_lo", "xt_mm", "xt_hi", "xt_lo", "g_mm", "u_mm", "silu", "hf", "h_hi", "h_lo",
                                   "y_mm", "y_ok", "warm", "added")}
        w_in, x_in = g.ex_w_in, g.ex_x_in
        UNITS = [(h, i) for h in range(2) for i in range(NI)]

        def ok(e):
            return not isinstance(e, int) or 0 <= e < E

        with nc.Block() as block:

            @block.sync
            def _(sp):
                def step(e, d):
                    u = e + 2
                    if ok(u):
                        need(sp, s["w_hi"], 3 * (u - 2))
                        need(sp, s["w_lo"], 3 * (u - 2))
                        expert_weights(sp, g, io, u, d % 2)
                pipeline(sp, step, 0, 0, E - 2, 2)

            @block.gpsimd
            def _(pool):
                def step(e, d):
                    u = e + 2
                    if ok(u):
                        pool.wait_ge(s["xt_mm"], CT * (u - 1))
                        gather_rows(pool, g, io, u)
                    u = e - 1
                    if ok(u):
                        c = (d + 1) % 2
                        need(pool, s["added"], 16 * CT * u)
                        for n in range(CT):
                            pool.wait_ge(s["y_ok"], CT * u + n + 1)
                            pool.indirect_dma_start(
                                out=io["out"], out_offset=bass.IndirectOffsetOnAxis(ap=lst[:, u * CT + n, 0:1], axis=0),
                                in_=res[:, c, n, :], in_offset=None, compute_op=ALU.add).then_inc(s["added"], 16)
                pool.wait_ge(g.out_done, 16 * NT)
                for e in range(E + 1):
                    step(e, e % 2)
                pool.wait_ge(s["added"], 16 * CT * E)

            @block.scalar
            def _(act):
                act.activation(sg[:, 0, 0:1], g.half[:, 0:1], ACT.Silu).then_inc(s["warm"], 1)
                act.wait_ge(s["warm"], 1)

                def silu(u, n):
                    v = 4 * u + n
                    act.wait_ge(s["g_mm"], v + 1)
                    need(act, s["hf"], v - 1)
                    act.activation(sg[:, n % 2], ps_g[n % 2][:, :], ACT.Silu, scale=1 / WS).then_inc(s["silu"], 1)

                def hidden_high(u, d, n):
                    v = 4 * u + n
                    h, i = UNITS[n]
                    act.wait_ge(s["hf"], v + 1)
                    need(act, s["y_mm"], CT * (u - 1))
                    act.activation(hid[:, d % 2, 0, i, h * HN:(h + 1) * HN], hf[:, n % 2], ACT.Copy).then_inc(s["h_hi"], 1)

                def rows_high(u, c, n):
                    act.wait_ge(s["xt_mm"], CT * u + n + 1)
                    if n == 0:
                        need(act, s["u_mm"], 4 * (u - 1))
                    act.activation(xT[:, c, 0, :, n * P:(n + 1) * P], ps_x[n % 2][:, :, :], ACT.Copy).then_inc(s["xt_hi"], 1)

                def weights_high(u, c, n):
                    act.wait_ge(w_in[c], 48 * (u // 2 + 1))
                    if n == 0:
                        need(act, s["u_mm"], 4 * (u - 1))
                    if n == 2:
                        need(act, s["y_mm"], CT * (u - 1))
                    act.activation(w[c][:, 0, PARTS[n]], raw[:, c, PARTS[n]], ACT.Copy, scale=WS).then_inc(s["w_hi"], 1)

                def step(e, d):
                    after = (d + 1) % 2
                    for n in range(4):
                        if ok(e):
                            silu(e, n)
                        if n < 3 and ok(e + 1) and ok(e):
                            weights_high(e + 1, after, n)
                        if ok(e):
                            hidden_high(e, d, n)
                        u = e + 1
                        if ok(u):
                            rows_high(u, after, n)
                            if n == 3:
                                rows_high(u, after, 4)
                        u = e - 1
                        if n == 0 and ok(u):
                            for i in range(CT):
                                act.wait_ge(s["y_mm"], CT * u + i + 1)
                                if i == 0:
                                    need(act, s["added"], 16 * CT * (u - 1))
                                act.activation(res[:, after, i], ps_y[i % 2][:, :], ACT.Copy,
                                               scale=lst[:, u * CT + i, 1:2].bitcast(f32)).then_inc(s["y_ok"], 1)
                pipeline(act, step, 1, 1, E, 2)

            @block.vector
            def _(dve):
                def unit(u, d, n):
                    v = 4 * u + n
                    h, i = UNITS[n]
                    cols = slice(h * HN, (h + 1) * HN)
                    dve.wait_ge(s["silu"], v + 1)
                    dve.wait_ge(s["u_mm"], v + 1)
                    need(dve, s["h_hi"], v - 1)
                    need(dve, s["h_lo"], v - 1)
                    dve.scalar_tensor_tensor(hf[:, n % 2], ps_u[n % 2][:, :], HS / WS, sg[:, n % 2], ALU.mult,
                                             ALU.mult).then_inc(s["hf"], 1)
                    dve.wait_ge(s["h_hi"], v + 1)
                    dve.tensor_tensor(hid[:, d % 2, 1, i, cols], hf[:, n % 2], hid[:, d % 2, 0, i, cols],
                                      ALU.subtract).then_inc(s["h_lo"], 1)

                def rows_low(u, c, n):
                    dve.wait_ge(s["xt_hi"], CT * u + n + 1)
                    cols = slice(n * P, (n + 1) * P)
                    dve.tensor_tensor(xT[:, c, 1, :, cols], ps_x[n % 2][:, :, :], xT[:, c, 0, :, cols],
                                      ALU.subtract).then_inc(s["xt_lo"], 1)

                def weights_low(u, c, n):
                    dve.wait_ge(s["w_hi"], 3 * (u - 1) + n + 1)
                    dve.scalar_tensor_tensor(w[c][:, 1, PARTS[n]], raw[:, c, PARTS[n]], WS, w[c][:, 0, PARTS[n]], ALU.mult,
                                             ALU.subtract).then_inc(s["w_lo"], 1)

                def step(e, d):
                    after = (d + 1) % 2
                    for n in range(4):
                        if ok(e):
                            unit(e, d, n)
                        if ok(e + 1):
                            rows_low(e + 1, after, n)
                            if n < 3:
                                if ok(e):
                                    weights_low(e + 1, after, n)
                            else:
                                rows_low(e + 1, after, 4)
                pipeline(dve, step, 1, 0, E, 2)

            @block.tensor
            def _(pe):
                def unit(u, d, n):
                    v = 4 * u + n
                    h, i = UNITS[n]
                    c = d % 2
                    if n == 0:
                        need(pe, s["w_lo"], 3 * (u - 1) + 2)
                    for bank, sem, read, at in ((ps_g, "g_mm", "silu", 0), (ps_u, "u_mm", "hf", KC * IE)):
                        need(pe, s[read], v - 1)
                        if n % 2 == 0 and at == 0:
                            pe.wait_ge(s["xt_lo"], CT * u + (3 if h == 0 else CT))
                        matmuls(pe, bank[n % 2][:, :],
                                lambda a, k: w[c][:, a, at + k * IE + i * P:at + k * IE + (i + 1) * P],
                                lambda a, k: xT[:, c, a, k, h * HN:(h + 1) * HN]).then_inc(s[sem], 1)

                def rows_transposed(u, c, n):
                    if n == 0:
                        pe.wait_ge(x_in[c], 16 * CT * (u // 2 + 1))
                    need(pe, s["xt_lo"], CT * u + max(n - 1, 0))
                    for k in range(KC):
                        last = pe.transpose(ps_x[n % 2][:, k, :], xg[:, c, n, k * P:(k + 1) * P], g.ident[:, :])
                    last.then_inc(s["xt_mm"], 1)

                def step(e, d):
                    after = (d + 1) % 2
                    for n in range(4):
                        if ok(e):
                            unit(e, d, n)
                        if ok(e + 1):
                            rows_transposed(e + 1, after, n)
                            if n == 3:
                                rows_transposed(e + 1, after, 4)
                        u = e - 1
                        if n == 0 and ok(u):
                            for i in range(CT):
                                pe.wait_ge(s["h_lo"], 4 * u + 4)
                                need(pe, s["w_lo"], 3 * u)
                                need(pe, s["y_ok"], CT * u + max(i - 1, 0))
                                matmuls(pe, ps_y[i % 2][:, :], lambda a, j: hid[:, after, a, j, i * P:(i + 1) * P],
                                        lambda a, j: w[after][:, a, 2 * KC * IE + j * D:2 * KC * IE + (j + 1) * D],
                                        ks=range(NI)).then_inc(s["y_mm"], 1)
                pipeline(pe, step, 1, 1, E, 2)


class State:
    pass


def program(nc, io, out):
    Scope.semaphores = []
    with ExitStack() as ctx:
        m = Scope(nc, ctx, "program")
        g = State()
        g.x = m.sb("x", [P, NT, D])
        g.ident = m.sb("ident", [P, P])
        g.half = m.sb("half", [P, 1])
        g.round_c = m.sb("round_c", [P, 2])
        g.eps = m.sb("eps", [P, 1])
        g.one = m.sb("one", [P, 1])
        g.ws = m.sb("ws", [P, 1])
        g.logits = m.sb("logits", [P, NT, E + 1])
        g.wgu = m.sb("wgu", [P, 2 * KC, 2, IS], f16)
        g.xs = m.sb("xs", [P, 2, 2, KC, S], f16)
        g.k1 = g.xs[:, :, :, :, :].rearrange("p s q k n -> p (s q k n)")[:, 0:2 * KC * JB] \
            .rearrange("p (q k n) -> p q k n", q=2, k=KC)
        half = g.wgu[:, 0:KC].rearrange("p k q n -> p (k q n)"), g.wgu[:, KC:2 * KC].rearrange("p k q n -> p (k q n)")
        g.m0 = half[0][:, 0:2 * KC * JB].rearrange("p (q k n) -> p q k n", q=2, k=KC)
        g.v0 = half[1][:, 0:2 * B * D].rearrange("p (q b n) -> p q b n", q=2, b=B)
        g.x_in = [m.sem(f"x_in{n}") for n in range(3)]
        g.keys_ok = m.sem("keys_ok")
        io = dict(io, out=out)
        io["xn_rows"] = nc.dram_tensor("xn_rows", [T + CAP, D], f32, kind="Internal").ap()
        io["xt_tiles"] = nc.dram_tensor("xt_tiles", [NT, P, 2 * KC * P], f16, kind="Internal").ap()
        io["lists"] = nc.dram_tensor("lists", [E * CAP, 2], u32, kind="Internal").ap()
        with ExitStack() as actx:
            a = Scope(nc, actx, "att")
            g.simb = a.sb("simb", [P, JB])
            g.v1 = a.sb("v1", [P, 2, B, D], f16)
            g.wq1 = a.sb("wq1", [P, 2, KC, D], f16)
            g.wo1 = a.sb("wo1", [P, 2, KC, D], f16)
            g.qr = a.sb("qr", [P, KC, D], bf16)
            g.rs = a.sb("rs", [P, D])
            g.kbd = a.sb("kbd", [P, 2, KC, HC, J], f16)
            setup(nc, g, io)
            layer0(nc, g)
            attention1(nc, g, io)
        Scope.clear_semaphores(nc)
        place = g.x[:, :, :].rearrange("p t n -> p (t n)")
        g.ex_raw = place[:, 0:2 * WN].rearrange("p (s n) -> p s n", s=2)
        g.ex_rows, g.ex_res = (place[:, o:o + 2 * CT * D].rearrange("p (s c n) -> p s c n", s=2, c=CT)
                               for o in (2 * WN, 2 * WN + 2 * CT * D))
        g.ex_slots = m.sb("ex_slots", [P, E * CT, 2], u32)
        g.ex_w0 = m.sb("ex_w0", [P, 2, WN], f16)
        g.res = m.sb("res", [P, TB, D])
        g.out_done = m.sem("out_done")
        g.ex_w_in = [m.sem(f"ex_w_in{n}") for n in range(2)]
        g.ex_x_in = [m.sem(f"ex_x_in{n}") for n in range(2)]
        shared(nc, g, io)
        experts(nc, g, io)


def layout(a):
    import numpy as np
    c = np.ascontiguousarray

    def chunks(v):
        return c(v.reshape(KC, P).T)

    return {
        "x": c(a["x"].reshape(T, D)),
        "ctxT": c(a["ctx_1024"].reshape(JB, D).T),
        "L0_Wk": c(a["L0_xattn_Wk"]), "L0_Wv": c(a["L0_xattn_Wv"]), "L0_WqT": c(a["L0_xattn_Wq"].T),
        "L0_bq": chunks(a["L0_xattn_bq"]), "L0_bk": chunks(a["L0_xattn_bk"]), "L0_bv": c(a["L0_xattn_bv"]),
        "L0_rhsT": c(a["L0_ffn_rhs"].T),
        "L1_wqT": c(a["L1_xattn_w_q"].T), "L1_wkT": c(a["L1_xattn_w_k"].T),
        "L1_wvT": c(a["L1_xattn_w_v"].T), "L1_woT": c(a["L1_xattn_w_o"].T),
        "gwT": c(a["L1_ffn_gate_w"].T),
        "dyn_gT": c(a["L1_ffn_dyn_gate_w"].transpose(0, 2, 1)), "dyn_uT": c(a["L1_ffn_dyn_up_w"].transpose(0, 2, 1)),
        "dyn_dT": c(a["L1_ffn_dyn_down_w"].transpose(0, 2, 1)),
        "sh_guT": c(np.concatenate([a["L1_ffn_sh_gate_w"][0].T, a["L1_ffn_sh_up_w"][0].T])),
        "sh_dT": c(a["L1_ffn_sh_down_w"][0].T),
    }


def kernel(**inputs):
    import numpy as np
    import concourse.bacc as bacc
    from concourse.bass_utils import run_bass_kernel_spmd

    nc = bacc.Bacc("TRN2", target_bir_lowering=False, num_devices=1)
    arrays = layout({name: np.asarray(v) for name, v in inputs.items()})
    io = {name: nc.dram_tensor("in_" + name, v.shape, mybir.dt.from_np(v.dtype), kind="ExternalInput").ap()
          for name, v in arrays.items()}
    out = nc.dram_tensor("out_rows", (T + CAP, D), f32, kind="ExternalOutput").ap()
    program(nc, io, out)
    r = run_bass_kernel_spmd(nc, [{"in_" + name: v for name, v in arrays.items()}], core_ids=[0])
    return r.results[0]["out_rows"][0:T].reshape(B, S, D)
```
